# Optimizing a Trainium2 kernel written in Bass

```python
import numpy as np
import jax
import jax.numpy as jnp

def _softmax(x, axis=-1):
    return jax.nn.softmax(x, axis=axis)

def _gelu(x):
    return jax.nn.gelu(x, approximate=True)

def _silu(x):
    return jax.nn.silu(x)

def _sigmoid(x):
    return jax.nn.sigmoid(x)

def _layernorm(x, axis=-1, eps=1e-05):
    m = jnp.mean(x, axis=axis, keepdims=True)
    v = jnp.var(x, axis=axis, keepdims=True)
    return (x - m) / jnp.sqrt(v + eps)

def _scatter_add(tgt, idx, src, axis=0):
    return tgt.at[idx].add(src)

def _segment_sum(src, seg, n):
    return jax.ops.segment_sum(src, seg, n)
kernel_name = 'mk_gnn_preln_d4_gnn_r8_5821b7'

def setup_inputs(seed: int=0):
    np.random.seed(seed)
    _w = jnp.asarray

    def _rec_inputs():
        import jax
        import jax.numpy as jnp
        _gk = jax.random.key(seed)
        x = -0.0001006 + 1 * jax.random.normal(jax.random.fold_in(_gk, 1), (12500, 96), jnp.float32)
        _s = jax.random.randint(jax.random.fold_in(_gk, 2), (100000,), 0, 12500, jnp.int32)
        _d = jax.random.randint(jax.random.fold_in(_gk, 3), (100000,), 0, 12500, jnp.int32)
        _loop = jnp.arange(12500, dtype=jnp.int32)
        src = jnp.concatenate([_s, _d, _loop])
        dst = jnp.concatenate([_d, _s, _loop])
        _o = jnp.argsort(dst, stable=True)
        src = src[_o]
        dst = dst[_o]
        return (x, src, dst)
    x, src, dst = _rec_inputs()

    def _L0_gnn_setup():
        import jax, jax.numpy as jnp
        import numpy as np
        N_NODES = 6250
        N_EDGES = 100000
        DIM = 96
        HEADS = 4
        LAYERS = 3
        NEG_SLOPE = 0.2

        def _gat_layer(x, src, dst, W, a_src, a_dst, b):
            N = x.shape[0]
            H, C = a_src.shape
            h = (x @ W).reshape(N, H, C)
            alpha_s = jnp.einsum('nhc,hc->nh', h, a_src)
            alpha_d = jnp.einsum('nhc,hc->nh', h, a_dst)
            e = jax.nn.leaky_relu(alpha_s[src] + alpha_d[dst], NEG_SLOPE)
            m = jax.ops.segment_max(e, dst, num_segments=N)
            m = jnp.where(jnp.isfinite(m), m, 0.0)
            ex = jnp.exp(e - m[dst])
            den = jax.ops.segment_sum(ex, dst, num_segments=N)
            alpha = ex / (den[dst] + 1e-16)
            msg = h[src] * alpha[:, :, None]
            out = jax.ops.segment_sum(msg, dst, num_segments=N)
            return out.reshape(N, H * C) + b
        key = jax.random.key(seed)
        ks = jax.random.split(key, 6)
        C = DIM // HEADS
        x = jax.random.normal(ks[0], (N_NODES, DIM), dtype=jnp.float32)
        edge_index = jax.random.randint(ks[1], (2, N_EDGES), 0, N_NODES, dtype=jnp.int32)
        W = jax.random.normal(ks[2], (LAYERS, DIM, DIM), dtype=jnp.float32) * (1.0 / np.sqrt(DIM))
        att_src = jax.random.normal(ks[3], (LAYERS, HEADS, C), dtype=jnp.float32) * (1.0 / np.sqrt(C))
        att_dst = jax.random.normal(ks[4], (LAYERS, HEADS, C), dtype=jnp.float32) * (1.0 / np.sqrt(C))
        bias = jnp.zeros((LAYERS, DIM), dtype=jnp.float32)
        return {'x': x, 'edge_index': edge_index, 'W': W, 'att_src': att_src, 'att_dst': att_dst, 'bias': bias}
    _L0_gnn_all = _L0_gnn_setup()
    _L0_gnn_in = {k: v for k, v in _L0_gnn_all.items() if k in ('W', 'att_src', 'att_dst', 'bias')}
    del _L0_gnn_all

    def _L1_gnn_setup():
        import jax, jax.numpy as jnp
        import numpy as np
        N_NODES = 6250
        N_EDGES = 100000
        D_MODEL = 96
        HEADS = 4
        key = jax.random.key(seed)
        ks = jax.random.split(key, 6)
        scale = 1.0 / np.sqrt(D_MODEL)
        return {'embeds': jax.random.normal(ks[0], (N_NODES, D_MODEL), dtype=jnp.float32), 'qW': jax.random.normal(ks[1], (D_MODEL, D_MODEL), dtype=jnp.float32) * scale, 'kW': jax.random.normal(ks[2], (D_MODEL, D_MODEL), dtype=jnp.float32) * scale, 'vW': jax.random.normal(ks[3], (D_MODEL, D_MODEL), dtype=jnp.float32) * scale, 'rows': jax.random.randint(ks[4], (N_EDGES,), 0, N_NODES, dtype=jnp.int32), 'cols': jax.random.randint(ks[5], (N_EDGES,), 0, N_NODES, dtype=jnp.int32)}
    _L1_gnn_all = _L1_gnn_setup()
    _L1_gnn_in = {k: v for k, v in _L1_gnn_all.items() if k in ('qW', 'kW', 'vW')}
    del _L1_gnn_all

    def _L2_gnn_setup():
        import jax, jax.numpy as jnp
        import numpy as np
        N_NODES = 6250
        N_EDGES = 100000
        D = 96
        DEPTH = 2
        key = jax.random.key(seed)
        ks = jax.random.split(key, 8)
        scale = 1.0 / np.sqrt(D)
        x = jax.random.normal(ks[0], (N_NODES, D), dtype=jnp.float32)
        W0 = jax.random.normal(ks[1], (DEPTH, D, D), dtype=jnp.float32) * scale
        b0 = jnp.zeros((DEPTH, D), dtype=jnp.float32)
        W1 = jax.random.normal(ks[2], (DEPTH, D, D), dtype=jnp.float32) * scale
        b1 = jnp.zeros((DEPTH, D), dtype=jnp.float32)
        W2 = jax.random.normal(ks[3], (DEPTH, 2 * D, D), dtype=jnp.float32) * (1.0 / np.sqrt(2 * D))
        b2 = jnp.zeros((DEPTH, D), dtype=jnp.float32)
        edge_src = jax.random.randint(ks[4], (N_EDGES,), 0, N_NODES, dtype=jnp.int64 if jax.config.jax_enable_x64 else jnp.int32)
        edge_dst = jnp.sort(jax.random.randint(ks[5], (N_EDGES,), 0, N_NODES, dtype=jnp.int64 if jax.config.jax_enable_x64 else jnp.int32))
        return {'x': x, 'W0': W0, 'b0': b0, 'W1': W1, 'b1': b1, 'W2': W2, 'b2': b2, 'edge_src': edge_src, 'edge_dst': edge_dst}
    _L2_gnn_all = _L2_gnn_setup()
    _L2_gnn_in = {k: v for k, v in _L2_gnn_all.items() if k in ('W0', 'b0', 'W1', 'b1', 'W2', 'b2')}
    del _L2_gnn_all

    def _L3_gnn_setup():
        import jax, jax.numpy as jnp
        import numpy as np
        N_NODES = 6250
        N_EDGES = 100000
        D_IN = 96
        D_OUT = 96
        key = jax.random.key(seed)
        k1, k2, k3, k4 = jax.random.split(key, 4)
        x = jax.random.normal(k1, (N_NODES, D_IN), dtype=jnp.float32)
        edge_index = jax.random.randint(k2, (2, N_EDGES), 0, N_NODES, dtype=jnp.int64)
        W = jax.random.normal(k3, (D_IN, D_OUT), dtype=jnp.float32) * (1.0 / np.sqrt(D_IN))
        b = jax.random.normal(k4, (D_OUT,), dtype=jnp.float32) * 0.01
        return {'x': x, 'edge_index': edge_index, 'W': W, 'b': b}
    _L3_gnn_all = _L3_gnn_setup()
    _L3_gnn_in = {k: v for k, v in _L3_gnn_all.items() if k in ('W', 'b')}
    del _L3_gnn_all
    return {'x': x, 'src': src, 'dst': dst, 'L0_gnn_W': _L0_gnn_in['W'], 'L0_gnn_att_src': _L0_gnn_in['att_src'], 'L0_gnn_att_dst': _L0_gnn_in['att_dst'], 'L0_gnn_bias': _L0_gnn_in['bias'], 'L1_gnn_qW': _L1_gnn_in['qW'], 'L1_gnn_kW': _L1_gnn_in['kW'], 'L1_gnn_vW': _L1_gnn_in['vW'], 'L2_gnn_W0': _L2_gnn_in['W0'], 'L2_gnn_b0': _L2_gnn_in['b0'], 'L2_gnn_W1': _L2_gnn_in['W1'], 'L2_gnn_b1': _L2_gnn_in['b1'], 'L2_gnn_W2': _L2_gnn_in['W2'], 'L2_gnn_b2': _L2_gnn_in['b2'], 'L3_gnn_W': _L3_gnn_in['W'], 'L3_gnn_b': _L3_gnn_in['b']}

def reference(x, src, dst, L0_gnn_W, L0_gnn_att_src, L0_gnn_att_dst, L0_gnn_bias, L1_gnn_qW, L1_gnn_kW, L1_gnn_vW, L2_gnn_W0, L2_gnn_b0, L2_gnn_W1, L2_gnn_b1, L2_gnn_W2, L2_gnn_b2, L3_gnn_W, L3_gnn_b):
    import jax
    import jax.numpy as jnp

    def _L0_gnn_ref(x, edge_index, W, att_src, att_dst, bias):
        import jax, jax.numpy as jnp
        import numpy as np
        N_NODES = 6250
        N_EDGES = 100000
        DIM = 96
        HEADS = 4
        LAYERS = 3
        NEG_SLOPE = 0.2

        def _gat_layer(x, src, dst, W, a_src, a_dst, b):
            N = x.shape[0]
            H, C = a_src.shape
            h = (x @ W).reshape(N, H, C)
            alpha_s = jnp.einsum('nhc,hc->nh', h, a_src)
            alpha_d = jnp.einsum('nhc,hc->nh', h, a_dst)
            e = jax.nn.leaky_relu(alpha_s[src] + alpha_d[dst], NEG_SLOPE)
            m = jax.ops.segment_max(e, dst, num_segments=N)
            m = jnp.where(jnp.isfinite(m), m, 0.0)
            ex = jnp.exp(e - m[dst])
            den = jax.ops.segment_sum(ex, dst, num_segments=N)
            alpha = ex / (den[dst] + 1e-16)
            msg = h[src] * alpha[:, :, None]
            out = jax.ops.segment_sum(msg, dst, num_segments=N)
            return out.reshape(N, H * C) + b
        src = edge_index[0]
        dst = edge_index[1]
        for l in range(W.shape[0]):
            x = jax.nn.relu(_gat_layer(x, src, dst, W[l], att_src[l], att_dst[l], bias[l]))
        return x

    def _L1_gnn_ref(embeds, qW, kW, vW, rows, cols):
        import jax, jax.numpy as jnp
        import numpy as np
        N_NODES = 6250
        N_EDGES = 100000
        D_MODEL = 96
        HEADS = 4
        nvar, d = embeds.shape
        dh = d // HEADS
        e = rows.shape[0]
        q = (embeds[rows] @ qW).reshape(e, HEADS, dh)
        k = (embeds[cols] @ kW).reshape(e, HEADS, dh)
        v = (embeds[cols] @ vW).reshape(e, HEADS, dh)
        scores = jnp.clip(jnp.einsum('ehd,ehd->eh', q, k), -10.0, 10.0)
        exp_s = jnp.exp(scores)
        norms = jax.ops.segment_sum(exp_s, rows, num_segments=nvar)[rows]
        w = exp_s / (norms + 1e-08)
        res = jax.ops.segment_sum(w[:, :, None] * v, rows, num_segments=nvar).reshape(nvar, d)
        return embeds + res

    def _L2_gnn_ref(x, W0, b0, W1, b1, W2, b2, edge_src, edge_dst):
        import jax, jax.numpy as jnp
        import numpy as np
        N_NODES = 6250
        N_EDGES = 100000
        D = 96
        DEPTH = 2
        n = x.shape[0]
        depth = W0.shape[0]
        for i in range(depth):
            h_self = x @ W1[i] + b1[i]
            h_nb = x @ W0[i] + b0[i]
            agg = jax.ops.segment_sum(h_nb[edge_src], edge_dst, num_segments=n)
            x = jnp.concatenate([h_self, agg], axis=-1) @ W2[i] + b2[i]
            x = x / jnp.std(x, axis=-1, ddof=1, keepdims=True)
        return x

    def _L3_gnn_ref(x, edge_index, W, b):
        import jax, jax.numpy as jnp
        import numpy as np
        N_NODES = 6250
        N_EDGES = 100000
        D_IN = 96
        D_OUT = 96
        num_nodes = x.shape[0]
        src, dst = (edge_index[0], edge_index[1])
        messages = x[src] @ W + b
        out = jax.ops.segment_sum(messages, dst, num_segments=num_nodes)
        deg = jax.ops.segment_sum(jnp.ones((dst.shape[0],), dtype=x.dtype), dst, num_segments=num_nodes)
        deg = jnp.clip(deg, 1.0, None)
        return out / deg[:, None]
    edge_index = jnp.stack([src, dst])
    h = jnp.maximum(_layernorm(x, axis=-1), 0.0)
    x = x + _L0_gnn_ref(h, edge_index, L0_gnn_W, L0_gnn_att_src, L0_gnn_att_dst, L0_gnn_bias)
    h = jnp.maximum(_layernorm(x, axis=-1), 0.0)
    x = x + _L1_gnn_ref(h, L1_gnn_qW, L1_gnn_kW, L1_gnn_vW, src, dst)
    h = jnp.maximum(_layernorm(x, axis=-1), 0.0)
    x = x + _L2_gnn_ref(h, L2_gnn_W0, L2_gnn_b0, L2_gnn_W1, L2_gnn_b1, L2_gnn_W2, L2_gnn_b2, src, dst)
    h = jnp.maximum(_layernorm(x, axis=-1), 0.0)
    x = x + _L3_gnn_ref(h, edge_index, L3_gnn_W, L3_gnn_b)
    return x

_drawn_inputs = setup_inputs


def setup_inputs(seed=0):
    import zlib

    import numpy as np

    out = dict(_drawn_inputs(seed))
    spreads = {'L0_gnn_bias': (0.0, 0.1),
     'L2_gnn_b0': (0.0, 0.1),
     'L2_gnn_b1': (0.0, 0.8),
     'L2_gnn_b2': (0.0, 0.779)}
    factors = {'L0_gnn_att_src': 3.593, 'L0_gnn_att_dst': 8.0, 'L3_gnn_b': 8.0}
    for name, (base, spread) in spreads.items():
        noise = np.random.default_rng([zlib.crc32(name.encode()), seed]).standard_normal(out[name].shape)
        drawn = base * np.exp(spread * noise) if base else spread * noise
        out[name] = jnp.asarray(drawn.astype(out[name].dtype))
    for name, factor in factors.items():
        out[name] = (out[name] * factor).astype(out[name].dtype)
    return out
```

```python
from contextlib import ExitStack, contextmanager

import numpy as np

import concourse.bass as bass
from concourse import mybir

P = 128
N, E, D, H = 12500, 212500, 96, 4
C = D // H
NT = -(-N // P)
N_FULL = N // P
N_TAIL = N - N_FULL * P
GROUP = 8
STEP = 2 * GROUP
T_MAX = (E + NT * (P - 1)) // P
STEPS = -(-T_MAX // STEP)
T = STEPS * STEP
TB = -(-T // P)
TP = TB * P
E_ROWS = 125
E_COLS = E // E_ROWS
assert E_ROWS * E_COLS == E
NODE_UNROLL = 14
RING = 2
NODE_ITERS = NT // NODE_UNROLL
assert NODE_ITERS * NODE_UNROLL == NT
ACC_W = D + H
FAR = 1 << 20
PHASE_SEMS = 200
BIG = 1e30
LN_EPS = 1e-5
SLOPE = 0.2

F32 = mybir.dt.float32
BF16 = mybir.dt.bfloat16
I32 = mybir.dt.int32
U16 = mybir.dt.uint16
ALU = mybir.AluOpType
ACT = mybir.ActivationFunctionType
AX = mybir.AxisListType.X


class Chain:

    def __init__(self, eng, sem, base=0):
        self.eng, self.sem, self.count = eng, sem, base

    def __call__(self, instruction):
        instruction.then_inc(self.sem, 1)
        self.count = self.count + 1
        self.eng.wait_ge(self.sem, self.count)


@contextmanager
def phase(nc, *names):
    with ExitStack() as ctx:
        sems = [ctx.enter_context(nc.semaphore(name, num=PHASE_SEMS + n)) for n, name in enumerate(names)]
        with nc.Block() as block:
            yield (block, *sems)
        nc.all_engine_barrier(sems_to_clear=range(PHASE_SEMS, PHASE_SEMS + len(names)))


class Graph:
    pass


def allocate_small(nc, ctx, g):
    def sb(name, shape, dt=F32):
        return ctx.enter_context(nc.sbuf_tensor(name, shape, dt))

    g.ones = sb("ones", [P, P])
    g.ident = sb("ident", [P, P])
    g.iota = sb("iota", [P, P])
    g.idx = sb("idx", [P, TP], U16)
    g.dloc = sb("dloc", [P, TP], BF16)
    g.run_break = sb("run_break", [P, T + 1], BF16)
    g.any_break_fwd = sb("any_break_fwd", [H, P])
    g.any_break_bwd = sb("any_break_bwd", [H, P])
    g.tile_row = sb("tile_row", [1, TP], U16)
    g.src_pad = nc.dram_tensor("src_pad", (E + P,), I32)
    g.dst_pad = nc.dram_tensor("dst_pad", (E + P,), I32)
    g.key_dram = nc.dram_tensor("key_dram", (P + TP * P,), F32)
    g.tile_dram = nc.dram_tensor("tile_dram", (TP,), U16)
    g.score_dram = nc.dram_tensor("score_dram", (H, TP * P), F32)
    g.weight_dram = nc.dram_tensor("weight_dram", (H, TP * P), F32)
    g.alpha_table = nc.dram_tensor("alpha_table", (NT * P, H), F32)
    g.row_table = nc.dram_tensor("row_table", (NT * P, D), F32)
    g.kv_table = nc.dram_tensor("kv_table", (NT * P, 2 * D), F32)


def constants(nc, g, tile_no):
    with phase(nc, "const_steps") as (block, const_steps):
        @block.gpsimd
        def _(pool):
            done = Chain(pool, const_steps)
            done(nc.gpsimd.memset(g.ones[:], 1.0))
            done(nc.gpsimd.memset(g.ident[:], 0.0))
            done(nc.gpsimd.affine_select(out=g.ident[:], in_=g.ident[:], compare_op=ALU.not_equal,
                                         fill=1.0, base=0, pattern=[[-1, P]], channel_multiplier=1))
            done(nc.gpsimd.iota(g.iota[:], pattern=[[1, P]], base=0, channel_multiplier=0,
                                allow_small_or_imprecise_dtypes=True))
            done(nc.gpsimd.iota(tile_no[:], pattern=[[P, TB]], base=0, channel_multiplier=1,
                                allow_small_or_imprecise_dtypes=True))


def plan_edge_tiles(nc, g, src, dst):
    with ExitStack() as ctx:
        def sb(name, shape, dt=F32):
            return ctx.enter_context(nc.sbuf_tensor(name, shape, dt))

        def pb(name, shape):
            return ctx.enter_context(nc.psum_tensor(name, shape, F32))

        tile_no = sb("tile_no", [P, TB])
        dst_i = sb("dst_i", [E_ROWS, E_COLS], I32)
        dst_f = sb("dst_f", [E_ROWS, E_COLS])
        below = sb("below", [E_ROWS, E_COLS], BF16)
        count = sb("count", [E_ROWS, NT])
        tail = sb("tail", [1, 2 * P], I32)
        first = sb("first", [P, NT + 1])
        tiles = sb("tiles", [P, NT])
        tiles_i = sb("tiles_i", [P, NT], I32)
        zeros = sb("zeros", [P, NT])
        last_tile = sb("last_tile", [P, NT])
        shift = sb("shift", [P, NT])
        shift_step = sb("shift_step", [P, NT - 1])
        reached = sb("reached", [P, TB, NT - 1])
        weighted = sb("weighted", [P, TB, NT - 1])
        node_tile = sb("node_tile", [P, TB])
        node_tile_i = sb("node_tile_i", [P, TB], U16)
        start = sb("start", [P, TB])
        start_i = sb("start_i", [P, TB], I32)
        src_t = sb("src_t", [P, TB, P], I32)
        dst_t = sb("dst_t", [P, TB, P], I32)
        src_tf = sb("src_tf", [P, TB, P])
        dst_tf = sb("dst_tf", [P, TB, P])
        dloc_t = sb("dloc_t", [P, TB, P])
        mine = sb("mine", [P, TB, P])
        key = sb("key", [P, TB, P])
        key_pad = sb("key_pad", [1, P])
        keys = sb("keys", [P, T + 2])
        any_break = sb("any_break", [P, 2])
        any_break4 = sb("any_break4", [P, 2, H])
        ps_count = pb("ps_count", [P, 512])
        ps_t = pb("ps_t", [P, 2, 512])
        fetched = g.plan_fetched

        constants(nc, g, tile_no)

        with phase(nc, "dst_loaded", "pads_set", "copied", "counted", "summed", "starts_ready",
                   "plan_steps") as (
                block, dst_loaded, pads_set, copied, counted, summed, starts_ready, plan_steps):
            @block.sync
            def _(sp):
                sp.dma_start(dst_i[:], dst.rearrange("(r c) -> r c", r=E_ROWS)).then_inc(dst_loaded, 16)
                for n, (pad, given) in enumerate(((g.src_pad, src), (g.dst_pad, dst))):
                    sp.dma_start(pad[0:E].rearrange("(r c) -> r c", r=E_ROWS),
                                 given.rearrange("(r c) -> r c", r=E_ROWS)).then_inc(copied, 16)
                sp.wait_ge(pads_set, 2)
                for n, pad in enumerate((g.src_pad, g.dst_pad)):
                    sp.dma_start(pad[E:E + P].rearrange("(r c) -> r c", r=1),
                                 tail[:, n * P:(n + 1) * P]).then_inc(copied, 16)
                sp.wait_ge(copied, 64)

            @block.vector
            def _(dve):
                nc.vector.memset(tail[:, 0:P], 0).then_inc(pads_set, 1)
                nc.vector.memset(tail[:, P:2 * P], FAR).then_inc(pads_set, 1)
                done = Chain(dve, plan_steps)
                dve.wait_ge(dst_loaded, 16)
                done(nc.vector.tensor_copy(dst_f[:], dst_i[:]))
                count_done = Chain(dve, counted)
                for j in range(1, NT):
                    count_done(nc.vector.tensor_scalar(out=below[:], in0=dst_f[:], scalar1=float(j * P),
                                                       scalar2=None, op0=ALU.is_lt, op1=ALU.add,
                                                       accum_out=count[:, j:j + 1]))
                done(nc.vector.memset(first[:, 0:1], 0.0))
                done(nc.vector.memset(first[:, NT:NT + 1], float(E)))
                done(nc.vector.memset(zeros[:], 0.0))
                dve.wait_ge(summed, 1)
                done(nc.vector.tensor_copy(first[:, 1:NT], ps_count[:, 1:NT]))
                done(nc.vector.tensor_tensor(tiles[:], first[:, 1:NT + 1], first[:, 0:NT], ALU.subtract))
                done(nc.vector.tensor_scalar(out=tiles_i[:], in0=tiles[:], scalar1=float(P - 1),
                                             scalar2=None, op0=ALU.add))
                done(nc.vector.tensor_scalar(out=tiles_i[:], in0=tiles_i[:], scalar1=P.bit_length() - 1,
                                             scalar2=None, op0=ALU.arith_shift_right))
                done(nc.vector.tensor_copy(tiles[:], tiles_i[:]))
                done(nc.vector.tensor_tensor_scan(out=last_tile[:], data0=tiles[:], data1=zeros[:],
                                                  initial=0.0, op0=ALU.add, op1=ALU.add))
                done(nc.vector.memset(shift[:, 0:1], 0.0))
                done(nc.vector.scalar_tensor_tensor(out=shift[:, 1:NT], in0=last_tile[:, 0:NT - 1],
                                                    scalar=float(P), in1=first[:, 1:NT],
                                                    op0=ALU.mult, op1=ALU.subtract))
                done(nc.vector.tensor_tensor(shift_step[:], shift[:, 1:NT], shift[:, 0:NT - 1],
                                             ALU.subtract))
                done(nc.vector.tensor_tensor(
                    reached[:], last_tile[:, 0:NT - 1].unsqueeze(1).to_broadcast([P, TB, NT - 1]),
                    tile_no[:].unsqueeze(2).to_broadcast([P, TB, NT - 1]), ALU.is_le))
                done(nc.vector.tensor_reduce(node_tile[:], reached[:], AX, ALU.add))
                done(nc.vector.tensor_tensor(
                    weighted[:], reached[:], shift_step[:].unsqueeze(1).to_broadcast([P, TB, NT - 1]),
                    ALU.mult))
                done(nc.vector.tensor_reduce(start[:], weighted[:], AX, ALU.add))
                done(nc.vector.scalar_tensor_tensor(out=start[:], in0=tile_no[:], scalar=float(P),
                                                    in1=start[:], op0=ALU.mult, op1=ALU.subtract))
                done(nc.vector.tensor_scalar(out=start_i[:], in0=start[:], scalar1=float(E),
                                             scalar2=0.0, op0=ALU.min, op1=ALU.max))
                done(nc.vector.tensor_copy(node_tile_i[:], node_tile[:]))
                nc.vector.memset(key_pad[:], -1.0).then_inc(starts_ready, 1)

            @block.tensor
            def _(pe):
                pe.wait_ge(counted, NT - 1)
                nc.tensor.matmul(ps_count[:, 1:NT], g.ones[0:E_ROWS, :], count[:, 1:NT],
                                 start=True, stop=True).then_inc(summed, 1)

            @block.gpsimd
            def _(pool):
                pool.wait_ge(starts_ready, 1)
                pool.wait_ge(copied, 64)
                for b in range(TB):
                    for pad, got in ((g.src_pad, src_t), (g.dst_pad, dst_t)):
                        nc.gpsimd.indirect_dma_start(
                            out=got[:, b, :], out_offset=None,
                            in_=bass.AP(pad, 0, [[1, 1], [1, E + P]]),
                            in_offset=bass.IndirectOffsetOnAxis(ap=start_i[:, b:b + 1], axis=1),
                        ).then_inc(fetched, 16)
                pool.wait_ge(fetched, 32 * TB)

        with phase(nc, "key_ready", "key_stored", "keys_loaded", "turned", "turned_used",
                   "breaks_ready", "breaks_turned", "layout_steps") as (
                block, key_ready, key_stored, keys_loaded, turned, turned_used, breaks_ready,
                breaks_turned, layout_steps):
            @block.vector
            def _(dve):
                done = Chain(dve, layout_steps)
                done(nc.vector.tensor_copy(src_tf[:], src_t[:]))
                done(nc.vector.tensor_copy(dst_tf[:], dst_t[:]))
                node_tile_b = node_tile[:].unsqueeze(2).to_broadcast([P, TB, P])
                done(nc.vector.scalar_tensor_tensor(out=dloc_t[:], in0=node_tile_b, scalar=float(-P),
                                                    in1=dst_tf[:], op0=ALU.mult, op1=ALU.add))
                done(nc.vector.tensor_scalar(out=mine[:], in0=dloc_t[:], scalar1=float(P),
                                             scalar2=None, op0=ALU.is_lt))
                nc.vector.scalar_tensor_tensor(out=key[:], in0=dst_tf[:], scalar=1.0, in1=mine[:],
                                               op0=ALU.add, op1=ALU.mult).then_inc(key_ready, 1)
                for b in range(TB):
                    dve.wait_ge(turned, b + 1)
                    cols = slice(b * P, (b + 1) * P)
                    nc.vector.tensor_copy(g.idx[:, cols], ps_t[:, b % 2, 0:P])
                    nc.vector.tensor_copy(g.dloc[:, cols], ps_t[:, b % 2, P:2 * P]).then_inc(turned_used, 1)
                dve.wait_ge(keys_loaded, 16)
                done(nc.vector.tensor_tensor(keys[:, 0:T + 1], keys[:, 0:T + 1], keys[:, 1:T + 2],
                                             ALU.not_equal))
                done(nc.vector.tensor_scalar(out=g.run_break[:], in0=keys[:, 0:T + 1], scalar1=-BIG,
                                             scalar2=None, op0=ALU.mult))
                done(nc.vector.tensor_reduce(any_break[:, 0:1], g.run_break[:, 0:T], AX, ALU.min))
                done(nc.vector.tensor_reduce(any_break[:, 1:2], g.run_break[:, 1:T + 1], AX, ALU.min))
                nc.vector.tensor_copy(any_break4[:], any_break[:].unsqueeze(2).to_broadcast([P, 2, H]))\
                    .then_inc(breaks_ready, 1)
                dve.wait_ge(breaks_turned, 1)
                done(nc.vector.tensor_copy(g.any_break_fwd[:], ps_count[0:H, 0:P]))
                done(nc.vector.tensor_copy(g.any_break_bwd[:], ps_count[0:H, P:2 * P]))

            @block.tensor
            def _(pe):
                pe.wait_ge(key_ready, 1)
                for b in range(TB):
                    if b >= 2:
                        pe.wait_ge(turned_used, b - 1)
                    nc.tensor.transpose(ps_t[:, b % 2, 0:P], src_tf[:, b, :], g.ident[:])
                    nc.tensor.transpose(ps_t[:, b % 2, P:2 * P], dloc_t[:, b, :], g.ident[:])\
                        .then_inc(turned, 1)
                pe.wait_ge(breaks_ready, 1)
                nc.tensor.transpose(ps_count[0:H, 0:P], any_break4[:, 0, :], g.ident[:])
                nc.tensor.transpose(ps_count[0:H, P:2 * P], any_break4[:, 1, :], g.ident[:])\
                    .then_inc(breaks_turned, 1)

            @block.sync
            def _(sp):
                key_slots = g.key_dram[P:P + TP * P].rearrange("(b t e) -> t b e", b=TB, t=P)
                sp.dma_start(g.key_dram[0:P].rearrange("(a e) -> a e", a=1), key_pad[:]).then_inc(key_stored, 16)
                sp.dma_start(g.tile_dram[:].rearrange("(b t) -> t b", t=P), node_tile_i[:],
                             allow_slow_non_contiguous=True).then_inc(key_stored, 16)
                sp.wait_ge(key_ready, 1)
                sp.dma_start(key_slots, key[:]).then_inc(key_stored, 16)
                sp.wait_ge(key_stored, 48)
                sp.dma_start(keys[:], bass.AP(g.key_dram, P - 1, [[T, P], [1, T + 2]])).then_inc(keys_loaded, 16)
                sp.dma_start(g.tile_row[:], g.tile_dram[:].rearrange("(a t) -> a t", a=1)).then_inc(key_stored, 16)
                sp.wait_ge(key_stored, 64)


def allocate_large(nc, ctx, g):
    def sb(name, shape, dt=F32):
        return ctx.enter_context(nc.sbuf_tensor(name, shape, dt))

    g.x = sb("x_res", [P, NT, D])
    g.h = sb("h_cur", [P, NT, D])
    g.acc = sb("acc", [P, NT, ACC_W])
    g.alpha_dst = sb("alpha_dst", [P, NT, H])
    g.edge_buf = sb("edge_buf", [P, NT * D])
    g.ring_buf = sb("ring_buf", [P, 2 * GROUP * (2 * D + P) + GROUP * P + 2 * GROUP * ACC_W])
    g.idx_stage = sb("idx_stage", [P, 2, GROUP], I32)
    g.score8 = sb("score8", [P, GROUP, H])
    g.gat_w = sb("gat_w", [D, 3, D + 2 * H])
    g.qkv_w = sb("qkv_w", [D, 3 * D])
    g.self_w = sb("self_w", [D, 2, D])
    g.sum_w = sb("sum_w", [D + 2, 2, D])
    g.mean_w = sb("mean_w", [D + 1, D])
    g.bias = sb("bias", [P, 3, D])
    g.mean = sb("mean", [P, NT])
    g.spread = sb("spread", [P, NT])
    g.recip = sb("recip", [P, NT, H])
    g.eps = sb("eps", [P, 1])
    g.carry = sb("carry", [H, 2, P])
    g.carry_col = sb("carry_col", [P, H])
    g.scores = g.edge_buf[:, 0:T * H].rearrange("p (t h) -> p t h", h=H)
    g.scores_back = g.edge_buf[:, 0:T * H].rearrange("p (h s) -> p h s", h=H)
    g.query = g.edge_buf[:, :].rearrange("p (n d) -> p n d", d=D)
    acc_flat = g.acc[:].rearrange("p n w -> p (n w)")
    g.acc_flat = acc_flat
    g.square = acc_flat[:, 0:NT * D].rearrange("p (n d) -> p n d", d=D)
    g.runs_fwd = acc_flat[:, 0:T * H].rearrange("p (h s) -> p h s", h=H)
    g.weight_rows = acc_flat[:, 0:TB * H * P].rearrange("p (b h e) -> p b h e", b=TB, h=H)
    g.runs = g.ring_buf[:, 0:T * H].rearrange("p (h s) -> p h s", h=H)
    at = 0

    def ring(size):
        nonlocal at
        at += size
        return g.ring_buf[:, at - size:at]

    rows = ring(2 * GROUP * 2 * D)
    g.kv_ring = rows.rearrange("p (r k w) -> p r k w", r=2, k=GROUP)
    g.row_ring = rows[:, 0:2 * GROUP * D].rearrange("p (r k w) -> p r k w", r=2, k=GROUP)
    g.sum_ring = rows[:, 0:2 * GROUP * (D + 1)].rearrange("p (r k w) -> p r k w", r=2, k=GROUP)
    g.alpha_ring = rows[:, 0:2 * GROUP * H].rearrange("p (r k w) -> p r k w", r=2, k=GROUP)
    g.onehot = ring(2 * GROUP * P).rearrange("p (r k n) -> p r k n", r=2, k=GROUP)
    g.onehot_t = ring(GROUP * P).rearrange("p (k e) -> p k e", k=GROUP)
    g.msg = ring(2 * GROUP * ACC_W).rearrange("p (r k w) -> p r k w", r=2, k=GROUP)
    at = 0
    g.stage = ring(RING * 2 * (D + 2)).rearrange("p (r s w) -> p r s w", r=RING, s=2)
    g.stage_t = ring(RING * 2 * P).rearrange("p (r s n) -> p r s n", r=RING, s=2)
    g.row_stage = ring(RING * 2 * D).rearrange("p (r w) -> p r w", r=RING)
    g.row_out = g.ring_buf[:, 0:2 * H * P].rearrange("p (r h e) -> p r h e", r=2, h=H)


def load_inputs(nc, g, x, gat_w, att_src, att_dst, gat_bias, qw, kw, vw, w0, b0, w1, b1, w2, b2, w3, b3):
    with ExitStack() as ctx:
        att = g.edge_buf[0:D, 0:6 * H].rearrange("p (l s) -> p l s", l=3)
        w01, w2s = (g.edge_buf[0:D, at:at + 4 * D].rearrange("p (i s d) -> p i s d", i=2, s=2)
                    for at in (D, 5 * D))
        w_t = g.edge_buf[0:D, 9 * D:16 * D].rearrange("p (n d) -> p n d", n=7)
        b01 = g.edge_buf[0:D, 16 * D:16 * D + 4].rearrange("p (i s) -> p i s", i=2)
        b2s = g.edge_buf[0:1, 17 * D:19 * D].rearrange("p (i d) -> p i d", i=2)
        bias_rows = g.edge_buf[0:1, 19 * D:23 * D].rearrange("p (i s d) -> p i s d", i=2, s=2)
        ps_w = ctx.enter_context(nc.psum_tensor("ps_w", [P, 2, 512], F32, allow_name_mangling=True))
        ps_m = ctx.enter_context(nc.psum_tensor("ps_m", [P, 512], F32, allow_name_mangling=True))
        with phase(nc, "zeroed", "loaded", "x_loaded", "w_turned", "w_kept", "product", "product_kept",
                   "rows_kept") as (
                block, zeroed, loaded, x_loaded, w_turned, w_kept, product, product_kept, rows_kept):
            n_att = 3 * 2 * H
            n_loads = n_att + 3 + 3 + 2 * 7 + 1 + 1 + 3

            @block.gpsimd
            def _(pool):
                nc.gpsimd.memset(g.x[:, N_FULL, :], 0.0).then_inc(zeroed, 1)
                nc.gpsimd.memset(att, 0.0).then_inc(zeroed, 1)
                nc.gpsimd.memset(g.eps[:], LN_EPS).then_inc(zeroed, 1)

            @block.sync
            def _(sp):
                def load(to, given):
                    sp.dma_start(to, given).then_inc(loaded, 16)

                for l in range(3):
                    load(g.gat_w[:, l, 0:D], gat_w[l])
                sp.wait_ge(zeroed, 3)
                for l in range(3):
                    for side, given in enumerate((att_src, att_dst)):
                        for h in range(H):
                            load(att[h * C:(h + 1) * C, l, side * H + h:side * H + h + 1],
                                 given[l, h].rearrange("(c a) -> c a", a=1))
                for i in range(2):
                    load(w01[:, i, 0, :], w0[i])
                    load(w01[:, i, 1, :], w1[i])
                    load(w2s[:, i, 0, :], w2[i, D:2 * D, :])
                    load(w2s[:, i, 1, :], w2[i, 0:D, :])
                    load(b01[:, i, 0:1], b0[i].rearrange("(c a) -> c a", a=1))
                    load(b01[:, i, 1:2], b1[i].rearrange("(c a) -> c a", a=1))
                    load(b2s[:, i, :], b2[i:i + 1, :])
                for n, w in enumerate((qw, kw, vw)):
                    load(g.qkv_w[:, n * D:(n + 1) * D], w)
                load(g.mean_w[0:D, :], w3)
                load(g.mean_w[D:D + 1, :], b3.rearrange("(a d) -> a d", a=1))
                for l in range(3):
                    load(g.bias[:, l, :], gat_bias[l:l + 1, :].to_broadcast([P, D]))
                sp.dma_start(g.x[:, 0:N_FULL, :], x[0:N_FULL * P, :].rearrange("(n p) d -> p n d", p=P))\
                    .then_inc(x_loaded, 16)
                sp.dma_start(g.x[0:N_TAIL, N_FULL, :], x[N_FULL * P:N, :]).then_inc(x_loaded, 16)
                sp.wait_ge(loaded, 16 * n_loads)
                sp.wait_ge(x_loaded, 32)
                sp.wait_ge(product_kept, 11)
                for i in range(2):
                    for side in range(2):
                        sp.dma_start(g.sum_w[D + side:D + side + 1, i, :], bias_rows[:, i, side, :])\
                            .then_inc(rows_kept, 16)
                sp.wait_ge(rows_kept, 64)

            turns = [g.gat_w[:, l, 0:D] for l in range(3)] + [w01[:, i, s, :] for i in range(2) for s in range(2)]

            @block.tensor
            def _(pe):
                pe.wait_ge(loaded, 16 * n_loads)
                for n, w in enumerate(turns):
                    if n >= 2:
                        pe.wait_ge(w_kept, n - 1)
                    nc.tensor.transpose(ps_w[0:D, n % 2, 0:D], w, g.ident[0:D, 0:D]).then_inc(w_turned, 1)
                pe.wait_ge(w_kept, 7)
                done = 0
                for l in range(3):
                    pe.wait_ge(product_kept, done)
                    nc.tensor.matmul(ps_m[0:D, 0:2 * H], w_t[:, l, :], att[:, l, :], start=True, stop=True)\
                        .then_inc(product, 1)
                    done += 1
                for i in range(2):
                    for side in range(2):
                        pe.wait_ge(product_kept, done)
                        nc.tensor.matmul(ps_m[0:D, 0:D], w_t[:, 3 + 2 * i + side, :], w2s[:, i, side, :],
                                         start=True, stop=True).then_inc(product, 1)
                        done += 1
                        pe.wait_ge(product_kept, done)
                        m = nc.tensor.matmul(ps_m[0:1, 0:D], b01[:, i, side:side + 1], w2s[:, i, side, :],
                                             start=True, stop=side == 0)
                        if side == 1:
                            m = nc.tensor.matmul(ps_m[0:1, 0:D], g.ones[0:1, 0:1], b2s[:, i, :],
                                                 start=False, stop=True)
                        m.then_inc(product, 1)
                        done += 1

            @block.vector
            def _(dve):
                for n in range(7):
                    dve.wait_ge(w_turned, n + 1)
                    nc.vector.tensor_copy(w_t[:, n, :], ps_w[0:D, n % 2, 0:D]).then_inc(w_kept, 1)
                done = 0

                def keep(to, what):
                    nonlocal done
                    done += 1
                    dve.wait_ge(product, done)
                    nc.vector.tensor_copy(to, what).then_inc(product_kept, 1)

                for l in range(3):
                    keep(g.gat_w[:, l, D:D + 2 * H], ps_m[0:D, 0:2 * H])
                for i in range(2):
                    for side in range(2):
                        keep(g.sum_w[0:D, i, :] if side == 0 else g.self_w[:, i, :], ps_m[0:D, 0:D])
                        keep(bias_rows[:, i, side, :], ps_m[0:1, 0:D])


def normalise(nc, g):
    with phase(nc, "norm_steps", "var_ready", "std_ready") as (block, norm_steps, var_ready, std_ready):
        @block.vector
        def _(dve):
            done = Chain(dve, norm_steps)
            done(nc.vector.tensor_reduce(g.mean[:], g.x[:], AX, ALU.add))
            done(nc.vector.scalar_tensor_tensor(
                out=g.h[:], in0=g.mean[:].unsqueeze(2).to_broadcast([P, NT, D]), scalar=-1.0 / D,
                in1=g.x[:], op0=ALU.mult, op1=ALU.add))
            done(nc.vector.tensor_tensor(g.square, g.h[:], g.h[:], ALU.mult))
            nc.vector.tensor_reduce(g.spread[:], g.square, AX, ALU.add).then_inc(var_ready, 1)
            dve.wait_ge(std_ready, 1)
            done(nc.vector.reciprocal(g.spread[:], g.spread[:]))
            done(nc.vector.scalar_tensor_tensor(
                out=g.h[:], in0=g.h[:], scalar=0.0,
                in1=g.spread[:].unsqueeze(2).to_broadcast([P, NT, D]), op0=ALU.max, op1=ALU.mult))

        @block.scalar
        def _(act):
            act.wait_ge(var_ready, 1)
            nc.scalar.activation(g.spread[:], g.spread[:], ACT.Sqrt, bias=g.eps[:], scale=1.0 / D)\
                .then_inc(std_ready, 1)


def standardise(nc, g, into_x):
    with phase(nc, "sd_steps", "var_ready", "std_ready") as (block, sd_steps, var_ready, std_ready):
        @block.vector
        def _(dve):
            done = Chain(dve, sd_steps)
            done(nc.vector.tensor_reduce(g.mean[:], g.h[:], AX, ALU.add))
            done(nc.vector.scalar_tensor_tensor(
                out=g.square, in0=g.mean[:].unsqueeze(2).to_broadcast([P, NT, D]), scalar=-1.0 / D,
                in1=g.h[:], op0=ALU.mult, op1=ALU.add))
            done(nc.vector.tensor_tensor(g.square, g.square, g.square, ALU.mult))
            nc.vector.tensor_reduce(g.spread[:], g.square, AX, ALU.add).then_inc(var_ready, 1)
            dve.wait_ge(std_ready, 1)
            done(nc.vector.reciprocal(g.spread[:], g.spread[:]))
            done(nc.vector.tensor_tensor(g.h[:], g.h[:], g.spread[:].unsqueeze(2).to_broadcast([P, NT, D]),
                                         ALU.mult))
            if into_x:
                done(nc.vector.tensor_tensor(g.x[:], g.x[:], g.h[:], ALU.add))

        @block.scalar
        def _(act):
            act.wait_ge(var_ready, 1)
            nc.scalar.activation(g.spread[:], g.spread[:], ACT.Sqrt, scale=1.0 / (D - 1)).then_inc(std_ready, 1)


def node_matmul(nc, g, sources, width, relu_in, keep, tables=(), table_cols=()):
    with ExitStack() as ctx:
        ps_turn = ctx.enter_context(nc.psum_tensor("ps_turn", [P, 2, 512], F32, allow_name_mangling=True))
        ps_out = ctx.enter_context(nc.psum_tensor("ps_out", [P, 2, 512], F32, allow_name_mangling=True))
        with phase(nc, "staged", "turned", "turn_kept", "product", "kept", "table_written0",
                   "table_written1") as (
                block, staged, turned, turn_kept, product, kept, table_written0, table_written1):
            table_written = (table_written0, table_written1)
            @block.scalar
            def _(act):
                func = ACT.Relu if relu_in else ACT.Copy
                with act.Fori(0, NODE_ITERS) as i:
                    for k in range(NODE_UNROLL):
                        n = i * NODE_UNROLL + k
                        act.wait_ge(turned, n + 1)
                        for s, (rows, cols, _) in enumerate(sources):
                            last = nc.scalar.activation(
                                g.stage[:, k % RING, s:s + 1, 0:cols],
                                rows[:, bass.ds(n, 1), 0:cols], func)
                        last.then_inc(staged, 1)

            @block.tensor
            def _(pe):
                pe.sem_inc(turned, RING)
                pe.sem_inc(product, RING)
                with pe.Fori(0, NODE_ITERS) as i:
                    for k in range(NODE_UNROLL):
                        n = i * NODE_UNROLL + k
                        r = k % RING
                        pe.wait_ge(staged, n + 1)
                        pe.wait_ge(turn_kept, n + 1)
                        for s, (_, cols, _) in enumerate(sources):
                            last = nc.tensor.transpose(ps_turn[0:cols, r, s * P:(s + 1) * P],
                                                       g.stage[:, r, s, 0:cols], g.ident[:])
                        last.then_inc(turned, 1)
                        pe.wait_ge(turn_kept, n + 1 + RING)
                        pe.wait_ge(kept, n + 1)
                        for s, (_, cols, weights) in enumerate(sources):
                            last = nc.tensor.matmul(ps_out[:, r, 0:width],
                                                    g.stage_t[0:cols, r, s, :], weights,
                                                    start=s == 0, stop=s == len(sources) - 1)
                        last.then_inc(product, 1)

            @block.vector
            def _(dve):
                dve.sem_inc(turn_kept, RING)
                dve.sem_inc(kept, RING)
                with dve.Fori(0, NODE_ITERS) as i:
                    for k in range(NODE_UNROLL):
                        n = i * NODE_UNROLL + k
                        r = k % RING
                        dve.wait_ge(turned, n + 1 + RING)
                        dve.wait_ge(product, n + 1)
                        for s, (_, cols, _) in enumerate(sources):
                            last = nc.vector.tensor_copy(g.stage_t[0:cols, r, s, :],
                                                         ps_turn[0:cols, r, s * P:(s + 1) * P])
                        last.then_inc(turn_kept, 1)
                        dve.wait_ge(product, n + 1 + RING)
                        for to, cols in keep:
                            last = nc.vector.tensor_copy(to[:, bass.ds(n, 1), :],
                                                         ps_out[:, r:r + 1, cols])
                        if tables:
                            dve.wait_ge(table_written[r],
                                        (i * (NODE_UNROLL // RING) + k // RING + 1) * (16 * len(tables)))
                            first, end = table_cols[0].start, table_cols[-1].stop
                            last = nc.vector.tensor_copy(g.row_stage[:, r, 0:end - first],
                                                         ps_out[:, r, first:end])
                        last.then_inc(kept, 1)

            if tables:
                @block.sync
                def _(sp):
                    for r in range(RING):
                        sp.sem_inc(table_written[r], 16 * len(tables))
                    with sp.Fori(0, NODE_ITERS) as i:
                        for k in range(NODE_UNROLL):
                            n = i * NODE_UNROLL + k
                            r = k % RING
                            sp.wait_ge(kept, n + 1 + RING)
                            for table, cols in zip(tables, table_cols):
                                at = cols.start - table_cols[0].start
                                sp.dma_start(
                                    table[:, :].rearrange("(n p) w -> p n w", p=P)[:, bass.ds(n, 1), :],
                                    g.row_stage[:, r:r + 1, at:at + cols.stop - cols.start])\
                                    .then_inc(table_written[r], 16)
                    for r in range(RING):
                        sp.wait_ge(table_written[r], 16 * len(tables) * (NT // RING + 1))


def table_store(nc, g, name, table, rows):
    with phase(nc, f"{name}_stored") as (block, stored):
        @block.sync
        def _(sp):
            sp.dma_start(table[:, :].rearrange("(n p) w -> p n w", p=P), rows).then_inc(stored, 16)
            sp.wait_ge(stored, 16)


def load_node_tiles(nc, g, engine, q):
    _, values = nc.values_load_multi_w_load_instructions(
        g.tile_row[0:1, bass.ds(q * GROUP, GROUP)], engines=[engine], min_val=0, max_val=NT - 1,
        skip_runtime_bounds_check_because="the plan counts at most NT - 1 starts for any edge tile")
    return values


def stage_indices(nc, g, act, idx_staged, rows_used, r, q):
    act.wait_ge(rows_used, q + 1)
    nc.scalar.activation(g.idx_stage[:, r, :], g.idx[:, bass.ds(q * GROUP, GROUP)], ACT.Copy)\
        .then_inc(idx_staged, 1)


def gather_loop(nc, g, table, width, ring, idx_staged, rows_landed, rows_used, group_begun, pool):
    with pool.Fori(0, STEPS) as i:
        for r in range(2):
            q = i * 2 + r
            pool.wait_ge(idx_staged, q + 1)
            pool.wait_ge(rows_used, q + 1)
            pool.sem_inc(group_begun, 1)
            for k in range(GROUP):
                nc.gpsimd.indirect_dma_start(
                    out=ring[:, r, k, 0:width], out_offset=None, in_=table[:, :],
                    in_offset=bass.IndirectOffsetOnAxis(ap=g.idx_stage[:, r, k:k + 1], axis=0),
                ).then_inc(rows_landed[r], 16)
    for r in range(2):
        pool.wait_ge(rows_landed[r], 16 * GROUP * STEPS)


def build_onehot(nc, g, dve, q, r):
    return nc.vector.tensor_tensor(
        g.onehot[:, r], g.iota[:].unsqueeze(1).to_broadcast([P, GROUP, P]),
        g.dloc[:, bass.ds(q * GROUP, GROUP)].unsqueeze(2).to_broadcast([P, GROUP, P]), ALU.is_equal)


def gat_scores(nc, g, l):
    with ExitStack() as ctx:
        ps_turn = ctx.enter_context(nc.psum_tensor("ps_turn", [P, 2, GROUP // 4, 512], F32, allow_name_mangling=True))
        ps_dst = ctx.enter_context(nc.psum_tensor("ps_dst", [P, 2, 512], F32, allow_name_mangling=True))
        rows_landed = g.rows_landed()
        with phase(nc, "group_begun", "idx_staged", "rows_used", "onehot_ready", "turned", "turn_kept", "dst_ready") as (
                block, group_begun, idx_staged, rows_used, onehot_ready, turned, turn_kept, dst_ready):
            @block.gpsimd
            def _(pool):
                gather_loop(nc, g, g.alpha_table, H, g.alpha_ring, idx_staged, rows_landed, rows_used, group_begun, pool)

            @block.scalar
            def _(act):
                act.sem_inc(turn_kept, 1)
                with act.Fori(0, STEPS) as i:
                    for r in range(2):
                        q = i * 2 + r
                        stage_indices(nc, g, act, idx_staged, rows_used, r, q)
                        act.wait_ge(turned, q + 1 + 2)
                        act.wait_ge(dst_ready, q + 2)
                        nc.scalar.activation(
                            g.onehot_t.rearrange("p (b k) e -> p b (k e)", b=GROUP // 4),
                            ps_turn[:, r], ACT.Copy).then_inc(turn_kept, 1)

            @block.tensor
            def _(pe):
                pe.sem_inc(turned, 2)
                pe.sem_inc(dst_ready, 2)
                with pe.Fori(0, STEPS) as i:
                    for r in range(2):
                        q = i * 2 + r
                        node_tiles = load_node_tiles(nc, g, mybir.EngineType.PE, q)
                        pe.wait_ge(onehot_ready, q + 1)
                        pe.wait_ge(turn_kept, q + 1)
                        for k in range(GROUP):
                            last = nc.tensor.transpose(ps_turn[:, r, k // 4, (k % 4) * P:(k % 4 + 1) * P],
                                                       g.onehot[:, r, k, :], g.ident[:])
                        last.then_inc(turned, 1)
                        pe.wait_ge(turn_kept, q + 2)
                        pe.wait_ge(rows_used, q + 1)
                        for k in range(GROUP):
                            last = nc.tensor.matmul(ps_dst[:, r:r + 1, k * H:(k + 1) * H], g.onehot_t[:, k, :],
                                                    g.alpha_dst[:, bass.ds(node_tiles[k], 1), :],
                                                    start=True, stop=True)
                        last.then_inc(dst_ready, 1)

            @block.vector
            def _(dve):
                dve.sem_inc(rows_used, 2)
                with dve.Fori(0, STEPS) as i:
                    for r in range(2):
                        q = i * 2 + r
                        dve.wait_ge(turned, q + 1)
                        build_onehot(nc, g, dve, q, r).then_inc(onehot_ready, 1)
                        dve.wait_ge(rows_landed[r], (i + 1) * (16 * GROUP))
                        dve.wait_ge(dst_ready, q + 1 + 2)
                        nc.vector.tensor_tensor(
                            g.scores[:, bass.ds(q * GROUP, GROUP), :], g.alpha_ring[:, r],
                            ps_dst[:, r, 0:GROUP * H].rearrange("p (k h) -> p k h", h=H), ALU.add)\
                            .then_inc(rows_used, 1)


def gat_softmax(nc, g, l):
    score_v = g.score_dram[:, :].rearrange("h (t e) -> t h e", e=P)
    weight_v = g.weight_dram[:, :].rearrange("h (t e) -> t h e", e=P)
    widths = [min(P, T - b * P) for b in range(TB)]
    with ExitStack() as ctx:
        ps_turn = ctx.enter_context(nc.psum_tensor("ps_turn", [P, 2, 512], F32, allow_name_mangling=True))
        ps_carry = ctx.enter_context(nc.psum_tensor("ps_carry", [P, 512], F32, allow_name_mangling=True))
        with phase(nc, "turned", "row_kept", "row_stored0", "row_stored1", "runs_loaded", "edge_scan",
                   "edge_turned", "carry_ready", "carry_turned", "below_max", "weighed", "weights_stored",
                   "weights_loaded", "back_turned", "back_kept", "scan_steps") as (
                block, turned, row_kept, row_stored0, row_stored1, runs_loaded, edge_scan, edge_turned,
                carry_ready, carry_turned, below_max, weighed, weights_stored, weights_loaded,
                back_turned, back_kept, scan_steps):
            row_stored = (row_stored0, row_stored1)

            @block.tensor
            def _(pe):
                for b, w in enumerate(widths):
                    if b >= 2:
                        pe.wait_ge(row_kept, b - 1)
                    for h in range(H):
                        last = nc.tensor.transpose(ps_turn[0:w, b % 2, h * P:(h + 1) * P],
                                                   g.scores[:, b * P:b * P + w, h], g.ident[:])
                    last.then_inc(turned, 1)
                for n in range(2):
                    edge = g.runs_fwd[:, :, T - 1] if n == 0 else g.scores_back[:, :, 0]
                    pe.wait_ge(edge_scan, n + 1)
                    nc.tensor.transpose(ps_carry[0:H, 0:P], edge, g.ident[:]).then_inc(edge_turned, 1)
                    pe.wait_ge(carry_ready, n + 1)
                    nc.tensor.transpose(ps_carry[:, P:P + H], g.carry[:, 1, :], g.ident[0:H, 0:H])\
                        .then_inc(carry_turned, 1)
                pe.wait_ge(weights_loaded, 16 * (H + 1))
                for b, w in enumerate(widths):
                    if b >= 2:
                        pe.wait_ge(back_kept, b - 1)
                    for h in range(H):
                        last = nc.tensor.transpose(ps_turn[:, b % 2, h * P:h * P + w],
                                                   g.weight_rows[0:w, b, h, :], g.ident[0:w, 0:w])
                    last.then_inc(back_turned, 1)

            @block.sync
            def _(sp):
                for b, w in enumerate(widths):
                    sp.wait_ge(row_kept, b + 1)
                    sp.dma_start(score_v[b * P:b * P + w], g.row_out[0:w, b % 2]).then_inc(row_stored[b % 2], 16)
                for r in range(2):
                    sp.wait_ge(row_stored[r], 16 * (TB // 2))
                sp.dma_start(g.runs, g.score_dram[:, 0:T * P].rearrange("h (p s) -> p h s", p=P))\
                    .then_inc(runs_loaded, 16)
                sp.wait_ge(weighed, 1)
                sp.dma_start(g.weight_dram[:, 0:T * P].rearrange("h (p s) -> p h s", p=P), g.runs)\
                    .then_inc(weights_stored, 16)
                sp.wait_ge(weights_stored, 16)
                full = (TB - 1) * P
                for h in range(H):
                    sp.dma_start(g.weight_rows[:, 0:TB - 1, h, :],
                                 g.weight_dram[h, 0:full * P].rearrange("(b t e) -> t b e", t=P, e=P))\
                        .then_inc(weights_loaded, 16)
                sp.dma_start(g.weight_rows[0:widths[-1], TB - 1], weight_v[full:T]).then_inc(weights_loaded, 16)
                sp.wait_ge(weights_loaded, 16 * (H + 1))

            @block.scalar
            def _(act):
                act.wait_ge(below_max, 1)
                nc.scalar.activation(g.runs, g.runs, ACT.Exp).then_inc(weighed, 1)

            @block.vector
            def _(dve):
                done = Chain(dve, scan_steps)
                for b, w in enumerate(widths):
                    dve.wait_ge(turned, b + 1)
                    if b >= 2:
                        dve.wait_ge(row_stored[b % 2], 16 * (b // 2))
                    ps = ps_turn[0:w, b % 2, :].rearrange("p (h e) -> p h e", h=H)
                    nc.vector.tensor_copy(g.row_out[0:w, b % 2], ps).then_inc(row_kept, 1)
                dve.wait_ge(runs_loaded, 16)
                done(nc.vector.scalar_tensor_tensor(out=g.runs, in0=g.runs, scalar=SLOPE, in1=g.runs,
                                                    op0=ALU.mult, op1=ALU.max))
                runs_back = g.scores_back

                def scan_fwd(h, initial):
                    return nc.vector.tensor_tensor_scan(
                        out=g.runs_fwd[:, h, :], data0=g.run_break[:, 0:T], data1=g.runs[:, h, :],
                        initial=initial, op0=ALU.add, op1=ALU.max)

                def scan_bwd(h, initial):
                    return nc.vector.tensor_tensor_scan(
                        out=runs_back[:, h, ::-1], data0=g.run_break[:, T:0:-1],
                        data1=g.runs_fwd[:, h, ::-1], initial=initial, op0=ALU.add, op1=ALU.max)

                for n, (scan, any_break) in enumerate(((scan_fwd, g.any_break_fwd), (scan_bwd, g.any_break_bwd))):
                    for h in range(H):
                        last = scan(h, -BIG)
                    last.then_inc(edge_scan, 1)
                    dve.wait_ge(edge_turned, n + 1)
                    done(nc.vector.tensor_copy(g.carry[:, 0, :], ps_carry[0:H, 0:P]))
                    done(nc.vector.memset(g.carry[:, 1, :], -BIG))
                    if n == 0:
                        nc.vector.tensor_tensor_scan(
                            out=g.carry[:, 1, 1:P], data0=any_break[:, 0:P - 1], data1=g.carry[:, 0, 0:P - 1],
                            initial=-BIG, op0=ALU.add, op1=ALU.max).then_inc(carry_ready, 1)
                    else:
                        nc.vector.tensor_tensor_scan(
                            out=g.carry[:, 1, P - 2::-1], data0=any_break[:, P - 1:0:-1],
                            data1=g.carry[:, 0, P - 1:0:-1],
                            initial=-BIG, op0=ALU.add, op1=ALU.max).then_inc(carry_ready, 1)
                    dve.wait_ge(carry_turned, n + 1)
                    done(nc.vector.tensor_copy(g.carry_col[:], ps_carry[:, P:P + H]))
                    for h in range(H):
                        done(scan(h, g.carry_col[:, h:h + 1]))
                nc.vector.tensor_tensor(g.runs, g.runs, runs_back, ALU.subtract).then_inc(below_max, 1)
                for b, w in enumerate(widths):
                    dve.wait_ge(back_turned, b + 1)
                    nc.vector.tensor_copy(
                        g.scores[:, b * P:b * P + w, :].rearrange("p t h -> p h t"),
                        ps_turn[:, b % 2, :].rearrange("p (h t) -> p h t", h=H)[:, :, 0:w]).then_inc(back_kept, 1)


def add_sums(nc, g, dve, done, ps_sum, node_tiles, r, width):
    for k in range(GROUP):
        sums = g.acc[:, bass.ds(node_tiles[k], 1), 0:width]
        part = ps_sum[:, r, k // 4:k // 4 + 1, (k % 4) * P:(k % 4) * P + width]
        done(nc.vector.tensor_tensor(sums, sums, part, ALU.add))


def sum_matmuls(nc, g, ps_sum, r, rows, width):
    for k in range(GROUP):
        last = nc.tensor.matmul(ps_sum[:, r, k // 4, (k % 4) * P:(k % 4) * P + width],
                                g.onehot[:, r, k, :], rows[:, r, k, 0:width], start=True, stop=True)
    return last


def gat_messages(nc, g, l):
    with ExitStack() as ctx:
        ps_sum = ctx.enter_context(nc.psum_tensor("ps_sum", [P, 2, GROUP // 4, 512], F32, allow_name_mangling=True))
        rows_landed = g.rows_landed()
        with phase(nc, "group_begun", "idx_staged", "rows_used", "onehot_ready", "weights_in_msg", "sums_ready",
                   "sum_steps") as (
                block, group_begun, idx_staged, rows_used, onehot_ready, weights_in_msg, sums_ready, sum_steps):
            @block.gpsimd
            def _(pool):
                gather_loop(nc, g, g.row_table, D, g.row_ring, idx_staged, rows_landed, rows_used, group_begun, pool)

            @block.scalar
            def _(act):
                with act.Fori(0, STEPS) as i:
                    for r in range(2):
                        q = i * 2 + r
                        stage_indices(nc, g, act, idx_staged, rows_used, r, q)
                        act.wait_ge(sums_ready, q + 1)
                        nc.scalar.activation(g.msg[:, r, :, D:D + H],
                                             g.scores[:, bass.ds(q * GROUP, GROUP), :], ACT.Copy)\
                            .then_inc(weights_in_msg, 1)

            @block.tensor
            def _(pe):
                pe.sem_inc(sums_ready, 2)
                with pe.Fori(0, STEPS) as i:
                    for r in range(2):
                        q = i * 2 + r
                        pe.wait_ge(onehot_ready, q + 1)
                        pe.wait_ge(weights_in_msg, q + 1)
                        pe.wait_ge(rows_used, q + 1 + 2)
                        sum_matmuls(nc, g, ps_sum, r, g.msg, D + H).then_inc(sums_ready, 1)

            @block.vector
            def _(dve):
                nc.vector.memset(g.acc_flat, 0.0).then_inc(sum_steps, 1)
                dve.wait_ge(sum_steps, 1)
                dve.sem_inc(rows_used, 2)
                with dve.Fori(0, STEPS) as i:
                    for r in range(2):
                        q = i * 2 + r
                        done = Chain(dve, sum_steps, q * GROUP + 1)
                        node_tiles = load_node_tiles(nc, g, mybir.EngineType.DVE, q)
                        dve.wait_ge(sums_ready, q + 1)
                        build_onehot(nc, g, dve, q, r).then_inc(onehot_ready, 1)
                        dve.wait_ge(rows_landed[r], (i + 1) * (16 * GROUP))
                        nc.vector.tensor_tensor(
                            g.msg[:, r, :, 0:D].rearrange("p k (h c) -> p k h c", h=H),
                            g.row_ring[:, r].rearrange("p k (h c) -> p k h c", h=H),
                            g.scores[:, bass.ds(q * GROUP, GROUP), :].unsqueeze(3)
                            .to_broadcast([P, GROUP, H, C]), ALU.mult).then_inc(rows_used, 1)
                        dve.wait_ge(sums_ready, q + 1 + 2)
                        add_sums(nc, g, dve, done, ps_sum, node_tiles, r, D + H)


def gat_finish(nc, g, l):
    with phase(nc, "finish_steps") as (block, finish_steps):
        @block.vector
        def _(dve):
            done = Chain(dve, finish_steps)
            done(nc.vector.tensor_scalar(out=g.recip[:], in0=g.acc[:, :, D:D + H], scalar1=1e-16,
                                         scalar2=None, op0=ALU.add))
            done(nc.vector.reciprocal(g.recip[:], g.recip[:]))
            done(nc.vector.tensor_tensor(
                g.h[:].rearrange("p n (h c) -> p n h c", h=H),
                g.acc[:, :, 0:D].rearrange("p n (h c) -> p n h c", h=H),
                g.recip[:].unsqueeze(3).to_broadcast([P, NT, H, C]), ALU.mult))
            done(nc.vector.tensor_tensor(g.h[:], g.h[:],
                                         g.bias[:, l, :].unsqueeze(1).to_broadcast([P, NT, D]), ALU.add))
            if l == 2:
                done(nc.vector.scalar_tensor_tensor(out=g.x[:], in0=g.h[:], scalar=0.0, in1=g.x[:],
                                                    op0=ALU.max, op1=ALU.add))


def attention(nc, g):
    with ExitStack() as ctx:
        ps_turn = ctx.enter_context(nc.psum_tensor("ps_turn", [P, GROUP // 4, 512], F32, allow_name_mangling=True))
        ps_query = ctx.enter_context(nc.psum_tensor("ps_query", [P, GROUP // 4, 512], F32, allow_name_mangling=True))
        ps_sum = ctx.enter_context(nc.psum_tensor("ps_sum", [P, 2, GROUP // 4, 512], F32, allow_name_mangling=True))
        rows_landed = g.rows_landed()
        with phase(nc, "group_begun", "idx_staged", "rows_used", "onehot_ready", "turned", "turn_kept", "query_ready",
                   "multiplied", "clipped", "weights_in_msg", "sums_ready", "sum_steps", "score_steps") as (
                block, group_begun, idx_staged, rows_used, onehot_ready, turned, turn_kept, query_ready,
                multiplied, clipped, weights_in_msg, sums_ready, sum_steps, score_steps):
            @block.gpsimd
            def _(pool):
                gather_loop(nc, g, g.kv_table, 2 * D, g.kv_ring, idx_staged, rows_landed, rows_used, group_begun, pool)

            @block.scalar
            def _(act):
                act.sem_inc(turn_kept, 1)
                with act.Fori(0, STEPS) as i:
                    for r in range(2):
                        q = i * 2 + r
                        stage_indices(nc, g, act, idx_staged, rows_used, r, q)
                        act.wait_ge(turned, q + 1)
                        act.wait_ge(query_ready, q + 1)
                        nc.scalar.activation(
                            g.onehot_t.rearrange("p (b k) e -> p b (k e)", b=GROUP // 4),
                            ps_turn[:], ACT.Copy).then_inc(turn_kept, 1)
                        act.wait_ge(clipped, q + 1)
                        act.wait_ge(sums_ready, q + 1)
                        nc.scalar.activation(g.msg[:, r, :, D:D + H], g.score8[:], ACT.Exp)\
                            .then_inc(weights_in_msg, 1)

            @block.tensor
            def _(pe):
                pe.sem_inc(sums_ready, 2)
                pe.sem_inc(query_ready, 1)
                with pe.Fori(0, STEPS) as i:
                    for r in range(2):
                        q = i * 2 + r
                        node_tiles = load_node_tiles(nc, g, mybir.EngineType.PE, q)
                        pe.wait_ge(onehot_ready, q + 1)
                        pe.wait_ge(turn_kept, q + 1)
                        for k in range(GROUP):
                            last = nc.tensor.transpose(ps_turn[:, k // 4, (k % 4) * P:(k % 4 + 1) * P],
                                                       g.onehot[:, r, k, :], g.ident[:])
                        last.then_inc(turned, 1)
                        pe.wait_ge(turn_kept, q + 2)
                        pe.wait_ge(multiplied, q + 1)
                        for k in range(GROUP):
                            last = nc.tensor.matmul(
                                ps_query[:, k // 4:k // 4 + 1, (k % 4) * D:(k % 4 + 1) * D], g.onehot_t[:, k, :],
                                g.query[:, bass.ds(node_tiles[k], 1), :], start=True, stop=True)
                        last.then_inc(query_ready, 1)
                        pe.wait_ge(weights_in_msg, q + 1)
                        pe.wait_ge(rows_used, q + 1 + 2)
                        sum_matmuls(nc, g, ps_sum, r, g.msg, D + H).then_inc(sums_ready, 1)

            @block.vector
            def _(dve):
                nc.vector.memset(g.acc_flat, 0.0).then_inc(sum_steps, 1)
                dve.wait_ge(sum_steps, 1)
                dve.sem_inc(rows_used, 2)
                dve.sem_inc(multiplied, 1)
                with dve.Fori(0, STEPS) as i:
                    for r in range(2):
                        q = i * 2 + r
                        done = Chain(dve, sum_steps, q * GROUP + 1)
                        node_tiles = load_node_tiles(nc, g, mybir.EngineType.DVE, q)
                        dve.wait_ge(sums_ready, q + 1)
                        build_onehot(nc, g, dve, q, r).then_inc(onehot_ready, 1)
                        dve.wait_ge(rows_landed[r], (i + 1) * (16 * GROUP))
                        dve.wait_ge(query_ready, q + 2)
                        keys = g.kv_ring[:, r, :, 0:D]
                        nc.vector.tensor_tensor(
                            keys.rearrange("p (b k) d -> p b k d", b=GROUP // 4),
                            keys.rearrange("p (b k) d -> p b k d", b=GROUP // 4),
                            ps_query[:, :, 0:4 * D].rearrange("p b (k d) -> p b k d", k=4), ALU.mult)\
                            .then_inc(multiplied, 1)
                        dve.wait_ge(multiplied, q + 2)
                        steps = Chain(dve, score_steps, q)
                        steps(nc.vector.tensor_reduce(
                            g.score8[:], keys.rearrange("p k (h c) -> p k h c", h=H), AX, ALU.add))
                        nc.vector.tensor_scalar(out=g.score8[:], in0=g.score8[:], scalar1=-10.0,
                                                scalar2=10.0, op0=ALU.max, op1=ALU.min).then_inc(clipped, 1)
                        dve.wait_ge(weights_in_msg, q + 1)
                        nc.vector.tensor_tensor(
                            g.msg[:, r, :, 0:D].rearrange("p k (h c) -> p k h c", h=H),
                            g.kv_ring[:, r, :, D:2 * D].rearrange("p k (h c) -> p k h c", h=H),
                            g.msg[:, r, :, D:D + H].unsqueeze(3)
                            .to_broadcast([P, GROUP, H, C]), ALU.mult).then_inc(rows_used, 1)
                        dve.wait_ge(sums_ready, q + 1 + 2)
                        add_sums(nc, g, dve, done, ps_sum, node_tiles, r, D + H)


def attention_finish(nc, g):
    with phase(nc, "finish_steps") as (block, finish_steps):
        @block.vector
        def _(dve):
            done = Chain(dve, finish_steps)
            done(nc.vector.tensor_scalar(out=g.recip[:], in0=g.acc[:, :, D:D + H], scalar1=1e-8,
                                         scalar2=None, op0=ALU.add))
            done(nc.vector.reciprocal(g.recip[:], g.recip[:]))
            done(nc.vector.tensor_tensor(
                g.query.rearrange("p n (h c) -> p n h c", h=H),
                g.acc[:, :, 0:D].rearrange("p n (h c) -> p n h c", h=H),
                g.recip[:].unsqueeze(3).to_broadcast([P, NT, H, C]), ALU.mult))
            done(nc.vector.tensor_tensor(g.x[:], g.x[:], g.h[:], ALU.add))
            done(nc.vector.tensor_tensor(g.x[:], g.x[:], g.query, ALU.add))


def plain_sums(nc, g):
    with ExitStack() as ctx:
        ps_sum = ctx.enter_context(nc.psum_tensor("ps_sum", [P, 2, GROUP // 4, 512], F32, allow_name_mangling=True))
        rows_landed = g.rows_landed()
        with phase(nc, "group_begun", "idx_staged", "rows_used", "onehot_ready", "ones_set", "sums_ready", "sum_steps") as (
                block, group_begun, idx_staged, rows_used, onehot_ready, ones_set, sums_ready, sum_steps):
            @block.gpsimd
            def _(pool):
                nc.gpsimd.memset(g.sum_ring[:, :, :, D:D + 1], 1.0).then_inc(ones_set, 1)
                gather_loop(nc, g, g.row_table, D, g.sum_ring, idx_staged, rows_landed, rows_used, group_begun, pool)

            @block.scalar
            def _(act):
                with act.Fori(0, STEPS) as i:
                    for r in range(2):
                        stage_indices(nc, g, act, idx_staged, rows_used, r, i * 2 + r)

            @block.tensor
            def _(pe):
                pe.wait_ge(ones_set, 1)
                pe.sem_inc(rows_used, 2)
                with pe.Fori(0, STEPS) as i:
                    for r in range(2):
                        q = i * 2 + r
                        pe.wait_ge(rows_landed[r], (i + 1) * (16 * GROUP))
                        pe.wait_ge(onehot_ready, q + 1)
                        pe.wait_ge(sums_ready, q + 1)
                        sum_matmuls(nc, g, ps_sum, r, g.sum_ring, D + 1).then_inc(rows_used, 1)

            @block.vector
            def _(dve):
                nc.vector.memset(g.acc_flat, 0.0).then_inc(sum_steps, 1)
                dve.wait_ge(sum_steps, 1)
                dve.sem_inc(sums_ready, 2)
                with dve.Fori(0, STEPS) as i:
                    for r in range(2):
                        q = i * 2 + r
                        done = Chain(dve, sum_steps, q * GROUP + 1)
                        node_tiles = load_node_tiles(nc, g, mybir.EngineType.DVE, q)
                        dve.wait_ge(rows_used, q + 1)
                        build_onehot(nc, g, dve, q, r).then_inc(onehot_ready, 1)
                        dve.wait_ge(rows_used, q + 1 + 2)
                        add_sums(nc, g, dve, done, ps_sum, node_tiles, r, D + 1)
                        dve.sem_inc(sums_ready, 1)
                last = Chain(dve, sum_steps, 2 * STEPS * GROUP + 1)
                last(nc.vector.memset(g.acc[:, :, D + 1:D + 2], 1.0))


def mean_finish(nc, g, out):
    with phase(nc, "finish_steps", "ready", "out_stored") as (block, finish_steps, ready, out_stored):
        @block.vector
        def _(dve):
            done = Chain(dve, finish_steps)
            done(nc.vector.tensor_scalar(out=g.spread[:], in0=g.acc[:, :, D], scalar1=1.0,
                                         scalar2=None, op0=ALU.max))
            done(nc.vector.reciprocal(g.spread[:], g.spread[:]))
            done(nc.vector.tensor_tensor(g.h[:], g.h[:], g.spread[:].unsqueeze(2).to_broadcast([P, NT, D]),
                                         ALU.mult))
            nc.vector.tensor_tensor(g.x[:], g.x[:], g.h[:], ALU.add).then_inc(ready, 1)

        @block.sync
        def _(sp):
            sp.wait_ge(ready, 1)
            sp.dma_start(out[0:N_FULL * P, :].rearrange("(n p) d -> p n d", p=P), g.x[:, 0:N_FULL, :])\
                .then_inc(out_stored, 16)
            sp.dma_start(out[N_FULL * P:N, :], g.x[0:N_TAIL, N_FULL, :]).then_inc(out_stored, 16)
            sp.wait_ge(out_stored, 32)


def gnn_kernel(nc, x, src, dst, gat_w, att_src, att_dst, gat_bias, qw, kw, vw, w0, b0, w1, b1, w2, b2,
               w3, b3, out):
    g = Graph()
    with ExitStack() as ctx:
        g.plan_fetched = ctx.enter_context(nc.semaphore("plan_fetched"))
        loops = [0]

        def rows_landed():
            loops[0] += 1
            return [ctx.enter_context(nc.semaphore(f"rows_landed{loops[0]}_{r}")) for r in range(2)]

        g.rows_landed = rows_landed
        allocate_small(nc, ctx, g)
        plan_edge_tiles(nc, g, src, dst)
        allocate_large(nc, ctx, g)
        load_inputs(nc, g, x, gat_w, att_src, att_dst, gat_bias, qw, kw, vw, w0, b0, w1, b1, w2, b2, w3, b3)

        normalise(nc, g)
        for l in range(3):
            node_matmul(nc, g, [(g.h[:], D, g.gat_w[:, l, :])], D + 2 * H, l > 0,
                        [(g.alpha_dst[:], slice(D + H, D + 2 * H))], (g.row_table, g.alpha_table),
                        (slice(0, D), slice(D, D + H)))
            gat_scores(nc, g, l)
            gat_softmax(nc, g, l)
            gat_messages(nc, g, l)
            gat_finish(nc, g, l)

        normalise(nc, g)
        node_matmul(nc, g, [(g.h[:], D, g.qkv_w[:])], 3 * D, False,
                    [(g.query, slice(0, D))], (g.kv_table,), (slice(D, 3 * D),))
        attention(nc, g)
        attention_finish(nc, g)

        normalise(nc, g)
        for i in range(2):
            table_store(nc, g, f"sum{i}", g.row_table, g.h[:])
            plain_sums(nc, g)
            node_matmul(nc, g, [(g.h[:], D, g.self_w[:, i, :]), (g.acc[:], D + 2, g.sum_w[:, i, :])],
                        D, False, [(g.h[:], slice(0, D))])
            standardise(nc, g, into_x=i == 1)

        normalise(nc, g)
        table_store(nc, g, "mean", g.row_table, g.h[:])
        plain_sums(nc, g)
        node_matmul(nc, g, [(g.acc[:], D + 1, g.mean_w[:])], D, False, [(g.h[:], slice(0, D))])
        mean_finish(nc, g, out)


_INS = ["x", "src", "dst", "L0_gnn_W", "L0_gnn_att_src", "L0_gnn_att_dst", "L0_gnn_bias", "L1_gnn_qW",
        "L1_gnn_kW", "L1_gnn_vW", "L2_gnn_W0", "L2_gnn_b0", "L2_gnn_W1", "L2_gnn_b1", "L2_gnn_W2",
        "L2_gnn_b2", "L3_gnn_W", "L3_gnn_b"]


def kernel(**inputs):
    import numpy as _np
    import concourse.bacc as _bacc
    from concourse import mybir as _mybir
    from concourse.bass_utils import run_bass_kernel_spmd as _run

    nc = _bacc.Bacc("TRN2", target_bir_lowering=False, num_devices=1)
    arrays, args = {}, []
    for name in _INS:
        a = _np.ascontiguousarray(inputs[name])
        arrays[f"in_{name}"] = a
        args.append(nc.dram_tensor(f"in_{name}", a.shape, _mybir.dt.from_np(a.dtype), kind="ExternalInput").ap())
    out = nc.dram_tensor("out", (N, D), F32, kind="ExternalOutput").ap()
    gnn_kernel(nc, *args, out)
    r = _run(nc, [arrays], core_ids=[0])
    return r.results[0]["out"]
```

```python
from contextlib import ExitStack, contextmanager

import numpy as np

import concourse.bass as bass
from concourse import mybir

P = 128
N, E, D, H = 12500, 212500, 96, 4
C = D // H
NT = -(-N // P)
N_FULL = N // P
N_TAIL = N - N_FULL * P
GROUP = 8
STEP = 2 * GROUP
T_MAX = (E + NT * (P - 1)) // P
STEPS = -(-T_MAX // STEP)
T = STEPS * STEP
TB = -(-T // P)
TP = TB * P
E_ROWS = 125
E_COLS = E // E_ROWS
assert E_ROWS * E_COLS == E
CHUNK = 80
CHUNKS = T // CHUNK
assert CHUNKS * CHUNK == T and CHUNK <= P
CHUNK_GROUPS = CHUNK // GROUP
LAG = 3
ROW_RING = 2 * CHUNK_GROUPS
NODE_UNROLL = 14
RING = 2
NODE_ITERS = NT // NODE_UNROLL
assert NODE_ITERS * NODE_UNROLL == NT
ACC_W = D + H
FAR = 1 << 20
PHASE_SEMS = 200
BIG = 1e30
LN_EPS = 1e-5
SLOPE = 0.2

F32 = mybir.dt.float32
BF16 = mybir.dt.bfloat16
I32 = mybir.dt.int32
U16 = mybir.dt.uint16
ALU = mybir.AluOpType
ACT = mybir.ActivationFunctionType
AX = mybir.AxisListType.X


class Chain:

    def __init__(self, eng, sem, base=0):
        self.eng, self.sem, self.count = eng, sem, base

    def __call__(self, instruction):
        instruction.then_inc(self.sem, 1)
        self.count = self.count + 1
        self.eng.wait_ge(self.sem, self.count)


@contextmanager
def phase(nc, *names):
    with ExitStack() as ctx:
        sems = [ctx.enter_context(nc.semaphore(name, num=PHASE_SEMS + n)) for n, name in enumerate(names)]
        with nc.Block() as block:
            yield (block, *sems)
        nc.all_engine_barrier(sems_to_clear=range(PHASE_SEMS, PHASE_SEMS + len(names)))


class Graph:
    pass


def allocate_small(nc, ctx, g):
    def sb(name, shape, dt=F32):
        return ctx.enter_context(nc.sbuf_tensor(name, shape, dt))

    g.ones = sb("ones", [P, P])
    g.ident = sb("ident", [P, P])
    g.iota = sb("iota", [P, P])
    g.idx = sb("idx", [P, TP], I32)
    g.dloc = sb("dloc", [P, TP], BF16)
    g.first_dloc = sb("first_dloc", [1, CHUNKS])
    g.tile_row = sb("tile_row", [1, TP], U16)
    g.src_pad = nc.dram_tensor("src_pad", (E + P,), I32)
    g.dst_pad = nc.dram_tensor("dst_pad", (E + P,), I32)
    g.key_dram = nc.dram_tensor("key_dram", (P + TP * P,), F32)
    g.tile_dram = nc.dram_tensor("tile_dram", (TP,), U16)
    g.break_dram = nc.dram_tensor("break_dram", (2, T), F32)
    g.gat_table = nc.dram_tensor("gat_table", (NT * P, D + H), F32)
    g.row_table = nc.dram_tensor("row_table", (NT * P, D), F32)
    g.kv_table = nc.dram_tensor("kv_table", (NT * P, 2 * D), F32)


def constants(nc, g, tile_no):
    with phase(nc, "const_steps") as (block, const_steps):
        @block.gpsimd
        def _(pool):
            done = Chain(pool, const_steps)
            done(nc.gpsimd.memset(g.ones[:], 1.0))
            done(nc.gpsimd.memset(g.ident[:], 0.0))
            done(nc.gpsimd.affine_select(out=g.ident[:], in_=g.ident[:], compare_op=ALU.not_equal,
                                         fill=1.0, base=0, pattern=[[-1, P]], channel_multiplier=1))
            done(nc.gpsimd.iota(g.iota[:], pattern=[[1, P]], base=0, channel_multiplier=0,
                                allow_small_or_imprecise_dtypes=True))
            done(nc.gpsimd.iota(tile_no[:], pattern=[[P, TB]], base=0, channel_multiplier=1,
                                allow_small_or_imprecise_dtypes=True))


def plan_edge_tiles(nc, g, src, dst):
    with ExitStack() as ctx:
        def sb(name, shape, dt=F32):
            return ctx.enter_context(nc.sbuf_tensor(name, shape, dt))

        def pb(name, shape):
            return ctx.enter_context(nc.psum_tensor(name, shape, F32))

        tile_no = sb("tile_no", [P, TB])
        dst_i = sb("dst_i", [E_ROWS, E_COLS], I32)
        dst_f = sb("dst_f", [E_ROWS, E_COLS])
        below = sb("below", [E_ROWS, E_COLS], BF16)
        count = sb("count", [E_ROWS, NT])
        tail = sb("tail", [1, 2 * P], I32)
        first = sb("first", [P, NT + 1])
        tiles = sb("tiles", [P, NT])
        tiles_i = sb("tiles_i", [P, NT], I32)
        zeros = sb("zeros", [P, NT])
        last_tile = sb("last_tile", [P, NT])
        shift = sb("shift", [P, NT])
        shift_step = sb("shift_step", [P, NT - 1])
        reached = sb("reached", [P, TB, NT - 1])
        weighted = sb("weighted", [P, TB, NT - 1])
        node_tile = sb("node_tile", [P, TB])
        node_tile_i = sb("node_tile_i", [P, TB], U16)
        start = sb("start", [P, TB])
        start_i = sb("start_i", [P, TB], I32)
        src_t = sb("src_t", [P, TB, P], I32)
        dst_t = sb("dst_t", [P, TB, P], I32)
        src_tf = sb("src_tf", [P, TB, P])
        dst_tf = sb("dst_tf", [P, TB, P])
        dloc_t = sb("dloc_t", [P, TB, P])
        mine = sb("mine", [P, TB, P])
        key = sb("key", [P, TB, P])
        key_pad = sb("key_pad", [1, P])
        ps_count = pb("ps_count", [P, 512])
        ps_t = pb("ps_t", [P, 2, 512])
        fetched = g.plan_fetched

        constants(nc, g, tile_no)

        with phase(nc, "dst_loaded", "pads_set", "copied", "counted", "summed", "starts_ready",
                   "plan_steps") as (
                block, dst_loaded, pads_set, copied, counted, summed, starts_ready, plan_steps):
            @block.sync
            def _(sp):
                sp.dma_start(dst_i[:], dst.rearrange("(r c) -> r c", r=E_ROWS)).then_inc(dst_loaded, 16)
                for n, (pad, given) in enumerate(((g.src_pad, src), (g.dst_pad, dst))):
                    sp.dma_start(pad[0:E].rearrange("(r c) -> r c", r=E_ROWS),
                                 given.rearrange("(r c) -> r c", r=E_ROWS)).then_inc(copied, 16)
                sp.wait_ge(pads_set, 2)
                for n, pad in enumerate((g.src_pad, g.dst_pad)):
                    sp.dma_start(pad[E:E + P].rearrange("(r c) -> r c", r=1),
                                 tail[:, n * P:(n + 1) * P]).then_inc(copied, 16)
                sp.wait_ge(copied, 64)

            @block.vector
            def _(dve):
                nc.vector.memset(tail[:, 0:P], 0).then_inc(pads_set, 1)
                nc.vector.memset(tail[:, P:2 * P], FAR).then_inc(pads_set, 1)
                done = Chain(dve, plan_steps)
                dve.wait_ge(dst_loaded, 16)
                done(nc.vector.tensor_copy(dst_f[:], dst_i[:]))
                count_done = Chain(dve, counted)
                for j in range(1, NT):
                    count_done(nc.vector.tensor_scalar(out=below[:], in0=dst_f[:], scalar1=float(j * P),
                                                       scalar2=None, op0=ALU.is_lt, op1=ALU.add,
                                                       accum_out=count[:, j:j + 1]))
                done(nc.vector.memset(first[:, 0:1], 0.0))
                done(nc.vector.memset(first[:, NT:NT + 1], float(E)))
                done(nc.vector.memset(zeros[:], 0.0))
                dve.wait_ge(summed, 1)
                done(nc.vector.tensor_copy(first[:, 1:NT], ps_count[:, 1:NT]))
                done(nc.vector.tensor_tensor(tiles[:], first[:, 1:NT + 1], first[:, 0:NT], ALU.subtract))
                done(nc.vector.tensor_scalar(out=tiles_i[:], in0=tiles[:], scalar1=float(P - 1),
                                             scalar2=None, op0=ALU.add))
                done(nc.vector.tensor_scalar(out=tiles_i[:], in0=tiles_i[:], scalar1=P.bit_length() - 1,
                                             scalar2=None, op0=ALU.arith_shift_right))
                done(nc.vector.tensor_copy(tiles[:], tiles_i[:]))
                done(nc.vector.tensor_tensor_scan(out=last_tile[:], data0=tiles[:], data1=zeros[:],
                                                  initial=0.0, op0=ALU.add, op1=ALU.add))
                done(nc.vector.memset(shift[:, 0:1], 0.0))
                done(nc.vector.scalar_tensor_tensor(out=shift[:, 1:NT], in0=last_tile[:, 0:NT - 1],
                                                    scalar=float(P), in1=first[:, 1:NT],
                                                    op0=ALU.mult, op1=ALU.subtract))
                done(nc.vector.tensor_tensor(shift_step[:], shift[:, 1:NT], shift[:, 0:NT - 1],
                                             ALU.subtract))
                done(nc.vector.tensor_tensor(
                    reached[:], last_tile[:, 0:NT - 1].unsqueeze(1).to_broadcast([P, TB, NT - 1]),
                    tile_no[:].unsqueeze(2).to_broadcast([P, TB, NT - 1]), ALU.is_le))
                done(nc.vector.tensor_reduce(node_tile[:], reached[:], AX, ALU.add))
                done(nc.vector.tensor_tensor(
                    weighted[:], reached[:], shift_step[:].unsqueeze(1).to_broadcast([P, TB, NT - 1]),
                    ALU.mult))
                done(nc.vector.tensor_reduce(start[:], weighted[:], AX, ALU.add))
                done(nc.vector.scalar_tensor_tensor(out=start[:], in0=tile_no[:], scalar=float(P),
                                                    in1=start[:], op0=ALU.mult, op1=ALU.subtract))
                done(nc.vector.tensor_scalar(out=start_i[:], in0=start[:], scalar1=float(E),
                                             scalar2=0.0, op0=ALU.min, op1=ALU.max))
                done(nc.vector.tensor_copy(node_tile_i[:], node_tile[:]))
                nc.vector.memset(key_pad[:], -1.0).then_inc(starts_ready, 1)

            @block.tensor
            def _(pe):
                pe.wait_ge(counted, NT - 1)
                nc.tensor.matmul(ps_count[:, 1:NT], g.ones[0:E_ROWS, :], count[:, 1:NT],
                                 start=True, stop=True).then_inc(summed, 1)

            @block.gpsimd
            def _(pool):
                pool.wait_ge(starts_ready, 1)
                pool.wait_ge(copied, 64)
                for b in range(TB):
                    for pad, got in ((g.src_pad, src_t), (g.dst_pad, dst_t)):
                        nc.gpsimd.indirect_dma_start(
                            out=got[:, b, :], out_offset=None,
                            in_=bass.AP(pad, 0, [[1, 1], [1, E + P]]),
                            in_offset=bass.IndirectOffsetOnAxis(ap=start_i[:, b:b + 1], axis=1),
                        ).then_inc(fetched, 16)
                pool.wait_ge(fetched, 32 * TB)

        with phase(nc, "key_ready", "key_stored", "turned", "turned_used", "layout_steps") as (
                block, key_ready, key_stored, turned, turned_used, layout_steps):
            @block.vector
            def _(dve):
                done = Chain(dve, layout_steps)
                done(nc.vector.tensor_copy(src_tf[:], src_t[:]))
                done(nc.vector.tensor_copy(dst_tf[:], dst_t[:]))
                node_tile_b = node_tile[:].unsqueeze(2).to_broadcast([P, TB, P])
                done(nc.vector.scalar_tensor_tensor(out=dloc_t[:], in0=node_tile_b, scalar=float(-P),
                                                    in1=dst_tf[:], op0=ALU.mult, op1=ALU.add))
                done(nc.vector.tensor_scalar(out=mine[:], in0=dloc_t[:], scalar1=float(P),
                                             scalar2=None, op0=ALU.is_lt))
                nc.vector.scalar_tensor_tensor(out=key[:], in0=dst_tf[:], scalar=1.0, in1=mine[:],
                                               op0=ALU.add, op1=ALU.mult).then_inc(key_ready, 1)
                for b in range(TB):
                    dve.wait_ge(turned, b + 1)
                    cols = slice(b * P, (b + 1) * P)
                    nc.vector.tensor_copy(g.idx[:, cols], ps_t[:, b % 2, 0:P])
                    nc.vector.tensor_copy(g.dloc[:, cols], ps_t[:, b % 2, P:2 * P]).then_inc(turned_used, 1)
                    if b == TB - 1:
                        dve.wait_ge(turned_used, TB)
                nc.vector.tensor_copy(g.first_dloc[:], g.dloc[0:1, 0:T:CHUNK])

            @block.tensor
            def _(pe):
                pe.wait_ge(key_ready, 1)
                for b in range(TB):
                    if b >= 2:
                        pe.wait_ge(turned_used, b - 1)
                    nc.tensor.transpose(ps_t[:, b % 2, 0:P], src_tf[:, b, :], g.ident[:])
                    nc.tensor.transpose(ps_t[:, b % 2, P:2 * P], dloc_t[:, b, :], g.ident[:])\
                        .then_inc(turned, 1)

            @block.sync
            def _(sp):
                key_slots = g.key_dram[P:P + TP * P].rearrange("(b t e) -> t b e", b=TB, t=P)
                sp.dma_start(g.key_dram[0:P].rearrange("(a e) -> a e", a=1), key_pad[:]).then_inc(key_stored, 16)
                sp.dma_start(g.tile_dram[:].rearrange("(b t) -> t b", t=P), node_tile_i[:],
                             allow_slow_non_contiguous=True).then_inc(key_stored, 16)
                sp.wait_ge(key_ready, 1)
                sp.dma_start(key_slots, key[:]).then_inc(key_stored, 16)
                sp.wait_ge(key_stored, 48)
                sp.dma_start(g.tile_row[:], g.tile_dram[:].rearrange("(a t) -> a t", a=1)).then_inc(key_stored, 16)
                sp.wait_ge(key_stored, 64)


def find_breaks(nc, g):
    keys = g.query_flat[0:CHUNK, 0:CHUNKS * (P + 2)].rearrange("p (c e) -> p c e", c=CHUNKS)
    row_break = g.query_flat[0:CHUNK, CHUNKS * (P + 2):CHUNKS * (P + 4)].rearrange("p (s c) -> p s c", s=2)
    with phase(nc, "keys_loaded", "breaks_ready", "breaks_stored", "break_steps") as (
            block, keys_loaded, breaks_ready, breaks_stored, break_steps):
        @block.vector
        def _(dve):
            done = Chain(dve, break_steps)
            dve.wait_ge(keys_loaded, 16)
            done(nc.vector.tensor_tensor(keys[:, :, 0:P + 1], keys[:, :, 0:P + 1], keys[:, :, 1:P + 2],
                                         ALU.not_equal))
            done(nc.vector.tensor_scalar(out=g.run_break, in0=keys[:, :, 0:P + 1], scalar1=-BIG,
                                         scalar2=None, op0=ALU.mult))
            done(nc.vector.tensor_reduce(row_break[:, 0, :], g.run_break[:, :, 0:P], AX, ALU.min))
            nc.vector.tensor_reduce(row_break[:, 1, :], g.run_break[:, :, 1:P + 1], AX, ALU.min)\
                .then_inc(breaks_ready, 1)

        @block.sync
        def _(sp):
            sp.dma_start(keys, bass.AP(g.key_dram, P - 1, [[P, CHUNK], [P * CHUNK, CHUNKS], [1, P + 2]]))\
                .then_inc(keys_loaded, 16)
            sp.wait_ge(breaks_ready, 1)
            for side in range(2):
                sp.dma_start(g.break_dram[side].rearrange("(c t) -> t c", t=CHUNK), row_break[:, side, :],
                             allow_slow_non_contiguous=True).then_inc(breaks_stored, 16)
            sp.wait_ge(breaks_stored, 32)
            sp.dma_start(g.any_break.rearrange("h s t -> h (s t)"),
                         g.break_dram[:, :].rearrange("(a s) t -> a (s t)", a=1).to_broadcast([H, 2 * T]))\
                .then_inc(breaks_stored, 16)
            sp.wait_ge(breaks_stored, 48)


def allocate_large(nc, ctx, g):
    def sb(name, shape, dt=F32):
        return ctx.enter_context(nc.sbuf_tensor(name, shape, dt))

    node = NT * D
    gather_ring = 2 * GROUP * 2 * D
    onehots = 2 * GROUP * P
    messages = 2 * GROUP * ACC_W
    edge_rings = gather_ring + onehots + GROUP * P + messages
    g.arena = sb("arena", [P, 3 * node + edge_rings])
    g.acc = sb("acc", [P, NT, ACC_W])
    g.alpha_dst = sb("alpha_dst", [P, NT, H])
    g.idx_stage = sb("idx_stage", [P, 2, GROUP], I32)
    g.score8 = sb("score8", [P, GROUP, H])
    g.gat_w = sb("gat_w", [D, 3, D + 2 * H])
    g.qkv_w = sb("qkv_w", [D, 3 * D])
    g.self_w = sb("self_w", [D, 2, D])
    g.sum_w = sb("sum_w", [D + 2, 2, D])
    g.mean_w = sb("mean_w", [D + 1, D])
    g.bias = sb("bias", [P, 3, D])
    g.mean = sb("mean", [P, NT])
    g.spread = sb("spread", [P, NT])
    g.recip = sb("recip", [P, NT, H])
    g.eps = sb("eps", [P, 1])
    g.acc_flat = g.acc[:].rearrange("p n w -> p (n w)")
    g.square = g.acc_flat[:, 0:NT * D].rearrange("p (n d) -> p n d", d=D)

    at = 0

    def take(size):
        nonlocal at
        at += size
        assert at <= 3 * node + edge_rings
        return g.arena[:, at - size:at]

    g.x = take(node).rearrange("p (n d) -> p n d", d=D)
    g.h = take(node).rearrange("p (n d) -> p n d", d=D)
    g.query_flat = take(node)
    g.query = g.query_flat.rearrange("p (n d) -> p n d", d=D)
    rings_at = at
    rows = take(gather_ring)
    g.kv_ring = rows.rearrange("p (r k w) -> p r k w", r=2, k=GROUP)
    g.sum_ring = rows[:, 0:2 * GROUP * (D + 1)].rearrange("p (r k w) -> p r k w", r=2, k=GROUP)
    g.onehot = take(onehots).rearrange("p (r k n) -> p r k n", r=2, k=GROUP)
    g.onehot_t = take(GROUP * P).rearrange("p (k e) -> p k e", k=GROUP)
    g.msg = take(messages).rearrange("p (r k w) -> p r k w", r=2, k=GROUP)
    at = rings_at
    g.stage = take(RING * 2 * (D + 2)).rearrange("p (r s w) -> p r s w", r=RING, s=2)
    g.stage_t = take(RING * 2 * P).rearrange("p (r s n) -> p r s n", r=RING, s=2)
    g.row_stage = take(RING * 2 * D).rearrange("p (r w) -> p r w", r=RING)
    g.any_break = take(2 * T)[0:H].rearrange("p (s t) -> p s t", s=2)
    g.run_break = take(-(-CHUNKS * (P + 1) // 2))[0:CHUNK].bitcast(BF16)[:, 0:CHUNKS * (P + 1)]\
        .rearrange("p (c e) -> p c e", c=CHUNKS)
    at = 0
    g.gat_rows = take(ROW_RING * GROUP * (D + H)).rearrange("p (t w) -> p t w", w=D + H)
    g.gat_ring = take(2 * GROUP * (D + H)).rearrange("p (r k w) -> p r k w", r=2, k=GROUP)
    g.gat_onehot_a, g.gat_onehot_b = (take(onehots).rearrange("p (r k n) -> p r k n", r=2, k=GROUP)
                                      for _ in range(2))
    g.gat_onehot_t = take(GROUP * P).rearrange("p (k e) -> p k e", k=GROUP)
    g.gat_msg = take(messages).rearrange("p (r k w) -> p r k w", r=2, k=GROUP)
    g.scores, g.weights = (take(CHUNK * H).rearrange("p (t h) -> p t h", h=H) for _ in range(2))
    g.score_rows, g.run_max, g.run_total = (
        take(H * P)[0:CHUNK].rearrange("p (h e) -> p h e", h=H) for _ in range(3))
    g.first_onehot = take(P)[0:1]
    g.carry_fwd = take(CHUNK + 1)[0:H]
    g.carry_bwd = take(CHUNK + 1)[0:H]
    g.carry_col = take(H)[0:CHUNK]
    g.drop = take(1)[0:H]
    g.chunk_break = take((P + 2) // 2)[0:CHUNK].bitcast(BF16)[:, 0:P + 1]
    g.chunk_end = take(CHUNK)[0:H]
    g.factor_row = take(H)[0:1]
    g.factor = take(H)
    assert at <= rings_at


def load_x(sp, g, x, x_loaded, tail_zeroed):
    sp.dma_start(g.x[:, 0:N_FULL, :], x[0:N_FULL * P, :].rearrange("(n p) d -> p n d", p=P))\
        .then_inc(x_loaded, 16)
    if tail_zeroed is not None:
        sp.wait_ge(tail_zeroed, 1)
    sp.dma_start(g.x[0:N_TAIL, N_FULL, :], x[N_FULL * P:N, :]).then_inc(x_loaded, 16)


def load_inputs(nc, g, x, gat_w, att_src, att_dst, gat_bias, qw, kw, vw, w0, b0, w1, b1, w2, b2, w3, b3):
    with ExitStack() as ctx:
        att = g.query_flat[0:D, 0:6 * H].rearrange("p (l s) -> p l s", l=3)
        w01, w2s = (g.query_flat[0:D, at:at + 4 * D].rearrange("p (i s d) -> p i s d", i=2, s=2)
                    for at in (D, 5 * D))
        w_t = g.query_flat[0:D, 9 * D:16 * D].rearrange("p (n d) -> p n d", n=7)
        b01 = g.query_flat[0:D, 16 * D:16 * D + 4].rearrange("p (i s) -> p i s", i=2)
        b2s = g.query_flat[0:1, 17 * D:19 * D].rearrange("p (i d) -> p i d", i=2)
        bias_rows = g.query_flat[0:1, 19 * D:23 * D].rearrange("p (i s d) -> p i s d", i=2, s=2)
        ps_w = ctx.enter_context(nc.psum_tensor("ps_w", [P, 2, 512], F32, allow_name_mangling=True))
        ps_m = ctx.enter_context(nc.psum_tensor("ps_m", [P, 512], F32, allow_name_mangling=True))
        with phase(nc, "zeroed", "loaded", "x_loaded", "w_turned", "w_kept", "product", "product_kept",
                   "rows_kept") as (
                block, zeroed, loaded, x_loaded, w_turned, w_kept, product, product_kept, rows_kept):
            n_att = 3 * 2 * H
            n_loads = n_att + 3 + 3 + 2 * 7 + 1 + 1 + 3

            @block.gpsimd
            def _(pool):
                nc.gpsimd.memset(g.x[:, N_FULL, :], 0.0).then_inc(zeroed, 1)
                nc.gpsimd.memset(att, 0.0).then_inc(zeroed, 1)
                nc.gpsimd.memset(g.eps[:], LN_EPS).then_inc(zeroed, 1)

            @block.sync
            def _(sp):
                def load(to, given):
                    sp.dma_start(to, given).then_inc(loaded, 16)

                for l in range(3):
                    load(g.gat_w[:, l, 0:D], gat_w[l])
                sp.wait_ge(zeroed, 3)
                for l in range(3):
                    for side, given in enumerate((att_src, att_dst)):
                        for h in range(H):
                            load(att[h * C:(h + 1) * C, l, side * H + h:side * H + h + 1],
                                 given[l, h].rearrange("(c a) -> c a", a=1))
                for i in range(2):
                    load(w01[:, i, 0, :], w0[i])
                    load(w01[:, i, 1, :], w1[i])
                    load(w2s[:, i, 0, :], w2[i, D:2 * D, :])
                    load(w2s[:, i, 1, :], w2[i, 0:D, :])
                    load(b01[:, i, 0:1], b0[i].rearrange("(c a) -> c a", a=1))
                    load(b01[:, i, 1:2], b1[i].rearrange("(c a) -> c a", a=1))
                    load(b2s[:, i, :], b2[i:i + 1, :])
                for n, w in enumerate((qw, kw, vw)):
                    load(g.qkv_w[:, n * D:(n + 1) * D], w)
                load(g.mean_w[0:D, :], w3)
                load(g.mean_w[D:D + 1, :], b3.rearrange("(a d) -> a d", a=1))
                for l in range(3):
                    load(g.bias[:, l, :], gat_bias[l:l + 1, :].to_broadcast([P, D]))
                load_x(sp, g, x, x_loaded, None)
                sp.wait_ge(loaded, 16 * n_loads)
                sp.wait_ge(x_loaded, 32)
                sp.wait_ge(product_kept, 11)
                for i in range(2):
                    for side in range(2):
                        sp.dma_start(g.sum_w[D + side:D + side + 1, i, :], bias_rows[:, i, side, :])\
                            .then_inc(rows_kept, 16)
                sp.wait_ge(rows_kept, 64)

            turns = [g.gat_w[:, l, 0:D] for l in range(3)] + [w01[:, i, s, :] for i in range(2) for s in range(2)]

            @block.tensor
            def _(pe):
                pe.wait_ge(loaded, 16 * n_loads)
                for n, w in enumerate(turns):
                    if n >= 2:
                        pe.wait_ge(w_kept, n - 1)
                    nc.tensor.transpose(ps_w[0:D, n % 2, 0:D], w, g.ident[0:D, 0:D]).then_inc(w_turned, 1)
                pe.wait_ge(w_kept, 7)
                done = 0
                for l in range(3):
                    pe.wait_ge(product_kept, done)
                    nc.tensor.matmul(ps_m[0:D, 0:2 * H], w_t[:, l, :], att[:, l, :], start=True, stop=True)\
                        .then_inc(product, 1)
                    done += 1
                for i in range(2):
                    for side in range(2):
                        pe.wait_ge(product_kept, done)
                        nc.tensor.matmul(ps_m[0:D, 0:D], w_t[:, 3 + 2 * i + side, :], w2s[:, i, side, :],
                                         start=True, stop=True).then_inc(product, 1)
                        done += 1
                        pe.wait_ge(product_kept, done)
                        m = nc.tensor.matmul(ps_m[0:1, 0:D], b01[:, i, side:side + 1], w2s[:, i, side, :],
                                             start=True, stop=side == 0)
                        if side == 1:
                            m = nc.tensor.matmul(ps_m[0:1, 0:D], g.ones[0:1, 0:1], b2s[:, i, :],
                                                 start=False, stop=True)
                        m.then_inc(product, 1)
                        done += 1

            @block.vector
            def _(dve):
                for n in range(7):
                    dve.wait_ge(w_turned, n + 1)
                    nc.vector.tensor_copy(w_t[:, n, :], ps_w[0:D, n % 2, 0:D]).then_inc(w_kept, 1)
                done = 0

                def keep(to, what):
                    nonlocal done
                    done += 1
                    dve.wait_ge(product, done)
                    nc.vector.tensor_copy(to, what).then_inc(product_kept, 1)

                for l in range(3):
                    keep(g.gat_w[:, l, D:D + 2 * H], ps_m[0:D, 0:2 * H])
                for i in range(2):
                    for side in range(2):
                        keep(g.sum_w[0:D, i, :] if side == 0 else g.self_w[:, i, :], ps_m[0:D, 0:D])
                        keep(bias_rows[:, i, side, :], ps_m[0:1, 0:D])


def normalise(nc, g):
    with phase(nc, "norm_steps", "var_ready", "std_ready") as (block, norm_steps, var_ready, std_ready):
        @block.vector
        def _(dve):
            done = Chain(dve, norm_steps)
            done(nc.vector.tensor_reduce(g.mean[:], g.x, AX, ALU.add))
            done(nc.vector.scalar_tensor_tensor(
                out=g.h, in0=g.mean[:].unsqueeze(2).to_broadcast([P, NT, D]), scalar=-1.0 / D,
                in1=g.x, op0=ALU.mult, op1=ALU.add))
            done(nc.vector.tensor_tensor(g.square, g.h, g.h, ALU.mult))
            nc.vector.tensor_reduce(g.spread[:], g.square, AX, ALU.add).then_inc(var_ready, 1)
            dve.wait_ge(std_ready, 1)
            done(nc.vector.reciprocal(g.spread[:], g.spread[:]))
            done(nc.vector.scalar_tensor_tensor(
                out=g.h, in0=g.h, scalar=0.0,
                in1=g.spread[:].unsqueeze(2).to_broadcast([P, NT, D]), op0=ALU.max, op1=ALU.mult))

        @block.scalar
        def _(act):
            act.wait_ge(var_ready, 1)
            nc.scalar.activation(g.spread[:], g.spread[:], ACT.Sqrt, bias=g.eps[:], scale=1.0 / D)\
                .then_inc(std_ready, 1)


def standardise(nc, g, into_x):
    with phase(nc, "sd_steps", "var_ready", "std_ready") as (block, sd_steps, var_ready, std_ready):
        @block.vector
        def _(dve):
            done = Chain(dve, sd_steps)
            done(nc.vector.tensor_reduce(g.mean[:], g.h, AX, ALU.add))
            done(nc.vector.scalar_tensor_tensor(
                out=g.square, in0=g.mean[:].unsqueeze(2).to_broadcast([P, NT, D]), scalar=-1.0 / D,
                in1=g.h, op0=ALU.mult, op1=ALU.add))
            done(nc.vector.tensor_tensor(g.square, g.square, g.square, ALU.mult))
            nc.vector.tensor_reduce(g.spread[:], g.square, AX, ALU.add).then_inc(var_ready, 1)
            dve.wait_ge(std_ready, 1)
            done(nc.vector.reciprocal(g.spread[:], g.spread[:]))
            done(nc.vector.tensor_tensor(g.h, g.h, g.spread[:].unsqueeze(2).to_broadcast([P, NT, D]),
                                         ALU.mult))
            if into_x:
                done(nc.vector.tensor_tensor(g.x, g.x, g.h, ALU.add))

        @block.scalar
        def _(act):
            act.wait_ge(var_ready, 1)
            nc.scalar.activation(g.spread[:], g.spread[:], ACT.Sqrt, scale=1.0 / (D - 1)).then_inc(std_ready, 1)


def node_matmul(nc, g, sources, width, relu_in, keep, tables=(), table_cols=()):
    with ExitStack() as ctx:
        ps_turn = ctx.enter_context(nc.psum_tensor("ps_turn", [P, 2, 512], F32, allow_name_mangling=True))
        ps_out = ctx.enter_context(nc.psum_tensor("ps_out", [P, 2, 512], F32, allow_name_mangling=True))
        with phase(nc, "staged", "turned", "turn_kept", "product", "kept", "table_written0",
                   "table_written1") as (
                block, staged, turned, turn_kept, product, kept, table_written0, table_written1):
            table_written = (table_written0, table_written1)
            @block.scalar
            def _(act):
                func = ACT.Relu if relu_in else ACT.Copy
                with act.Fori(0, NODE_ITERS) as i:
                    for k in range(NODE_UNROLL):
                        n = i * NODE_UNROLL + k
                        act.wait_ge(turned, n + 1)
                        for s, (rows, cols, _) in enumerate(sources):
                            last = nc.scalar.activation(
                                g.stage[:, k % RING, s:s + 1, 0:cols],
                                rows[:, bass.ds(n, 1), 0:cols], func)
                        last.then_inc(staged, 1)

            @block.tensor
            def _(pe):
                pe.sem_inc(turned, RING)
                pe.sem_inc(product, RING)
                with pe.Fori(0, NODE_ITERS) as i:
                    for k in range(NODE_UNROLL):
                        n = i * NODE_UNROLL + k
                        r = k % RING
                        pe.wait_ge(staged, n + 1)
                        pe.wait_ge(turn_kept, n + 1)
                        for s, (_, cols, _) in enumerate(sources):
                            last = nc.tensor.transpose(ps_turn[0:cols, r, s * P:(s + 1) * P],
                                                       g.stage[:, r, s, 0:cols], g.ident[:])
                        last.then_inc(turned, 1)
                        pe.wait_ge(turn_kept, n + 1 + RING)
                        pe.wait_ge(kept, n + 1)
                        for s, (_, cols, weights) in enumerate(sources):
                            last = nc.tensor.matmul(ps_out[:, r, 0:width],
                                                    g.stage_t[0:cols, r, s, :], weights,
                                                    start=s == 0, stop=s == len(sources) - 1)
                        last.then_inc(product, 1)

            @block.vector
            def _(dve):
                dve.sem_inc(turn_kept, RING)
                dve.sem_inc(kept, RING)
                with dve.Fori(0, NODE_ITERS) as i:
                    for k in range(NODE_UNROLL):
                        n = i * NODE_UNROLL + k
                        r = k % RING
                        dve.wait_ge(turned, n + 1 + RING)
                        dve.wait_ge(product, n + 1)
                        for s, (_, cols, _) in enumerate(sources):
                            last = nc.vector.tensor_copy(g.stage_t[0:cols, r, s, :],
                                                         ps_turn[0:cols, r, s * P:(s + 1) * P])
                        last.then_inc(turn_kept, 1)
                        dve.wait_ge(product, n + 1 + RING)
                        for to, cols in keep:
                            last = nc.vector.tensor_copy(to[:, bass.ds(n, 1), :],
                                                         ps_out[:, r:r + 1, cols])
                        if tables:
                            dve.wait_ge(table_written[r],
                                        (i * (NODE_UNROLL // RING) + k // RING + 1) * (16 * len(tables)))
                            first, end = table_cols[0].start, table_cols[-1].stop
                            last = nc.vector.tensor_copy(g.row_stage[:, r, 0:end - first],
                                                         ps_out[:, r, first:end])
                        last.then_inc(kept, 1)

            if tables:
                @block.sync
                def _(sp):
                    for r in range(RING):
                        sp.sem_inc(table_written[r], 16 * len(tables))
                    with sp.Fori(0, NODE_ITERS) as i:
                        for k in range(NODE_UNROLL):
                            n = i * NODE_UNROLL + k
                            r = k % RING
                            sp.wait_ge(kept, n + 1 + RING)
                            for table, cols in zip(tables, table_cols):
                                at = cols.start - table_cols[0].start
                                sp.dma_start(
                                    table[:, :].rearrange("(n p) w -> p n w", p=P)[:, bass.ds(n, 1), :],
                                    g.row_stage[:, r:r + 1, at:at + cols.stop - cols.start])\
                                    .then_inc(table_written[r], 16)
                    for r in range(RING):
                        sp.wait_ge(table_written[r], 16 * len(tables) * (NT // RING + 1))


def table_store(nc, g, name, table, rows):
    with phase(nc, f"{name}_stored") as (block, stored):
        @block.sync
        def _(sp):
            sp.dma_start(table[:, :].rearrange("(n p) w -> p n w", p=P), rows).then_inc(stored, 16)
            sp.wait_ge(stored, 16)


def load_node_tiles(nc, g, engine, q):
    _, values = nc.values_load_multi_w_load_instructions(
        g.tile_row[0:1, bass.ds(q * GROUP, GROUP)], engines=[engine], min_val=0, max_val=NT - 1,
        skip_runtime_bounds_check_because="the plan counts at most NT - 1 starts for any edge tile")
    return values


def stage_indices(nc, g, act, idx_staged, rows_used, r, q):
    act.wait_ge(rows_used, q + 1)
    nc.scalar.activation(g.idx_stage[:, r, :], g.idx[:, bass.ds(q * GROUP, GROUP)], ACT.Copy)\
        .then_inc(idx_staged, 1)


def gather_loop(nc, g, table, width, ring, idx_staged, rows_landed, rows_used, group_begun, pool):
    with pool.Fori(0, STEPS) as i:
        for r in range(2):
            q = i * 2 + r
            pool.wait_ge(idx_staged, q + 1)
            pool.wait_ge(rows_used, q + 1)
            pool.sem_inc(group_begun, 1)
            for k in range(GROUP):
                nc.gpsimd.indirect_dma_start(
                    out=ring[:, r, k, 0:width], out_offset=None, in_=table[:, :],
                    in_offset=bass.IndirectOffsetOnAxis(ap=g.idx_stage[:, r, k:k + 1], axis=0),
                ).then_inc(rows_landed[r], 16)
    for r in range(2):
        pool.wait_ge(rows_landed[r], 16 * GROUP * STEPS)


def build_onehot(nc, g, onehot, q, r):
    return nc.vector.tensor_tensor(
        onehot[:, r], g.iota[:].unsqueeze(1).to_broadcast([P, GROUP, P]),
        g.dloc[:, bass.ds(q * GROUP, GROUP)].unsqueeze(2).to_broadcast([P, GROUP, P]), ALU.is_equal)


def add_sums(nc, g, dve, done, ps_sum, node_tiles, width):
    for k in range(GROUP):
        sums = g.acc[:, bass.ds(node_tiles[k], 1), 0:width]
        part = ps_sum[:, k // 4:k // 4 + 1, (k % 4) * P:(k % 4) * P + width]
        done(nc.vector.tensor_tensor(sums, sums, part, ALU.add))


def sum_matmuls(nc, onehot, ps_sum, r, rows, width):
    for k in range(GROUP):
        last = nc.tensor.matmul(ps_sum[:, k // 4, (k % 4) * P:(k % 4) * P + width],
                                onehot[:, r, k, :], rows[:, r, k, 0:width], start=True, stop=True)
    return last


def gat_edges(nc, g, l):
    CG = CHUNK_GROUPS
    rows_landed = g.rows_landed()
    with ExitStack() as ctx:
        def pb(name, shape):
            return ctx.enter_context(nc.psum_tensor(name, shape, F32, allow_name_mangling=True))

        ps_turn = pb("ps_turn", [P, GROUP // 4, 512])
        ps_sum = pb("ps_sum", [P, GROUP // 4, 512])
        ps_dst = pb("ps_dst", [P, 512])[:, 0:GROUP * H].rearrange("p (k h) -> p k h", h=H)
        ps_rows = pb("ps_rows", [P, 512])
        ps_back = ps_rows[:, 0:H * CHUNK].rearrange("p (h t) -> p h t", h=H)
        ps_misc = pb("ps_misc", [P, 512])
        ps_edge, ps_carry = ps_misc[0:H, 0:CHUNK], ps_misc[0:CHUNK, CHUNK:CHUNK + H]
        ps_scale = pb("ps_scale", [P, 512])
        ps_factor_row, ps_factor = ps_scale[0:1, 0:H], ps_scale[:, H:2 * H]
        with phase(nc, "group_begun", "idx_staged0", "idx_staged1", "moved0", "moved1",
                   "onehot_a_ready", "turned", "turn_kept", "dst_ready", "scored",
                   "onehot_b_ready", "msg_built", "weights_in_msg", "summed", "acc_steps",
                   "rows_turned", "edge_ready", "edge_turned", "carry_ready", "carry_turned",
                   "below_max", "weighed", "back_turned", "weights_ready",
                   "drop_ready", "factor_ready", "factor_turned", "factor_row_ready", "factor_spread",
                   "soft_steps", "soft_turn", "move_begun") as (
                block, group_begun, idx_staged0, idx_staged1, moved0, moved1,
                onehot_a_ready, turned, turn_kept, dst_ready, scored,
                onehot_b_ready, msg_built, weights_in_msg, summed, acc_steps,
                rows_turned, edge_ready, edge_turned, carry_ready, carry_turned,
                below_max, weighed, back_turned, weights_ready,
                drop_ready, factor_ready, factor_turned, factor_row_ready, factor_spread,
                soft_steps, soft_turn, move_begun):
            idx_staged, moved = (idx_staged0, idx_staged1), (moved0, moved1)

            def walk(eng, body):
                body(0, True, None, None)
                body(1, True, LAG, CG)
                with eng.Fori(2, CHUNKS) as c:
                    body(c, True, 0, CG)
                body(CHUNKS, False, 0, CG)
                body(CHUNKS + 1, False, 0, LAG)

            def stage3_group(c, g_):
                return (c - 1) * CG + g_ - LAG, (c - 2 if g_ < LAG else c - 1), (g_ - LAG) % CG

            def has_softmax(c):
                return not isinstance(c, int) or 1 <= c <= CHUNKS

            @block.gpsimd
            def _(pool):
                with pool.Fori(0, STEPS) as i:
                    for r in range(2):
                        pool.wait_ge(idx_staged[r], (i + 1) * 16)
                        pool.wait_ge(moved[r], (i + 1) * 16)
                        pool.sem_inc(group_begun, 1)
                        for k in range(GROUP):
                            nc.gpsimd.indirect_dma_start(
                                out=g.gat_ring[:, r, k, :], out_offset=None, in_=g.gat_table[:, :],
                                in_offset=bass.IndirectOffsetOnAxis(ap=g.idx_stage[:, r, k:k + 1], axis=0),
                            ).then_inc(rows_landed[r], 16)
                for r in range(2):
                    pool.wait_ge(rows_landed[r], 16 * GROUP * STEPS)

            @block.sync
            def _(sp):
                def stage_indices(q, r):
                    sp.dma_start(g.idx_stage[:, r, :], g.idx[:, bass.ds(q * GROUP, GROUP)])\
                        .then_inc(idx_staged[r], 16)

                for r in range(2):
                    sp.sem_inc(moved[r], 16)
                    stage_indices(r, r)
                with sp.Fori(0, CHUNKS) as c:
                    with sp.Fori(0, CG // 2) as u:
                        for r in range(2):
                            q = c * CG + u * 2 + r
                            i = c * (CG // 2) + u
                            sp.wait_ge(rows_landed[r], (i + 1) * (16 * GROUP))
                            sp.wait_ge(msg_built, q + 1)
                            sp.sem_inc(move_begun, 1)
                            sp.dma_start(
                                g.gat_rows[:, bass.ds((c & 1) * CHUNK + (u * 2 + r) * GROUP, GROUP), :],
                                g.gat_ring[:, r]).then_inc(moved[r], 16)
                            stage_indices(q + 2, r)
                for r in range(2):
                    sp.wait_ge(moved[r], 16 * (STEPS + 1))
                    sp.wait_ge(idx_staged[r], 16 * (STEPS + 1))

            @block.scalar
            def _(act):
                act.sem_inc(turn_kept, 1)

                def body(c, stage1, first, end):
                    for g_ in range(CG):
                        r = g_ % 2
                        if first is not None and first <= g_ < end:
                            q, chunk, place = stage3_group(c, g_)
                            rm = (g_ - LAG) % 2
                            if place == 0:
                                act.wait_ge(weights_ready, chunk + 1)
                            act.wait_ge(summed, q + 1)
                            nc.scalar.activation(g.gat_msg[:, rm, :, D:D + H],
                                                 g.weights[:, place * GROUP:(place + 1) * GROUP, :], ACT.Copy)\
                                .then_inc(weights_in_msg, 1)
                        if stage1:
                            q = c * CG + g_
                            act.wait_ge(turned, q + 1 + 2)
                            act.wait_ge(dst_ready, q + 1)
                            nc.scalar.activation(
                                g.gat_onehot_t.rearrange("p (b k) e -> p b (k e)", b=GROUP // 4),
                                ps_turn[:], ACT.Copy).then_inc(turn_kept, 1)
                        if g_ == 1 and has_softmax(c):
                            act.wait_ge(drop_ready, c)
                            nc.scalar.activation(g.drop, g.drop, ACT.Exp).then_inc(factor_ready, 1)
                            act.wait_ge(below_max, c)
                            nc.scalar.activation(g.score_rows, g.score_rows, ACT.Exp).then_inc(weighed, 1)

                walk(act, body)

            @block.tensor
            def _(pe):
                pe.sem_inc(turned, 2)
                pe.sem_inc(dst_ready, 1)
                pe.sem_inc(summed, 2)

                def turn(to, what, n):
                    return nc.tensor.transpose(to, what, g.ident[0:n, 0:n])

                def soft(c, point):
                    if not has_softmax(c):
                        return
                    if point == "start":
                        pe.wait_ge(scored, c * CG + 2)
                        for h in range(H):
                            last = turn(ps_rows[0:CHUNK, h * P:(h + 1) * P], g.scores[:, :, h], P)
                        last.then_inc(rows_turned, 1)
                    elif point in ((0, 0), (0, 2)):
                        n = (c - 1) * 2 + (point == (0, 2)) + 1
                        pe.wait_ge(edge_ready, n)
                        edge = g.run_max[:, :, P - 1] if point == (0, 0) else g.run_total[:, :, 0]
                        pe.sem_inc(soft_turn, 1)
                        turn(ps_edge, edge, CHUNK).then_inc(edge_turned, 1)
                    elif point in ((0, 1), (1, 0)):
                        n = (c - 1) * 2 + (point == (1, 0)) + 1
                        pe.wait_ge(carry_ready, n)
                        carry = g.carry_fwd[:, 0:CHUNK] if point == (0, 1) else g.carry_bwd[:, 1:CHUNK + 1]
                        pe.sem_inc(soft_turn, 1)
                        turn(ps_carry, carry, H).then_inc(carry_turned, 1)
                    elif point == (1, 1):
                        pe.wait_ge(factor_ready, c)
                        pe.sem_inc(soft_turn, 1)
                        turn(ps_factor_row, g.drop, H).then_inc(factor_turned, 1)
                    elif point == (1, 2):
                        pe.wait_ge(weighed, c)
                        for h in range(H):
                            last = turn(ps_back[:, h, :], g.score_rows[:, h, :], CHUNK)
                        last.then_inc(back_turned, 1)
                    elif point == (2, 0):
                        pe.wait_ge(factor_row_ready, c)
                        nc.tensor.matmul(ps_factor, g.first_onehot, g.factor_row, start=True, stop=True)\
                            .then_inc(factor_spread, 1)

                def body(c, stage1, first, end):
                    soft(c, "start")
                    for g_ in range(CG):
                        r = g_ % 2
                        q1 = c * CG + g_
                        if stage1:
                            node_tiles = load_node_tiles(nc, g, mybir.EngineType.PE, q1)
                            pe.wait_ge(onehot_a_ready, q1 + 1)
                            pe.wait_ge(turn_kept, q1 + 1)
                            for k in range(GROUP):
                                last = turn(ps_turn[:, k // 4, (k % 4) * P:(k % 4 + 1) * P],
                                            g.gat_onehot_a[:, r, k, :], P)
                            last.then_inc(turned, 1)
                        soft(c, (g_, 0))
                        if first is not None and first <= g_ < end:
                            q, _, _ = stage3_group(c, g_)
                            rm = (g_ - LAG) % 2
                            pe.wait_ge(onehot_b_ready, q + 1)
                            pe.wait_ge(weights_in_msg, q + 1)
                            pe.wait_ge(msg_built, q + 1 + ROW_RING)
                            pe.wait_ge(acc_steps, q * GROUP + 1)
                            sum_matmuls(nc, g.gat_onehot_b, ps_sum, rm, g.gat_msg, D + H).then_inc(summed, 1)
                        soft(c, (g_, 1))
                        if stage1:
                            pe.wait_ge(turn_kept, q1 + 2)
                            pe.wait_ge(scored, q1 + 2)
                            for k in range(GROUP):
                                last = nc.tensor.matmul(
                                    ps_dst[:, k:k + 1, :], g.gat_onehot_t[:, k, :],
                                    g.alpha_dst[:, bass.ds(node_tiles[k], 1), :], start=True, stop=True)
                            last.then_inc(dst_ready, 1)
                        soft(c, (g_, 2))

                walk(pe, body)

            @block.vector
            def _(dve):
                nc.vector.memset(g.acc_flat, 0.0).then_inc(acc_steps, 1)
                dve.wait_ge(acc_steps, 1)
                dve.sem_inc(scored, 2)
                dve.sem_inc(msg_built, ROW_RING)
                opened = Chain(dve, soft_steps)
                opened(nc.vector.memset(g.carry_fwd, -BIG))
                opened(nc.vector.memset(g.carry_bwd, -BIG))
                SOFT = 2 * H + 12

                def add_scores(c, g_):
                    q = c * CG + g_
                    r = g_ % 2
                    dve.wait_ge(dst_ready, q + 1 + 1)
                    dve.wait_ge(moved[r], (c * (CG // 2) + g_ // 2 + 2) * 16)
                    if has_softmax(c):
                        dve.wait_ge(rows_turned, c)
                    nc.vector.tensor_tensor(
                        g.scores[:, g_ * GROUP:(g_ + 1) * GROUP, :],
                        g.gat_rows[:, bass.ds((c & 1) * CHUNK + g_ * GROUP, GROUP), D:D + H],
                        ps_dst, ALU.add).then_inc(scored, 1)

                def add_group(c, g_):
                    q, _, _ = stage3_group(c, g_)
                    node_tiles = load_node_tiles(nc, g, mybir.EngineType.DVE, q)
                    dve.wait_ge(summed, q + 1 + 2)
                    add_sums(nc, g, dve, Chain(dve, acc_steps, q * GROUP + 1), ps_sum, node_tiles,
                             D + H)

                state = {}

                def soft(c, point):
                    if not has_softmax(c):
                        return
                    cc = c - 1
                    if point == (0, 0):
                        state["done"] = Chain(dve, soft_steps, cc * SOFT + 2)
                    done = state.get("done")
                    tiles = bass.ds(cc * CHUNK, CHUNK)

                    def scan_fwd(h, initial):
                        return nc.vector.tensor_tensor_scan(
                            out=g.run_max[:, h, :], data0=g.chunk_break[:, 0:P], data1=g.score_rows[:, h, :],
                            initial=initial, op0=ALU.add, op1=ALU.max)

                    def scan_bwd(h, initial):
                        return nc.vector.tensor_tensor_scan(
                            out=g.run_total[:, h, ::-1], data0=g.chunk_break[:, P:0:-1],
                            data1=g.run_max[:, h, ::-1], initial=initial, op0=ALU.add, op1=ALU.max)

                    if point == (0, 0):
                        dve.wait_ge(rows_turned, c)
                        done(nc.vector.tensor_copy(g.chunk_end, g.any_break[:, 1, tiles]))
                        done(nc.vector.tensor_copy(
                            g.chunk_break, g.run_break[:, bass.ds(cc, 1), :].rearrange("p a e -> p (a e)")))
                        rows = ps_rows[0:CHUNK, :].rearrange("p (h e) -> p h e", h=H)
                        done(nc.vector.tensor_scalar(out=g.run_max, in0=rows, scalar1=SLOPE,
                                                     scalar2=None, op0=ALU.mult))
                        done(nc.vector.tensor_tensor(g.score_rows, g.run_max, rows, ALU.max))
                        for h in range(H):
                            last = scan_fwd(h, -BIG)
                        last.then_inc(edge_ready, 1)
                    elif point == (0, 1):
                        dve.wait_ge(edge_turned, cc * 2 + 1)
                        nc.vector.tensor_tensor_scan(
                            out=g.carry_fwd[:, 1:CHUNK + 1], data0=g.any_break[:, 0, tiles], data1=ps_edge,
                            initial=g.carry_fwd[:, 0:1], op0=ALU.add, op1=ALU.max).then_inc(carry_ready, 1)
                    elif point == (0, 2):
                        dve.wait_ge(carry_turned, cc * 2 + 1)
                        done(nc.vector.tensor_copy(g.carry_col, ps_carry))
                        for h in range(H):
                            done(scan_fwd(h, g.carry_col[:, h:h + 1]))
                        for h in range(H):
                            last = scan_bwd(h, -BIG)
                        last.then_inc(edge_ready, 1)
                    elif point == (1, 0):
                        dve.wait_ge(edge_turned, cc * 2 + 2)
                        nc.vector.tensor_tensor_scan(
                            out=g.carry_bwd[:, CHUNK - 1::-1], data0=g.chunk_end[:, ::-1],
                            data1=ps_edge[:, ::-1], initial=-BIG, op0=ALU.add, op1=ALU.max)\
                            .then_inc(carry_ready, 1)
                    elif point == (1, 1):
                        dve.wait_ge(carry_ready, cc * 2 + 2)
                        done(nc.vector.tensor_tensor(g.drop, g.carry_fwd[:, 0:1], g.carry_bwd[:, 0:1],
                                                     ALU.subtract))
                        nc.vector.tensor_scalar(out=g.drop, in0=g.drop, scalar1=0.0, scalar2=None,
                                                op0=ALU.min).then_inc(drop_ready, 1)
                        dve.wait_ge(carry_turned, cc * 2 + 2)
                        done(nc.vector.tensor_copy(g.carry_fwd[:, 0:1], g.carry_fwd[:, CHUNK:CHUNK + 1]))
                        done(nc.vector.tensor_copy(g.carry_col, ps_carry))
                        for h in range(H):
                            done(scan_bwd(h, g.carry_col[:, h:h + 1]))
                        nc.vector.tensor_tensor(g.score_rows, g.score_rows, g.run_total, ALU.subtract)\
                            .then_inc(below_max, 1)
                    elif point == (1, 2):
                        dve.wait_ge(factor_turned, c)
                        done(nc.vector.tensor_scalar(
                            out=g.first_onehot, in0=g.iota[0:1, :],
                            scalar1=g.first_dloc[0:1, bass.ds(cc, 1)], scalar2=None, op0=ALU.is_equal))
                        nc.vector.tensor_scalar(out=g.factor_row, in0=ps_factor_row, scalar1=-1.0,
                                                scalar2=None, op0=ALU.add).then_inc(factor_row_ready, 1)
                    elif point == (2, 1):
                        dve.wait_ge(back_turned, c)
                        if not (isinstance(c, int) and c == 1):
                            dve.wait_ge(weights_in_msg, cc * CG)
                            dve.wait_ge(msg_built, cc * CG + ROW_RING)
                        nc.vector.tensor_copy(g.weights.rearrange("p t h -> p h t"), ps_back)\
                            .then_inc(weights_ready, 1)
                    elif point == (2, 2):
                        dve.wait_ge(factor_spread, c)
                        done(nc.vector.tensor_scalar(out=g.factor, in0=ps_factor, scalar1=1.0,
                                                     scalar2=None, op0=ALU.add))
                        state["scale"] = True

                def scale_open_node(c):
                    cc = c - 1
                    done = state["done"]
                    node_tile = nc.values_load(
                        g.tile_row[0:1, bass.ds(cc * CHUNK, 1)], engines=[mybir.EngineType.DVE],
                        min_val=0, max_val=NT - 1,
                        skip_runtime_bounds_check_because="the plan counts at most NT - 1 starts")
                    sums = g.acc[:, bass.ds(node_tile, 1), 0:D].rearrange("p a (h c) -> p (a h) c", h=H)
                    done(nc.vector.tensor_tensor(sums, sums, g.factor.unsqueeze(2).to_broadcast([P, H, C]),
                                                 ALU.mult))
                    sums = g.acc[:, bass.ds(node_tile, 1), D:D + H].rearrange("p a h -> p (a h)")
                    done(nc.vector.tensor_tensor(sums, sums, g.factor, ALU.mult))

                def body(c, stage1, first, end):
                    if isinstance(c, int) and c == 0:
                        left_scores = left_sums = False
                    else:
                        left_scores = not isinstance(c, int) or c <= CHUNKS
                        left_sums = not isinstance(c, int) or c >= 2
                    for g_ in range(CG):
                        r = g_ % 2
                        q1 = c * CG + g_
                        stage3 = first is not None and first <= g_ < end
                        if g_ == 0 and left_scores:
                            add_scores(c - 1, CG - 1)
                        if stage1:
                            dve.wait_ge(turned, q1 + 1)
                            build_onehot(nc, g, g.gat_onehot_a, q1, r).then_inc(onehot_a_ready, 1)
                        if stage3:
                            q, chunk, place = stage3_group(c, g_)
                            rm = (g_ - LAG) % 2
                            dve.wait_ge(summed, q + 1)
                            build_onehot(nc, g, g.gat_onehot_b, q, rm).then_inc(onehot_b_ready, 1)
                        soft(c, (g_, 0))
                        if stage3:
                            if place == 0:
                                dve.wait_ge(weights_ready, chunk + 1)
                            nc.vector.tensor_tensor(
                                g.gat_msg[:, rm, :, 0:D].rearrange("p k (h c) -> p k h c", h=H),
                                g.gat_rows[:, bass.ds((chunk & 1) * CHUNK + place * GROUP, GROUP), 0:D]
                                .rearrange("p k (h c) -> p k h c", h=H),
                                g.weights[:, place * GROUP:(place + 1) * GROUP, :].unsqueeze(3)
                                .to_broadcast([P, GROUP, H, C]), ALU.mult).then_inc(msg_built, 1)
                        soft(c, (g_, 1))
                        if stage1 and g_ > 0:
                            add_scores(c, g_ - 1)
                        if g_ == 0:
                            if left_sums:
                                add_group(c - 1, CG - 1)
                        elif first is not None and first <= g_ - 1 < end:
                            add_group(c, g_ - 1)
                        soft(c, (g_, 2))
                        if g_ == LAG and has_softmax(c):
                            scale_open_node(c)
                            assert not isinstance(state["done"].count, int) or \
                                state["done"].count == c * SOFT + 2, state["done"].count

                walk(dve, body)


def gat_finish(nc, g, l, x):
    with phase(nc, "finish_steps", "tail_zeroed", "x_loaded") as (
            block, finish_steps, tail_zeroed, x_loaded):
        if l == 2:
            @block.gpsimd
            def _(pool):
                nc.gpsimd.memset(g.x[:, N_FULL, :], 0.0).then_inc(tail_zeroed, 1)

            @block.sync
            def _(sp):
                load_x(sp, g, x, x_loaded, tail_zeroed)

        @block.vector
        def _(dve):
            done = Chain(dve, finish_steps)
            done(nc.vector.tensor_scalar(out=g.recip[:], in0=g.acc[:, :, D:D + H], scalar1=1e-16,
                                         scalar2=None, op0=ALU.add))
            done(nc.vector.reciprocal(g.recip[:], g.recip[:]))
            done(nc.vector.tensor_tensor(
                g.h.rearrange("p n (h c) -> p n h c", h=H),
                g.acc[:, :, 0:D].rearrange("p n (h c) -> p n h c", h=H),
                g.recip[:].unsqueeze(3).to_broadcast([P, NT, H, C]), ALU.mult))
            done(nc.vector.tensor_tensor(g.h, g.h,
                                         g.bias[:, l, :].unsqueeze(1).to_broadcast([P, NT, D]), ALU.add))
            if l == 2:
                dve.wait_ge(x_loaded, 32)
                done(nc.vector.scalar_tensor_tensor(out=g.x, in0=g.h, scalar=0.0, in1=g.x,
                                                    op0=ALU.max, op1=ALU.add))


def attention(nc, g):
    with ExitStack() as ctx:
        ps_turn = ctx.enter_context(nc.psum_tensor("ps_turn", [P, GROUP // 4, 512], F32, allow_name_mangling=True))
        ps_query = ctx.enter_context(nc.psum_tensor("ps_query", [P, GROUP // 4, 512], F32, allow_name_mangling=True))
        ps_sum = ctx.enter_context(nc.psum_tensor("ps_sum", [P, 2, GROUP // 4, 512], F32, allow_name_mangling=True))
        rows_landed = g.rows_landed()
        with phase(nc, "group_begun", "idx_staged", "rows_used", "onehot_ready", "turned", "turn_kept", "query_ready",
                   "multiplied", "clipped", "weights_in_msg", "sums_ready", "sum_steps", "score_steps") as (
                block, group_begun, idx_staged, rows_used, onehot_ready, turned, turn_kept, query_ready,
                multiplied, clipped, weights_in_msg, sums_ready, sum_steps, score_steps):
            @block.gpsimd
            def _(pool):
                gather_loop(nc, g, g.kv_table, 2 * D, g.kv_ring, idx_staged, rows_landed, rows_used, group_begun, pool)

            @block.scalar
            def _(act):
                act.sem_inc(turn_kept, 1)
                with act.Fori(0, STEPS) as i:
                    for r in range(2):
                        q = i * 2 + r
                        stage_indices(nc, g, act, idx_staged, rows_used, r, q)
                        act.wait_ge(turned, q + 1)
                        act.wait_ge(query_ready, q + 1)
                        nc.scalar.activation(
                            g.onehot_t.rearrange("p (b k) e -> p b (k e)", b=GROUP // 4),
                            ps_turn[:], ACT.Copy).then_inc(turn_kept, 1)
                        act.wait_ge(clipped, q + 1)
                        act.wait_ge(sums_ready, q + 1)
                        nc.scalar.activation(g.msg[:, r, :, D:D + H], g.score8[:], ACT.Exp)\
                            .then_inc(weights_in_msg, 1)

            @block.tensor
            def _(pe):
                pe.sem_inc(sums_ready, 2)
                pe.sem_inc(query_ready, 1)
                with pe.Fori(0, STEPS) as i:
                    for r in range(2):
                        q = i * 2 + r
                        node_tiles = load_node_tiles(nc, g, mybir.EngineType.PE, q)
                        pe.wait_ge(onehot_ready, q + 1)
                        pe.wait_ge(turn_kept, q + 1)
                        for k in range(GROUP):
                            last = nc.tensor.transpose(ps_turn[:, k // 4, (k % 4) * P:(k % 4 + 1) * P],
                                                       g.onehot[:, r, k, :], g.ident[:])
                        last.then_inc(turned, 1)
                        pe.wait_ge(turn_kept, q + 2)
                        pe.wait_ge(multiplied, q + 1)
                        for k in range(GROUP):
                            last = nc.tensor.matmul(
                                ps_query[:, k // 4:k // 4 + 1, (k % 4) * D:(k % 4 + 1) * D], g.onehot_t[:, k, :],
                                g.query[:, bass.ds(node_tiles[k], 1), :], start=True, stop=True)
                        last.then_inc(query_ready, 1)
                        pe.wait_ge(weights_in_msg, q + 1)
                        pe.wait_ge(rows_used, q + 1 + 2)
                        sum_matmuls(nc, g.onehot, ps_sum[:, r], r, g.msg, D + H).then_inc(sums_ready, 1)

            @block.vector
            def _(dve):
                nc.vector.memset(g.acc_flat, 0.0).then_inc(sum_steps, 1)
                dve.wait_ge(sum_steps, 1)
                dve.sem_inc(rows_used, 2)
                dve.sem_inc(multiplied, 1)
                with dve.Fori(0, STEPS) as i:
                    for r in range(2):
                        q = i * 2 + r
                        done = Chain(dve, sum_steps, q * GROUP + 1)
                        node_tiles = load_node_tiles(nc, g, mybir.EngineType.DVE, q)
                        dve.wait_ge(sums_ready, q + 1)
                        build_onehot(nc, g, g.onehot, q, r).then_inc(onehot_ready, 1)
                        dve.wait_ge(rows_landed[r], (i + 1) * (16 * GROUP))
                        dve.wait_ge(query_ready, q + 2)
                        keys = g.kv_ring[:, r, :, 0:D]
                        nc.vector.tensor_tensor(
                            keys.rearrange("p (b k) d -> p b k d", b=GROUP // 4),
                            keys.rearrange("p (b k) d -> p b k d", b=GROUP // 4),
                            ps_query[:, :, 0:4 * D].rearrange("p b (k d) -> p b k d", k=4), ALU.mult)\
                            .then_inc(multiplied, 1)
                        dve.wait_ge(multiplied, q + 2)
                        steps = Chain(dve, score_steps, q)
                        steps(nc.vector.tensor_reduce(
                            g.score8[:], keys.rearrange("p k (h c) -> p k h c", h=H), AX, ALU.add))
                        nc.vector.tensor_scalar(out=g.score8[:], in0=g.score8[:], scalar1=-10.0,
                                                scalar2=10.0, op0=ALU.max, op1=ALU.min).then_inc(clipped, 1)
                        dve.wait_ge(weights_in_msg, q + 1)
                        nc.vector.tensor_tensor(
                            g.msg[:, r, :, 0:D].rearrange("p k (h c) -> p k h c", h=H),
                            g.kv_ring[:, r, :, D:2 * D].rearrange("p k (h c) -> p k h c", h=H),
                            g.msg[:, r, :, D:D + H].unsqueeze(3)
                            .to_broadcast([P, GROUP, H, C]), ALU.mult).then_inc(rows_used, 1)
                        dve.wait_ge(sums_ready, q + 1 + 2)
                        add_sums(nc, g, dve, done, ps_sum[:, r], node_tiles, D + H)


def attention_finish(nc, g):
    with phase(nc, "finish_steps") as (block, finish_steps):
        @block.vector
        def _(dve):
            done = Chain(dve, finish_steps)
            done(nc.vector.tensor_scalar(out=g.recip[:], in0=g.acc[:, :, D:D + H], scalar1=1e-8,
                                         scalar2=None, op0=ALU.add))
            done(nc.vector.reciprocal(g.recip[:], g.recip[:]))
            done(nc.vector.tensor_tensor(
                g.query.rearrange("p n (h c) -> p n h c", h=H),
                g.acc[:, :, 0:D].rearrange("p n (h c) -> p n h c", h=H),
                g.recip[:].unsqueeze(3).to_broadcast([P, NT, H, C]), ALU.mult))
            done(nc.vector.tensor_tensor(g.x, g.x, g.h, ALU.add))
            done(nc.vector.tensor_tensor(g.x, g.x, g.query, ALU.add))


def plain_sums(nc, g):
    with ExitStack() as ctx:
        ps_sum = ctx.enter_context(nc.psum_tensor("ps_sum", [P, 2, GROUP // 4, 512], F32, allow_name_mangling=True))
        rows_landed = g.rows_landed()
        with phase(nc, "group_begun", "idx_staged", "rows_used", "onehot_ready", "ones_set", "sums_ready", "sum_steps") as (
                block, group_begun, idx_staged, rows_used, onehot_ready, ones_set, sums_ready, sum_steps):
            @block.gpsimd
            def _(pool):
                nc.gpsimd.memset(g.sum_ring[:, :, :, D:D + 1], 1.0).then_inc(ones_set, 1)
                gather_loop(nc, g, g.row_table, D, g.sum_ring, idx_staged, rows_landed, rows_used, group_begun, pool)

            @block.scalar
            def _(act):
                with act.Fori(0, STEPS) as i:
                    for r in range(2):
                        stage_indices(nc, g, act, idx_staged, rows_used, r, i * 2 + r)

            @block.tensor
            def _(pe):
                pe.wait_ge(ones_set, 1)
                pe.sem_inc(rows_used, 2)
                with pe.Fori(0, STEPS) as i:
                    for r in range(2):
                        q = i * 2 + r
                        pe.wait_ge(rows_landed[r], (i + 1) * (16 * GROUP))
                        pe.wait_ge(onehot_ready, q + 1)
                        pe.wait_ge(sums_ready, q + 1)
                        sum_matmuls(nc, g.onehot, ps_sum[:, r], r, g.sum_ring, D + 1).then_inc(rows_used, 1)

            @block.vector
            def _(dve):
                nc.vector.memset(g.acc_flat, 0.0).then_inc(sum_steps, 1)
                dve.wait_ge(sum_steps, 1)
                dve.sem_inc(sums_ready, 2)
                with dve.Fori(0, STEPS) as i:
                    for r in range(2):
                        q = i * 2 + r
                        done = Chain(dve, sum_steps, q * GROUP + 1)
                        node_tiles = load_node_tiles(nc, g, mybir.EngineType.DVE, q)
                        dve.wait_ge(rows_used, q + 1)
                        build_onehot(nc, g, g.onehot, q, r).then_inc(onehot_ready, 1)
                        dve.wait_ge(rows_used, q + 1 + 2)
                        add_sums(nc, g, dve, done, ps_sum[:, r], node_tiles, D + 1)
                        dve.sem_inc(sums_ready, 1)
                last = Chain(dve, sum_steps, 2 * STEPS * GROUP + 1)
                last(nc.vector.memset(g.acc[:, :, D + 1:D + 2], 1.0))


def mean_finish(nc, g, out):
    with phase(nc, "finish_steps", "ready", "out_stored") as (block, finish_steps, ready, out_stored):
        @block.vector
        def _(dve):
            done = Chain(dve, finish_steps)
            done(nc.vector.tensor_scalar(out=g.spread[:], in0=g.acc[:, :, D], scalar1=1.0,
                                         scalar2=None, op0=ALU.max))
            done(nc.vector.reciprocal(g.spread[:], g.spread[:]))
            done(nc.vector.tensor_tensor(g.h, g.h, g.spread[:].unsqueeze(2).to_broadcast([P, NT, D]),
                                         ALU.mult))
            nc.vector.tensor_tensor(g.x, g.x, g.h, ALU.add).then_inc(ready, 1)

        @block.sync
        def _(sp):
            sp.wait_ge(ready, 1)
            sp.dma_start(out[0:N_FULL * P, :].rearrange("(n p) d -> p n d", p=P), g.x[:, 0:N_FULL, :])\
                .then_inc(out_stored, 16)
            sp.dma_start(out[N_FULL * P:N, :], g.x[0:N_TAIL, N_FULL, :]).then_inc(out_stored, 16)
            sp.wait_ge(out_stored, 32)


def gnn_kernel(nc, x, src, dst, gat_w, att_src, att_dst, gat_bias, qw, kw, vw, w0, b0, w1, b1, w2, b2,
               w3, b3, out):
    g = Graph()
    with ExitStack() as ctx:
        g.plan_fetched = ctx.enter_context(nc.semaphore("plan_fetched"))
        loops = [0]

        def rows_landed():
            loops[0] += 1
            return [ctx.enter_context(nc.semaphore(f"rows_landed{loops[0]}_{r}")) for r in range(2)]

        g.rows_landed = rows_landed
        allocate_small(nc, ctx, g)
        plan_edge_tiles(nc, g, src, dst)
        allocate_large(nc, ctx, g)
        load_inputs(nc, g, x, gat_w, att_src, att_dst, gat_bias, qw, kw, vw, w0, b0, w1, b1, w2, b2, w3, b3)

        find_breaks(nc, g)

        normalise(nc, g)
        for l in range(3):
            node_matmul(nc, g, [(g.h, D, g.gat_w[:, l, :])], D + 2 * H, l > 0,
                        [(g.alpha_dst[:], slice(D + H, D + 2 * H))], (g.gat_table,), (slice(0, D + H),))
            gat_edges(nc, g, l)
            gat_finish(nc, g, l, x)

        normalise(nc, g)
        node_matmul(nc, g, [(g.h, D, g.qkv_w[:])], 3 * D, False,
                    [(g.query, slice(0, D))], (g.kv_table,), (slice(D, 3 * D),))
        attention(nc, g)
        attention_finish(nc, g)

        normalise(nc, g)
        for i in range(2):
            table_store(nc, g, f"sum{i}", g.row_table, g.h)
            plain_sums(nc, g)
            node_matmul(nc, g, [(g.h, D, g.self_w[:, i, :]), (g.acc[:], D + 2, g.sum_w[:, i, :])],
                        D, False, [(g.h, slice(0, D))])
            standardise(nc, g, into_x=i == 1)

        normalise(nc, g)
        table_store(nc, g, "mean", g.row_table, g.h)
        plain_sums(nc, g)
        node_matmul(nc, g, [(g.acc[:], D + 1, g.mean_w[:])], D, False, [(g.h, slice(0, D))])
        mean_finish(nc, g, out)


_INS = ["x", "src", "dst", "L0_gnn_W", "L0_gnn_att_src", "L0_gnn_att_dst", "L0_gnn_bias", "L1_gnn_qW",
        "L1_gnn_kW", "L1_gnn_vW", "L2_gnn_W0", "L2_gnn_b0", "L2_gnn_W1", "L2_gnn_b1", "L2_gnn_W2",
        "L2_gnn_b2", "L3_gnn_W", "L3_gnn_b"]


def kernel(**inputs):
    import numpy as _np
    import concourse.bacc as _bacc
    from concourse import mybir as _mybir
    from concourse.bass_utils import run_bass_kernel_spmd as _run

    nc = _bacc.Bacc("TRN2", target_bir_lowering=False, num_devices=1)
    arrays, args = {}, []
    for name in _INS:
        a = _np.ascontiguousarray(inputs[name])
        arrays[f"in_{name}"] = a
        args.append(nc.dram_tensor(f"in_{name}", a.shape, _mybir.dt.from_np(a.dtype), kind="ExternalInput").ap())
    out = nc.dram_tensor("out", (N, D), F32, kind="ExternalOutput").ap()
    gnn_kernel(nc, *args, out)
    r = _run(nc, [arrays], core_ids=[0])
    return r.results[0]["out"]
```

```python
from contextlib import ExitStack, contextmanager

import numpy as np

import concourse.bass as bass
from concourse import mybir

P = 128
N, E, D, H = 12500, 212500, 96, 4
C = D // H
NT = -(-N // P)
N_FULL = N // P
N_TAIL = N - N_FULL * P
GROUP = 8
STEP = 2 * GROUP
T_MAX = (E + NT * (P - 1)) // P
STEPS = -(-T_MAX // STEP)
T = STEPS * STEP
TB = -(-T // P)
TP = TB * P
E_ROWS = 125
E_COLS = E // E_ROWS
assert E_ROWS * E_COLS == E
SORT_COLS = 10
SORT_STEPS = E_COLS // (2 * SORT_COLS)
assert SORT_STEPS * 2 * SORT_COLS == E_COLS and NT % 2 == 0
CHUNK = 80
CHUNKS = T // CHUNK
assert CHUNKS * CHUNK == T and CHUNK <= P
CHUNK_GROUPS = CHUNK // GROUP
LAG = 3
ROW_RING = 2 * CHUNK_GROUPS
NODE_UNROLL = 14
RING = 2
NODE_ITERS = NT // NODE_UNROLL
STORED = NODE_UNROLL // 2
assert NODE_ITERS * NODE_UNROLL == NT
ACC_W = D + H
FAR = 1 << 20
PHASE_SEMS = 200
BIG = 1e30
LN_EPS = 1e-5
SLOPE = 0.2

F32 = mybir.dt.float32
BF16 = mybir.dt.bfloat16
I32 = mybir.dt.int32
U16 = mybir.dt.uint16
ALU = mybir.AluOpType
ACT = mybir.ActivationFunctionType
AX = mybir.AxisListType.X


class Chain:

    def __init__(self, eng, sem, base=0):
        self.eng, self.sem, self.count = eng, sem, base

    def __call__(self, instruction):
        instruction.then_inc(self.sem, 1)
        self.count = self.count + 1
        self.eng.wait_ge(self.sem, self.count)


@contextmanager
def phase(nc, *names):
    with ExitStack() as ctx:
        sems = [ctx.enter_context(nc.semaphore(name, num=PHASE_SEMS + n)) for n, name in enumerate(names)]
        with nc.Block() as block:
            yield (block, *sems)
        nc.all_engine_barrier(sems_to_clear=range(PHASE_SEMS, PHASE_SEMS + len(names)))


class Graph:
    pass


def allocate_small(nc, ctx, g):
    def sb(name, shape, dt=F32):
        return ctx.enter_context(nc.sbuf_tensor(name, shape, dt))

    g.ones = sb("ones", [P, P])
    g.ident = sb("ident", [P, P])
    g.iota = sb("iota", [P, P])
    g.part_no = sb("part_no", [P, 1])
    g.idx = sb("idx", [P, TP], I32)
    g.dloc = sb("dloc", [P, TP], BF16)
    g.first_dloc = sb("first_dloc", [1, CHUNKS])
    g.tile_row = sb("tile_row", [1, TP], U16)
    g.far_pad = nc.dram_tensor("far_pad", (E + P,), I32)
    g.own_pad = nc.dram_tensor("own_pad", (E + P,), I32)
    g.edge_pairs = nc.dram_tensor("edge_pairs", (E, 2), I32)
    g.idx_dram = nc.dram_tensor("idx_dram", (2, P, TP), I32)
    g.dloc_dram = nc.dram_tensor("dloc_dram", (2, P, TP), BF16)
    g.dloc_row_dram = nc.dram_tensor("dloc_row_dram", (2, TP * P), BF16)
    g.tile_row_dram = nc.dram_tensor("tile_row_dram", (2, TP), U16)
    g.key_dram = nc.dram_tensor("key_dram", (P + TP * P,), F32)
    g.tile_dram = nc.dram_tensor("tile_dram", (TP,), U16)
    g.break_dram = nc.dram_tensor("break_dram", (2, T), F32)
    g.gat_table = nc.dram_tensor("gat_table", (NT * P, D + H), F32)
    g.row_table = nc.dram_tensor("row_table", (NT * P, D), F32)
    g.kv_table = nc.dram_tensor("kv_table", (NT * P, 2 * D), F32)


def constants(nc, g, tile_no):
    with phase(nc, "const_steps") as (block, const_steps):
        @block.gpsimd
        def _(pool):
            done = Chain(pool, const_steps)
            done(nc.gpsimd.memset(g.ones[:], 1.0))
            done(nc.gpsimd.memset(g.ident[:], 0.0))
            done(nc.gpsimd.affine_select(out=g.ident[:], in_=g.ident[:], compare_op=ALU.not_equal,
                                         fill=1.0, base=0, pattern=[[-1, P]], channel_multiplier=1))
            done(nc.gpsimd.iota(g.iota[:], pattern=[[1, P]], base=0, channel_multiplier=0,
                                allow_small_or_imprecise_dtypes=True))
            done(nc.gpsimd.iota(g.part_no[:], pattern=[[1, 1]], base=0, channel_multiplier=1,
                                allow_small_or_imprecise_dtypes=True))
            done(nc.gpsimd.iota(tile_no[:], pattern=[[P, TB]], base=0, channel_multiplier=1,
                                allow_small_or_imprecise_dtypes=True))


class Buffers:
    pass


def plan_edge_tiles(nc, g, src, dst):
    with ExitStack() as ctx:
        def sb(name, shape, dt=F32):
            return ctx.enter_context(nc.sbuf_tensor(name, shape, dt))

        def pb(name, shape):
            return ctx.enter_context(nc.psum_tensor(name, shape, F32))

        b = Buffers()
        b.tile_no = sb("tile_no", [P, TB])
        b.own_i = sb("own_i", [E_ROWS, E_COLS], I32)
        b.far_i = sb("far_i", [E_ROWS, E_COLS], I32)
        b.node_tile_i = sb("edge_node_tile_i", [E_ROWS, E_COLS], I32)
        b.node_tile = sb("edge_node_tile", [E_ROWS, E_COLS], BF16)
        b.below = sb("below", [E_ROWS, E_COLS], BF16)
        b.source_count = sb("source_count", [E_ROWS, NT + 1])
        b.destination_count = sb("destination_count", [E_ROWS, NT + 1])
        b.tail = sb("tail", [1, 2 * P], I32)
        b.key_pad = sb("key_pad", [1, P])
        b.ps_count = pb("ps_count", [P, 512])
        b.ps_t = pb("ps_t", [P, 2, 512])

        constants(nc, g, b.tile_no)
        lists_and_tails(nc, g, b, src, dst)
        load_ends(nc, g, b, src, dst)
        sort_by_source(nc, g, b)
        lay_out(nc, g, b, 0, b.source_count)
        lists_and_tails(nc, g, b, src, dst)
        lay_out(nc, g, b, 1, b.destination_count)


def lists_and_tails(nc, g, b, src, dst):
    with phase(nc, "pads_set", "copied") as (block, pads_set, copied):
        @block.vector
        def _(dve):
            nc.vector.memset(b.tail[:, 0:P], 0).then_inc(pads_set, 1)
            nc.vector.memset(b.tail[:, P:2 * P], FAR).then_inc(pads_set, 1)

        @block.sync
        def _(sp):
            for pad, given in ((g.far_pad, src), (g.own_pad, dst)):
                sp.dma_start(pad[0:E].rearrange("(r c) -> r c", r=E_ROWS),
                             given.rearrange("(r c) -> r c", r=E_ROWS)).then_inc(copied, 16)
            sp.wait_ge(pads_set, 2)
            for n, pad in enumerate((g.far_pad, g.own_pad)):
                sp.dma_start(pad[E:E + P].rearrange("(r c) -> r c", r=1),
                             b.tail[:, n * P:(n + 1) * P]).then_inc(copied, 16)
            sp.wait_ge(copied, 64)


def load_ends(nc, g, b, src, dst):
    with phase(nc, "own_loaded", "far_loaded", "count_steps") as (block, own_loaded, far_loaded, count_steps):
        @block.sync
        def _(sp):
            sp.dma_start(b.own_i[:], src.rearrange("(r c) -> r c", r=E_ROWS)).then_inc(own_loaded, 16)
            sp.dma_start(b.far_i[:], dst.rearrange("(r c) -> r c", r=E_ROWS)).then_inc(far_loaded, 16)
            sp.wait_ge(far_loaded, 16)

        @block.vector
        def _(dve):
            dve.wait_ge(own_loaded, 16)
            count_below(nc, b, Chain(dve, count_steps), b.own_i, b.source_count)


def count_below(nc, b, done, ends, count):
    done(nc.vector.tensor_scalar(out=b.node_tile_i[:], in0=ends[:], scalar1=P.bit_length() - 1,
                                 scalar2=None, op0=ALU.arith_shift_right))
    done(nc.vector.tensor_copy(b.node_tile[:], b.node_tile_i[:]))
    done(nc.vector.memset(count[:, 0:1], 0.0))
    done(nc.vector.memset(count[:, NT:NT + 1], float(E_COLS)))
    for j in range(1, NT):
        done(nc.vector.tensor_scalar(out=b.below[:], in0=b.node_tile[:], scalar1=float(j), scalar2=None,
                                     op0=ALU.is_lt, op1=ALU.add, accum_out=count[:, j:j + 1]))


def sort_by_source(nc, g, b):
    with ExitStack() as ctx:
        def sb(name, shape, dt=F32):
            return ctx.enter_context(nc.sbuf_tensor(name, shape, dt))

        earlier = sb("earlier", [E_ROWS, E_ROWS])
        in_tile = sb("in_tile", [E_ROWS, NT])
        base = sb("base", [E_ROWS, NT])
        mask = sb("mask", [E_ROWS, 2, E_COLS], BF16)
        running = sb("running", [E_ROWS, 2, E_COLS])
        masked = sb("masked", [E_ROWS, 2, E_COLS])
        place = sb("place", [E_ROWS, E_COLS])
        pairs = sb("pairs", [E_ROWS, E_COLS, 2], I32)
        place_stage = sb("place_stage", [E_ROWS, 2, SORT_COLS], I32)
        pair_stage = sb("pair_stage", [E_ROWS, 2, SORT_COLS, 2], I32)

        with phase(nc, "earlier_ready", "in_tile_ready", "base_summed", "base_steps",
                   "masks_ready", "running_ready", "masked_ready", "added") as (
                block, earlier_ready, in_tile_ready, base_summed, base_steps,
                masks_ready, running_ready, masked_ready, added):
            @block.gpsimd
            def _(pool):
                done = Chain(pool, earlier_ready)
                done(nc.gpsimd.memset(earlier[:], 1.0))
                done(nc.gpsimd.affine_select(out=earlier[:], in_=earlier[:], compare_op=ALU.is_gt,
                                             fill=0.0, base=0, pattern=[[1, E_ROWS]],
                                             channel_multiplier=-1))
                nc.gpsimd.memset(place[:], -1.0).then_inc(added, 2)
                with pool.Fori(0, NT // 2) as i:
                    for r in range(2):
                        j = i * 2 + r
                        pool.wait_ge(masked_ready, j + 1)
                        pool.wait_ge(added, j + 2)
                        nc.gpsimd.tensor_tensor(place[:], place[:], masked[:, r, :], ALU.add)\
                            .then_inc(added, 1)

            @block.tensor
            def _(pe):
                pe.wait_ge(earlier_ready, 2)
                pe.wait_ge(in_tile_ready, 1)
                nc.tensor.matmul(b.ps_count[0:E_ROWS, 0:NT], g.ones[0:E_ROWS, 0:E_ROWS],
                                 b.source_count[:, 0:NT], start=True, stop=False)
                nc.tensor.matmul(b.ps_count[0:E_ROWS, 0:NT], earlier[:], in_tile[:],
                                 start=False, stop=True).then_inc(base_summed, 1)

            @block.vector
            def _(dve):
                done = Chain(dve, base_steps)
                nc.vector.tensor_tensor(in_tile[:], b.source_count[:, 1:NT + 1],
                                        b.source_count[:, 0:NT], ALU.subtract).then_inc(in_tile_ready, 1)
                dve.wait_ge(base_summed, 1)
                done(nc.vector.tensor_copy(base[:], b.ps_count[0:E_ROWS, 0:NT]))
                with dve.Fori(0, NT // 2) as i:
                    for r in range(2):
                        nc.vector.tensor_scalar(
                            out=mask[:, r, :], in0=b.node_tile[:],
                            scalar1=g.iota[0:E_ROWS, bass.ds(i * 2 + r, 1)],
                            scalar2=None, op0=ALU.is_equal).then_inc(masks_ready, 1)
                    for r in range(2):
                        dve.wait_ge(masks_ready, i * 2 + r + 1)
                        nc.vector.tensor_tensor_scan(
                            out=running[:, r, :], data0=mask[:, r, :], data1=mask[:, r, :],
                            initial=base[:, bass.ds(i * 2 + r, 1)], op0=ALU.add, op1=ALU.max)\
                            .then_inc(running_ready, 1)
                    for r in range(2):
                        dve.wait_ge(running_ready, i * 2 + r + 1)
                        dve.wait_ge(added, i * 2 + r + 1)
                        nc.vector.tensor_tensor(masked[:, r, :], running[:, r, :], mask[:, r, :],
                                                ALU.mult).then_inc(masked_ready, 1)
                    dve.wait_ge(masked_ready, i * 2 + 2)

        scattered = g.scattered
        with phase(nc, "pairs_ready", "staged", "scatter_begun", "count_steps") as (
                block, pairs_ready, staged, scatter_begun, count_steps):
            @block.vector
            def _(dve):
                nc.vector.tensor_copy(pairs[:, :, 0], b.far_i[:]).then_inc(pairs_ready, 1)
                nc.vector.tensor_copy(pairs[:, :, 1], b.own_i[:]).then_inc(pairs_ready, 1)
                count_below(nc, b, Chain(dve, count_steps), b.far_i, b.destination_count)

            @block.scalar
            def _(act):
                def stage(i, r):
                    cols = bass.ds((i * 2 + r) * SORT_COLS, SORT_COLS)
                    nc.scalar.activation(place_stage[:, r, :], place[:, cols], ACT.Copy).then_inc(staged, 1)
                    nc.scalar.activation(pair_stage[:, r], pairs[:, cols, :], ACT.Copy).then_inc(staged, 1)

                act.wait_ge(pairs_ready, 2)
                for r in range(2):
                    stage(0, r)
                with act.Fori(1, SORT_STEPS) as i:
                    for r in range(2):
                        act.wait_ge(scattered[r], i * (16 * SORT_COLS))
                        stage(i, r)

            @block.gpsimd
            def _(pool):
                with pool.Fori(0, SORT_STEPS) as i:
                    for r in range(2):
                        pool.wait_ge(staged, (i * 2 + r + 1) * 2)
                        pool.sem_inc(scatter_begun, 1)
                        for k in range(SORT_COLS):
                            nc.gpsimd.indirect_dma_start(
                                out=g.edge_pairs[:, :],
                                out_offset=bass.IndirectOffsetOnAxis(ap=place_stage[:, r, k:k + 1], axis=0),
                                in_=pair_stage[:, r, k, :], in_offset=None,
                            ).then_inc(scattered[r], 16)
                for r in range(2):
                    pool.wait_ge(scattered[r], 16 * SORT_COLS * SORT_STEPS)

        with phase(nc, "pairs_loaded", "split", "stored") as (block, pairs_loaded, split, stored):
            @block.sync
            def _(sp):
                sp.dma_start(pairs[:], g.edge_pairs[:, :].rearrange("(r c) s -> r c s", r=E_ROWS))\
                    .then_inc(pairs_loaded, 16)
                for n, (pad, part) in enumerate(((g.far_pad, b.far_i), (g.own_pad, b.own_i))):
                    sp.wait_ge(split, n + 1)
                    sp.dma_start(pad[0:E].rearrange("(r c) -> r c", r=E_ROWS), part[:]).then_inc(stored, 16)
                sp.wait_ge(stored, 32)

            @block.vector
            def _(dve):
                dve.wait_ge(pairs_loaded, 16)
                for n, part in enumerate((b.far_i, b.own_i)):
                    nc.vector.tensor_copy(part[:], pairs[:, :, n]).then_inc(split, 1)


def lay_out(nc, g, b, plan, count):
    with ExitStack() as ctx:
        def sb(name, shape, dt=F32):
            return ctx.enter_context(nc.sbuf_tensor(f"{name}{plan}", shape, dt))

        ps_count, ps_t, tile_no, key_pad = b.ps_count, b.ps_t, b.tile_no, b.key_pad
        first = sb("first", [P, NT + 1])
        tiles = sb("tiles", [P, NT])
        tiles_i = sb("tiles_i", [P, NT], I32)
        zeros = sb("zeros", [P, NT])
        last_tile = sb("last_tile", [P, NT])
        shift = sb("shift", [P, NT])
        shift_step = sb("shift_step", [P, NT - 1])
        reached = sb("reached", [P, TB, NT - 1])
        weighted = sb("weighted", [P, TB, NT - 1])
        node_tile = sb("node_tile", [P, TB])
        node_tile_i = sb("node_tile_i", [P, TB], U16)
        start = sb("start", [P, TB])
        start_i = sb("start_i", [P, TB], I32)
        src_t = sb("src_t", [P, TB, P], I32)
        dst_t = sb("dst_t", [P, TB, P], I32)
        src_tf = sb("src_tf", [P, TB, P])
        dst_tf = sb("dst_tf", [P, TB, P])
        dloc_t = sb("dloc_t", [P, TB, P])
        dloc_tb = sb("dloc_tb", [P, TB, P], BF16)
        mine = sb("mine", [P, TB, P])
        key = sb("key", [P, TB, P])
        fetched = g.plan_fetched

        with phase(nc, "summed", "starts_ready", "plan_steps") as (
                block, summed, starts_ready, plan_steps):
            @block.vector
            def _(dve):
                done = Chain(dve, plan_steps)
                done(nc.vector.memset(first[:, 0:1], 0.0))
                done(nc.vector.memset(first[:, NT:NT + 1], float(E)))
                done(nc.vector.memset(zeros[:], 0.0))
                dve.wait_ge(summed, 1)
                done(nc.vector.tensor_copy(first[:, 1:NT], ps_count[:, 1:NT]))
                done(nc.vector.tensor_tensor(tiles[:], first[:, 1:NT + 1], first[:, 0:NT], ALU.subtract))
                done(nc.vector.tensor_scalar(out=tiles_i[:], in0=tiles[:], scalar1=float(P - 1),
                                             scalar2=None, op0=ALU.add))
                done(nc.vector.tensor_scalar(out=tiles_i[:], in0=tiles_i[:], scalar1=P.bit_length() - 1,
                                             scalar2=None, op0=ALU.arith_shift_right))
                done(nc.vector.tensor_copy(tiles[:], tiles_i[:]))
                done(nc.vector.tensor_tensor_scan(out=last_tile[:], data0=tiles[:], data1=zeros[:],
                                                  initial=0.0, op0=ALU.add, op1=ALU.add))
                done(nc.vector.memset(shift[:, 0:1], 0.0))
                done(nc.vector.scalar_tensor_tensor(out=shift[:, 1:NT], in0=last_tile[:, 0:NT - 1],
                                                    scalar=float(P), in1=first[:, 1:NT],
                                                    op0=ALU.mult, op1=ALU.subtract))
                done(nc.vector.tensor_tensor(shift_step[:], shift[:, 1:NT], shift[:, 0:NT - 1],
                                             ALU.subtract))
                done(nc.vector.tensor_tensor(
                    reached[:], last_tile[:, 0:NT - 1].unsqueeze(1).to_broadcast([P, TB, NT - 1]),
                    tile_no[:].unsqueeze(2).to_broadcast([P, TB, NT - 1]), ALU.is_le))
                done(nc.vector.tensor_reduce(node_tile[:], reached[:], AX, ALU.add))
                done(nc.vector.tensor_tensor(
                    weighted[:], reached[:], shift_step[:].unsqueeze(1).to_broadcast([P, TB, NT - 1]),
                    ALU.mult))
                done(nc.vector.tensor_reduce(start[:], weighted[:], AX, ALU.add))
                done(nc.vector.scalar_tensor_tensor(out=start[:], in0=tile_no[:], scalar=float(P),
                                                    in1=start[:], op0=ALU.mult, op1=ALU.subtract))
                done(nc.vector.tensor_scalar(out=start_i[:], in0=start[:], scalar1=float(E),
                                             scalar2=0.0, op0=ALU.min, op1=ALU.max))
                done(nc.vector.tensor_copy(node_tile_i[:], node_tile[:]))
                nc.vector.memset(key_pad[:], -1.0).then_inc(starts_ready, 1)

            @block.tensor
            def _(pe):
                nc.tensor.matmul(ps_count[:, 1:NT], g.ones[0:E_ROWS, :], count[:, 1:NT],
                                 start=True, stop=True).then_inc(summed, 1)

            @block.gpsimd
            def _(pool):
                pool.wait_ge(starts_ready, 1)
                for block_no in range(TB):
                    for pad, got in ((g.far_pad, src_t), (g.own_pad, dst_t)):
                        nc.gpsimd.indirect_dma_start(
                            out=got[:, block_no, :], out_offset=None,
                            in_=bass.AP(pad, 0, [[1, 1], [1, E + P]]),
                            in_offset=bass.IndirectOffsetOnAxis(ap=start_i[:, block_no:block_no + 1], axis=1),
                        ).then_inc(fetched, 16)
                pool.wait_ge(fetched, 32 * TB * (plan + 1))

        with phase(nc, "key_ready", "key_stored", "turned", "turned_used", "layout_steps",
                   "plan_stored") as (
                block, key_ready, key_stored, turned, turned_used, layout_steps, plan_stored):
            @block.vector
            def _(dve):
                done = Chain(dve, layout_steps)
                done(nc.vector.tensor_copy(src_tf[:], src_t[:]))
                done(nc.vector.tensor_copy(dst_tf[:], dst_t[:]))
                node_tile_b = node_tile[:].unsqueeze(2).to_broadcast([P, TB, P])
                done(nc.vector.scalar_tensor_tensor(out=dloc_t[:], in0=node_tile_b, scalar=float(-P),
                                                    in1=dst_tf[:], op0=ALU.mult, op1=ALU.add))
                done(nc.vector.tensor_copy(dloc_tb[:], dloc_t[:]))
                done(nc.vector.tensor_scalar(out=mine[:], in0=dloc_t[:], scalar1=float(P),
                                             scalar2=None, op0=ALU.is_lt))
                nc.vector.scalar_tensor_tensor(out=key[:], in0=dst_tf[:], scalar=1.0, in1=mine[:],
                                               op0=ALU.add, op1=ALU.mult).then_inc(key_ready, 1)
                for n in range(TB):
                    dve.wait_ge(turned, n + 1)
                    cols = slice(n * P, (n + 1) * P)
                    nc.vector.tensor_copy(g.idx[:, cols], ps_t[:, n % 2, 0:P])
                    nc.vector.tensor_copy(g.dloc[:, cols], ps_t[:, n % 2, P:2 * P]).then_inc(turned_used, 1)
                    if n == TB - 1:
                        dve.wait_ge(turned_used, TB)
                nc.vector.tensor_copy(g.first_dloc[:], g.dloc[0:1, 0:T:CHUNK])

            @block.tensor
            def _(pe):
                pe.wait_ge(key_ready, 1)
                for n in range(TB):
                    if n >= 2:
                        pe.wait_ge(turned_used, n - 1)
                    nc.tensor.transpose(ps_t[:, n % 2, 0:P], src_tf[:, n, :], g.ident[:])
                    nc.tensor.transpose(ps_t[:, n % 2, P:2 * P], dloc_t[:, n, :], g.ident[:])\
                        .then_inc(turned, 1)

            @block.sync
            def _(sp):
                key_slots = g.key_dram[P:P + TP * P].rearrange("(b t e) -> t b e", b=TB, t=P)
                sp.dma_start(g.key_dram[0:P].rearrange("(a e) -> a e", a=1), key_pad[:]).then_inc(key_stored, 16)
                sp.dma_start(g.tile_dram[:].rearrange("(b t) -> t b", t=P), node_tile_i[:],
                             allow_slow_non_contiguous=True).then_inc(key_stored, 16)
                sp.wait_ge(key_ready, 1)
                sp.dma_start(key_slots, key[:]).then_inc(key_stored, 16)
                sp.dma_start(g.dloc_row_dram[plan].rearrange("(b t e) -> t b e", b=TB, t=P), dloc_tb[:])\
                    .then_inc(key_stored, 16)
                sp.wait_ge(key_stored, 64)
                sp.dma_start(g.tile_row[:], g.tile_dram[:].rearrange("(a t) -> a t", a=1)).then_inc(key_stored, 16)
                sp.wait_ge(key_stored, 80)
                sp.wait_ge(turned_used, TB)
                sp.dma_start(g.idx_dram[plan], g.idx[:]).then_inc(plan_stored, 16)
                sp.dma_start(g.dloc_dram[plan], g.dloc[:]).then_inc(plan_stored, 16)
                sp.dma_start(g.tile_row_dram[plan:plan + 1, :], g.tile_row[:]).then_inc(plan_stored, 16)
                sp.wait_ge(plan_stored, 48)


def switch_plan(nc, g, plan):
    with phase(nc, f"plan{plan}_loaded") as (block, loaded):
        @block.sync
        def _(sp):
            sp.dma_start(g.idx[:], g.idx_dram[plan]).then_inc(loaded, 16)
            sp.dma_start(g.dloc[:], g.dloc_dram[plan]).then_inc(loaded, 16)
            sp.dma_start(g.tile_row[:], g.tile_row_dram[plan:plan + 1, :]).then_inc(loaded, 16)
            sp.wait_ge(loaded, 48)


def find_breaks(nc, g):
    keys = g.query_flat[0:CHUNK, 0:CHUNKS * (P + 2)].rearrange("p (c e) -> p c e", c=CHUNKS)
    row_break = g.query_flat[0:CHUNK, CHUNKS * (P + 2):CHUNKS * (P + 4)].rearrange("p (s c) -> p s c", s=2)
    with phase(nc, "keys_loaded", "breaks_ready", "breaks_stored", "break_steps") as (
            block, keys_loaded, breaks_ready, breaks_stored, break_steps):
        @block.vector
        def _(dve):
            done = Chain(dve, break_steps)
            dve.wait_ge(keys_loaded, 16)
            done(nc.vector.tensor_tensor(keys[:, :, 0:P + 1], keys[:, :, 0:P + 1], keys[:, :, 1:P + 2],
                                         ALU.not_equal))
            done(nc.vector.tensor_scalar(out=g.run_break, in0=keys[:, :, 0:P + 1], scalar1=-BIG,
                                         scalar2=None, op0=ALU.mult))
            done(nc.vector.tensor_reduce(row_break[:, 0, :], g.run_break[:, :, 0:P], AX, ALU.min))
            nc.vector.tensor_reduce(row_break[:, 1, :], g.run_break[:, :, 1:P + 1], AX, ALU.min)\
                .then_inc(breaks_ready, 1)

        @block.sync
        def _(sp):
            sp.dma_start(keys, bass.AP(g.key_dram, P - 1, [[P, CHUNK], [P * CHUNK, CHUNKS], [1, P + 2]]))\
                .then_inc(keys_loaded, 16)
            sp.wait_ge(breaks_ready, 1)
            for side in range(2):
                sp.dma_start(g.break_dram[side].rearrange("(c t) -> t c", t=CHUNK), row_break[:, side, :],
                             allow_slow_non_contiguous=True).then_inc(breaks_stored, 16)
            sp.wait_ge(breaks_stored, 32)
            sp.dma_start(g.any_break.rearrange("h s t -> h (s t)"),
                         g.break_dram[:, :].rearrange("(a s) t -> a (s t)", a=1).to_broadcast([H, 2 * T]))\
                .then_inc(breaks_stored, 16)
            sp.wait_ge(breaks_stored, 48)


def allocate_large(nc, ctx, g):
    def sb(name, shape, dt=F32):
        return ctx.enter_context(nc.sbuf_tensor(name, shape, dt))

    node = NT * D
    gather_ring = 2 * GROUP * 2 * D
    onehots = 2 * GROUP * P
    messages = 2 * GROUP * ACC_W
    edge_rings = gather_ring + onehots + GROUP * P + messages
    g.arena = sb("arena", [P, 3 * node + edge_rings])
    g.acc = sb("acc", [P, NT, ACC_W])
    g.alpha_dst = sb("alpha_dst", [P, NT, H])
    g.idx_stage = sb("idx_stage", [P, 2, GROUP], I32)
    g.score8 = sb("score8", [P, GROUP, H])
    g.dloc_rows = sb("dloc_rows", [P, 2, GROUP * P], BF16)
    g.gat_w = sb("gat_w", [D, 3, D + 2 * H])
    g.qkv_w = sb("qkv_w", [D, 3 * D])
    g.self_w = sb("self_w", [D, 2, D])
    g.sum_w = sb("sum_w", [D + 2, 2, D])
    g.mean_w = sb("mean_w", [D + 1, D])
    g.bias = sb("bias", [P, 3, D])
    g.mean = sb("mean", [P, NT])
    g.spread = sb("spread", [P, NT])
    g.recip = sb("recip", [P, NT, H])
    g.eps = sb("eps", [P, 1])
    g.acc_flat = g.acc[:].rearrange("p n w -> p (n w)")
    g.square = g.acc_flat[:, 0:NT * D].rearrange("p (n d) -> p n d", d=D)

    at = 0

    def take(size):
        nonlocal at
        at += size
        assert at <= 3 * node + edge_rings
        return g.arena[:, at - size:at]

    g.x = take(node).rearrange("p (n d) -> p n d", d=D)
    g.h = take(node).rearrange("p (n d) -> p n d", d=D)
    g.query_flat = take(node)
    g.query = g.query_flat.rearrange("p (n d) -> p n d", d=D)
    rings_at = at
    rows = take(gather_ring)
    g.kv_ring = rows.rearrange("p (r k w) -> p r k w", r=2, k=GROUP)
    g.sum_ring = rows[:, 0:2 * GROUP * (D + 1)].rearrange("p (r k w) -> p r k w", r=2, k=GROUP)
    g.onehot = take(onehots).rearrange("p (r k n) -> p r k n", r=2, k=GROUP)
    g.onehot_t = take(GROUP * P).rearrange("p (k e) -> p k e", k=GROUP)
    g.msg = take(messages).rearrange("p (r k w) -> p r k w", r=2, k=GROUP)
    at = rings_at
    g.stage = take(RING * 2 * (D + 2)).rearrange("p (r s w) -> p r s w", r=RING, s=2)
    g.stage_t = take(RING * 2 * P).rearrange("p (r s n) -> p r s n", r=RING, s=2)
    g.row_stage = g.arena[:, at:at + 2 * STORED * 2 * D]
    take(2 * STORED * (D + H))
    g.any_break = take(2 * T)[0:H].rearrange("p (s t) -> p s t", s=2)
    g.run_break = take(-(-CHUNKS * (P + 1) // 2))[0:CHUNK].bitcast(BF16)[:, 0:CHUNKS * (P + 1)]\
        .rearrange("p (c e) -> p c e", c=CHUNKS)
    at = 0
    g.gat_rows = take(ROW_RING * GROUP * (D + H)).rearrange("p (t w) -> p t w", w=D + H)
    g.gat_ring = take(2 * GROUP * (D + H)).rearrange("p (r k w) -> p r k w", r=2, k=GROUP)
    g.gat_onehot = take(onehots).rearrange("p (r k n) -> p r k n", r=2, k=GROUP)
    g.gat_onehot_t = take(GROUP * P).bitcast(BF16).rearrange("p (r k e) -> p r k e", r=2, k=GROUP)
    g.alpha_parts = take(NT * H * 3 // 2).bitcast(BF16).rearrange("p (n h s) -> p n h s", n=NT, h=H)
    g.alpha_rest = take(NT * H).rearrange("p (n h) -> p n h", n=NT)
    g.dst_scores = take(GROUP * H).rearrange("p (k h) -> p k h", k=GROUP)
    g.gat_msg = take(messages).rearrange("p (r k w) -> p r k w", r=2, k=GROUP)
    g.scores, g.weights = (take(CHUNK * H).rearrange("p (t h) -> p t h", h=H) for _ in range(2))
    g.score_rows, g.run_max, g.run_total = (
        take(H * P)[0:CHUNK].rearrange("p (h e) -> p h e", h=H) for _ in range(3))
    g.first_onehot = take(P)[0:1]
    g.carry_fwd = take(CHUNK + 1)[0:H]
    g.carry_bwd = take(CHUNK + 1)[0:H]
    g.carry_col = take(H)[0:CHUNK]
    g.drop = take(1)[0:H]
    g.chunk_break = take((P + 2) // 2)[0:CHUNK].bitcast(BF16)[:, 0:P + 1]
    g.chunk_end = take(CHUNK)[0:H]
    g.factor_row = take(H)[0:1]
    g.factor = take(H)
    assert at <= rings_at


def load_x(sp, g, x, x_loaded, tail_zeroed):
    sp.dma_start(g.x[:, 0:N_FULL, :], x[0:N_FULL * P, :].rearrange("(n p) d -> p n d", p=P))\
        .then_inc(x_loaded, 16)
    if tail_zeroed is not None:
        sp.wait_ge(tail_zeroed, 1)
    sp.dma_start(g.x[0:N_TAIL, N_FULL, :], x[N_FULL * P:N, :]).then_inc(x_loaded, 16)


def load_inputs(nc, g, x, gat_w, att_src, att_dst, gat_bias, qw, kw, vw, w0, b0, w1, b1, w2, b2, w3, b3):
    with ExitStack() as ctx:
        att = g.query_flat[0:D, 0:6 * H].rearrange("p (l s) -> p l s", l=3)
        w01, w2s = (g.query_flat[0:D, at:at + 4 * D].rearrange("p (i s d) -> p i s d", i=2, s=2)
                    for at in (D, 5 * D))
        w_t = g.query_flat[0:D, 9 * D:16 * D].rearrange("p (n d) -> p n d", n=7)
        b01 = g.query_flat[0:D, 16 * D:16 * D + 4].rearrange("p (i s) -> p i s", i=2)
        b2s = g.query_flat[0:1, 17 * D:19 * D].rearrange("p (i d) -> p i d", i=2)
        bias_rows = g.query_flat[0:1, 19 * D:23 * D].rearrange("p (i s d) -> p i s d", i=2, s=2)
        ps_w = ctx.enter_context(nc.psum_tensor("ps_w", [P, 2, 512], F32, allow_name_mangling=True))
        ps_m = ctx.enter_context(nc.psum_tensor("ps_m", [P, 512], F32, allow_name_mangling=True))
        with phase(nc, "zeroed", "loaded", "x_loaded", "w_turned", "w_kept", "product", "product_kept",
                   "rows_kept") as (
                block, zeroed, loaded, x_loaded, w_turned, w_kept, product, product_kept, rows_kept):
            n_att = 3 * 2 * H
            n_loads = n_att + 3 + 3 + 2 * 7 + 1 + 1 + 3

            @block.gpsimd
            def _(pool):
                nc.gpsimd.memset(g.x[:, N_FULL, :], 0.0).then_inc(zeroed, 1)
                nc.gpsimd.memset(att, 0.0).then_inc(zeroed, 1)
                nc.gpsimd.memset(g.eps[:], LN_EPS).then_inc(zeroed, 1)

            @block.sync
            def _(sp):
                def load(to, given):
                    sp.dma_start(to, given).then_inc(loaded, 16)

                for l in range(3):
                    load(g.gat_w[:, l, 0:D], gat_w[l])
                sp.wait_ge(zeroed, 3)
                for l in range(3):
                    for side, given in enumerate((att_src, att_dst)):
                        for h in range(H):
                            load(att[h * C:(h + 1) * C, l, side * H + h:side * H + h + 1],
                                 given[l, h].rearrange("(c a) -> c a", a=1))
                for i in range(2):
                    load(w01[:, i, 0, :], w0[i])
                    load(w01[:, i, 1, :], w1[i])
                    load(w2s[:, i, 0, :], w2[i, D:2 * D, :])
                    load(w2s[:, i, 1, :], w2[i, 0:D, :])
                    load(b01[:, i, 0:1], b0[i].rearrange("(c a) -> c a", a=1))
                    load(b01[:, i, 1:2], b1[i].rearrange("(c a) -> c a", a=1))
                    load(b2s[:, i, :], b2[i:i + 1, :])
                for n, w in enumerate((qw, kw, vw)):
                    load(g.qkv_w[:, n * D:(n + 1) * D], w)
                load(g.mean_w[0:D, :], w3)
                load(g.mean_w[D:D + 1, :], b3.rearrange("(a d) -> a d", a=1))
                for l in range(3):
                    load(g.bias[:, l, :], gat_bias[l:l + 1, :].to_broadcast([P, D]))
                load_x(sp, g, x, x_loaded, None)
                sp.wait_ge(loaded, 16 * n_loads)
                sp.wait_ge(x_loaded, 32)
                sp.wait_ge(product_kept, 11)
                for i in range(2):
                    for side in range(2):
                        sp.dma_start(g.sum_w[D + side:D + side + 1, i, :], bias_rows[:, i, side, :])\
                            .then_inc(rows_kept, 16)
                sp.wait_ge(rows_kept, 64)

            turns = [g.gat_w[:, l, 0:D] for l in range(3)] + [w01[:, i, s, :] for i in range(2) for s in range(2)]

            @block.tensor
            def _(pe):
                pe.wait_ge(loaded, 16 * n_loads)
                for n, w in enumerate(turns):
                    if n >= 2:
                        pe.wait_ge(w_kept, n - 1)
                    nc.tensor.transpose(ps_w[0:D, n % 2, 0:D], w, g.ident[0:D, 0:D]).then_inc(w_turned, 1)
                pe.wait_ge(w_kept, 7)
                done = 0
                for l in range(3):
                    pe.wait_ge(product_kept, done)
                    nc.tensor.matmul(ps_m[0:D, 0:2 * H], w_t[:, l, :], att[:, l, :], start=True, stop=True)\
                        .then_inc(product, 1)
                    done += 1
                for i in range(2):
                    for side in range(2):
                        pe.wait_ge(product_kept, done)
                        nc.tensor.matmul(ps_m[0:D, 0:D], w_t[:, 3 + 2 * i + side, :], w2s[:, i, side, :],
                                         start=True, stop=True).then_inc(product, 1)
                        done += 1
                        pe.wait_ge(product_kept, done)
                        m = nc.tensor.matmul(ps_m[0:1, 0:D], b01[:, i, side:side + 1], w2s[:, i, side, :],
                                             start=True, stop=side == 0)
                        if side == 1:
                            m = nc.tensor.matmul(ps_m[0:1, 0:D], g.ones[0:1, 0:1], b2s[:, i, :],
                                                 start=False, stop=True)
                        m.then_inc(product, 1)
                        done += 1

            @block.vector
            def _(dve):
                for n in range(7):
                    dve.wait_ge(w_turned, n + 1)
                    nc.vector.tensor_copy(w_t[:, n, :], ps_w[0:D, n % 2, 0:D]).then_inc(w_kept, 1)
                done = 0

                def keep(to, what):
                    nonlocal done
                    done += 1
                    dve.wait_ge(product, done)
                    nc.vector.tensor_copy(to, what).then_inc(product_kept, 1)

                for l in range(3):
                    keep(g.gat_w[:, l, D:D + 2 * H], ps_m[0:D, 0:2 * H])
                for i in range(2):
                    for side in range(2):
                        keep(g.sum_w[0:D, i, :] if side == 0 else g.self_w[:, i, :], ps_m[0:D, 0:D])
                        keep(bias_rows[:, i, side, :], ps_m[0:1, 0:D])


def normalise(nc, g, table=None):
    halves = (slice(0, NT // 2), slice(NT // 2, NT))
    with phase(nc, "norm_steps", "centred", "squared", "var_ready", "std_ready", "normed", "norm_stored") as (
            block, norm_steps, centred, squared, var_ready, std_ready, normed, norm_stored):
        @block.vector
        def _(dve):
            done = Chain(dve, norm_steps)
            done(nc.vector.tensor_reduce(g.mean[:], g.x, AX, ALU.add))
            for half in halves:
                nc.vector.scalar_tensor_tensor(
                    out=g.h[:, half, :], in0=g.mean[:, half].unsqueeze(2).to_broadcast([P, NT // 2, D]),
                    scalar=-1.0 / D, in1=g.x[:, half, :], op0=ALU.mult, op1=ALU.add).then_inc(centred, 1)
            for n, half in enumerate(halves):
                dve.wait_ge(squared, n + 1)
                nc.vector.tensor_reduce(g.spread[:, half], g.square[:, half, :], AX, ALU.add)\
                    .then_inc(var_ready, 1)
            dve.wait_ge(std_ready, 1)
            done(nc.vector.reciprocal(g.spread[:], g.spread[:]))
            for half in halves:
                nc.vector.scalar_tensor_tensor(
                    out=g.h[:, half, :], in0=g.h[:, half, :], scalar=0.0,
                    in1=g.spread[:, half].unsqueeze(2).to_broadcast([P, NT // 2, D]),
                    op0=ALU.max, op1=ALU.mult).then_inc(normed, 1)

        @block.scalar
        def _(act):
            for n, half in enumerate(halves):
                act.wait_ge(centred, n + 1)
                nc.scalar.activation(g.square[:, half, :], g.h[:, half, :], ACT.Square).then_inc(squared, 1)
            act.wait_ge(var_ready, 2)
            nc.scalar.activation(g.spread[:], g.spread[:], ACT.Sqrt, bias=g.eps[:], scale=1.0 / D)\
                .then_inc(std_ready, 1)

        if table is not None:
            @block.sync
            def _(sp):
                for n, half in enumerate(halves):
                    sp.wait_ge(normed, n + 1)
                    sp.dma_start(table[:, :].rearrange("(n p) w -> p n w", p=P)[:, half, :],
                                 g.h[:, half, :]).then_inc(norm_stored, 16)
                sp.wait_ge(norm_stored, 32)


def standardise(nc, g, into_x):
    with phase(nc, "sd_steps", "var_ready", "std_ready") as (block, sd_steps, var_ready, std_ready):
        @block.vector
        def _(dve):
            done = Chain(dve, sd_steps)
            done(nc.vector.tensor_reduce(g.mean[:], g.h, AX, ALU.add))
            done(nc.vector.scalar_tensor_tensor(
                out=g.square, in0=g.mean[:].unsqueeze(2).to_broadcast([P, NT, D]), scalar=-1.0 / D,
                in1=g.h, op0=ALU.mult, op1=ALU.add))
            done(nc.vector.tensor_tensor(g.square, g.square, g.square, ALU.mult))
            nc.vector.tensor_reduce(g.spread[:], g.square, AX, ALU.add).then_inc(var_ready, 1)
            dve.wait_ge(std_ready, 1)
            done(nc.vector.reciprocal(g.spread[:], g.spread[:]))
            done(nc.vector.tensor_tensor(g.h, g.h, g.spread[:].unsqueeze(2).to_broadcast([P, NT, D]),
                                         ALU.mult))
            if into_x:
                done(nc.vector.tensor_tensor(g.x, g.x, g.h, ALU.add))

        @block.scalar
        def _(act):
            act.wait_ge(var_ready, 1)
            nc.scalar.activation(g.spread[:], g.spread[:], ACT.Sqrt, scale=1.0 / (D - 1)).then_inc(std_ready, 1)


def node_matmul(nc, g, sources, width, relu_in, keep, tables=(), table_cols=()):
    with ExitStack() as ctx:
        ps_turn = ctx.enter_context(nc.psum_tensor("ps_turn", [P, 2, 512], F32, allow_name_mangling=True))
        ps_out = ctx.enter_context(nc.psum_tensor("ps_out", [P, 2, 512], F32, allow_name_mangling=True))
        with phase(nc, "staged", "turned", "turn_kept", "product", "kept", "table_written0",
                   "table_written1") as (
                block, staged, turned, turn_kept, product, kept, table_written0, table_written1):
            table_written = (table_written0, table_written1)
            if tables:
                first, end = table_cols[0].start, table_cols[-1].stop
                row_stage = g.row_stage[:, 0:2 * STORED * (end - first)]\
                    .rearrange("p (f n w) -> p f n w", f=2, n=STORED)
            @block.scalar
            def _(act):
                func = ACT.Relu if relu_in else ACT.Copy
                with act.Fori(0, NODE_ITERS) as i:
                    for k in range(NODE_UNROLL):
                        n = i * NODE_UNROLL + k
                        act.wait_ge(turned, n + 1)
                        for s, (rows, cols, _) in enumerate(sources):
                            last = nc.scalar.activation(
                                g.stage[:, k % RING, s:s + 1, 0:cols],
                                rows[:, bass.ds(n, 1), 0:cols], func)
                        last.then_inc(staged, 1)

            @block.tensor
            def _(pe):
                pe.sem_inc(turned, RING)
                pe.sem_inc(product, RING)

                def turn(n, r):
                    pe.wait_ge(staged, n + 1)
                    pe.wait_ge(turn_kept, n + 1)
                    for s, (_, cols, _) in enumerate(sources):
                        last = nc.tensor.transpose(ps_turn[0:cols, r, s * P:(s + 1) * P],
                                                   g.stage[:, r, s, 0:cols], g.ident[:])
                    last.then_inc(turned, 1)

                with pe.Fori(0, NODE_ITERS) as i:
                    for k in range(NODE_UNROLL):
                        n = i * NODE_UNROLL + k
                        r = k % RING
                        if k == 0:
                            turn(n, 0)
                        if k < NODE_UNROLL - 1:
                            turn(n + 1, 1 - r)
                        pe.wait_ge(turn_kept, n + 1 + RING)
                        pe.wait_ge(kept, n + 1)
                        for s, (_, cols, weights) in enumerate(sources):
                            last = nc.tensor.matmul(ps_out[:, r, 0:width],
                                                    g.stage_t[0:cols, r, s, :], weights,
                                                    start=s == 0, stop=s == len(sources) - 1)
                        last.then_inc(product, 1)

            @block.vector
            def _(dve):
                dve.sem_inc(turn_kept, RING)
                dve.sem_inc(kept, RING)

                def keep_turned(n, r):
                    dve.wait_ge(turned, n + 1 + RING)
                    dve.wait_ge(product, n + 1)
                    for s, (_, cols, _) in enumerate(sources):
                        last = nc.vector.tensor_copy(g.stage_t[0:cols, r, s, :],
                                                     ps_turn[0:cols, r, s * P:(s + 1) * P])
                    last.then_inc(turn_kept, 1)

                with dve.Fori(0, NODE_ITERS) as i:
                    for k in range(NODE_UNROLL):
                        n = i * NODE_UNROLL + k
                        r = k % RING
                        if k == 0:
                            keep_turned(n, 0)
                        if k < NODE_UNROLL - 1:
                            keep_turned(n + 1, 1 - r)
                        dve.wait_ge(product, n + 1 + RING)
                        for to, cols in keep:
                            last = nc.vector.tensor_copy(to[:, bass.ds(n, 1), :],
                                                         ps_out[:, r:r + 1, cols])
                        if tables:
                            half = k // STORED
                            if k % STORED == 0:
                                dve.wait_ge(table_written[half], (i + 1) * (16 * len(tables)))
                            last = nc.vector.tensor_copy(row_stage[:, half, k % STORED, :],
                                                         ps_out[:, r, first:end])
                        last.then_inc(kept, 1)

            if tables:
                @block.sync
                def _(sp):
                    for half in range(2):
                        sp.sem_inc(table_written[half], 16 * len(tables))
                    with sp.Fori(0, NODE_ITERS) as i:
                        for half in range(2):
                            n = i * NODE_UNROLL + half * STORED
                            sp.wait_ge(kept, n + STORED + RING)
                            for table, cols in zip(tables, table_cols):
                                at = cols.start - first
                                sp.dma_start(
                                    table[:, :].rearrange("(n p) w -> p n w", p=P)[:, bass.ds(n, STORED), :],
                                    row_stage[:, half, :, at:at + cols.stop - cols.start])\
                                    .then_inc(table_written[half], 16)
                    for half in range(2):
                        sp.wait_ge(table_written[half], 16 * len(tables) * (NODE_ITERS + 1))


def table_store(nc, g, name, table, rows):
    with phase(nc, f"{name}_stored") as (block, stored):
        @block.sync
        def _(sp):
            sp.dma_start(table[:, :].rearrange("(n p) w -> p n w", p=P), rows).then_inc(stored, 16)
            sp.wait_ge(stored, 16)


def load_node_tiles(nc, g, engine, q):
    _, values = nc.values_load_multi_w_load_instructions(
        g.tile_row[0:1, bass.ds(q * GROUP, GROUP)], engines=[engine], min_val=0, max_val=NT - 1,
        skip_runtime_bounds_check_because="the plan counts at most NT - 1 starts for any edge tile")
    return values


def stage_indices(nc, g, act, idx_staged, rows_used, r, q):
    act.wait_ge(rows_used, q + 1)
    nc.scalar.activation(g.idx_stage[:, r, :], g.idx[:, bass.ds(q * GROUP, GROUP)], ACT.Copy)\
        .then_inc(idx_staged, 1)


def gather_loop(nc, g, table, width, ring, idx_staged, rows_landed, rows_used, group_begun, pool):
    with pool.Fori(0, STEPS) as i:
        for r in range(2):
            q = i * 2 + r
            pool.wait_ge(idx_staged, q + 1)
            pool.wait_ge(rows_used, q + 1)
            pool.sem_inc(group_begun, 1)
            for k in range(GROUP):
                nc.gpsimd.indirect_dma_start(
                    out=ring[:, r, k, 0:width], out_offset=None, in_=table[:, :],
                    in_offset=bass.IndirectOffsetOnAxis(ap=g.idx_stage[:, r, k:k + 1], axis=0),
                ).then_inc(rows_landed[r], 16)
    for r in range(2):
        pool.wait_ge(rows_landed[r], 16 * GROUP * STEPS)


def build_onehot(nc, g, onehot, q, r):
    return nc.vector.tensor_tensor(
        onehot[:, r], g.iota[:].unsqueeze(1).to_broadcast([P, GROUP, P]),
        g.dloc[:, bass.ds(q * GROUP, GROUP)].unsqueeze(2).to_broadcast([P, GROUP, P]), ALU.is_equal)


def load_dloc_rows(nc, g, engine, plan, q, r, loaded):
    engine.dma_start(g.dloc_rows[:, r, :],
                     g.dloc_row_dram[plan:plan + 1, bass.ds(q * (GROUP * P), GROUP * P)]
                     .to_broadcast([P, GROUP * P])).then_inc(loaded, 16)


def build_onehot_t(nc, g, onehot_t, r):
    return nc.vector.tensor_scalar(out=onehot_t.rearrange("p k e -> p (k e)"), in0=g.dloc_rows[:, r, :],
                                   scalar1=g.part_no[:], scalar2=None, op0=ALU.is_equal)


def add_sums(nc, g, dve, done, ps_sum, node_tiles, width):
    for k in range(GROUP):
        sums = g.acc[:, bass.ds(node_tiles[k], 1), 0:width]
        part = ps_sum[:, k // 4:k // 4 + 1, (k % 4) * P:(k % 4) * P + width]
        done(nc.vector.tensor_tensor(sums, sums, part, ALU.add))


def sum_matmuls(nc, onehot, ps_sum, r, rows, width):
    for k in range(GROUP):
        last = nc.tensor.matmul(ps_sum[:, k // 4, (k % 4) * P:(k % 4) * P + width],
                                onehot[:, r, k, :], rows[:, r, k, 0:width], start=True, stop=True)
    return last


def gat_edges(nc, g, l):
    CG = CHUNK_GROUPS
    rows_landed = g.rows_landed()
    with ExitStack() as ctx:
        def pb(name, shape):
            return ctx.enter_context(nc.psum_tensor(name, shape, F32, allow_name_mangling=True))

        ps_sum = pb("ps_sum", [P, 2, GROUP // 4, 512])
        ps_dst = pb("ps_dst", [P, 512])[:, 0:GROUP * H * 3].rearrange("p (k h s) -> p k h s", k=GROUP, h=H)
        ps_rows = pb("ps_rows", [P, 512])
        ps_back = ps_rows[:, 0:H * CHUNK].rearrange("p (h t) -> p h t", h=H)
        ps_misc = pb("ps_misc", [P, 512])
        ps_edge, ps_carry = ps_misc[0:H, 0:CHUNK], ps_misc[0:CHUNK, CHUNK:CHUNK + H]
        ps_scale = pb("ps_scale", [P, 512])
        ps_factor_row, ps_factor = ps_scale[0:1, 0:H], ps_scale[:, H:2 * H]
        with phase(nc, "group_begun", "idx_staged0", "idx_staged1", "moved0", "moved1",
                   "rows_loaded0", "rows_loaded1", "onehot_t_ready", "dst_ready", "scored", "split_steps",
                   "onehot_ready", "msg_built", "weights_in_msg", "summed", "acc_steps",
                   "rows_turned", "edge_ready", "edge_turned", "carry_ready", "carry_turned",
                   "below_max", "weighed", "back_turned", "weights_ready",
                   "drop_ready", "factor_ready", "factor_turned", "factor_row_ready", "factor_spread",
                   "soft_steps", "soft_turn", "move_begun", "load_begun") as (
                block, group_begun, idx_staged0, idx_staged1, moved0, moved1,
                rows_loaded0, rows_loaded1, onehot_t_ready, dst_ready, scored, split_steps,
                onehot_ready, msg_built, weights_in_msg, summed, acc_steps,
                rows_turned, edge_ready, edge_turned, carry_ready, carry_turned,
                below_max, weighed, back_turned, weights_ready,
                drop_ready, factor_ready, factor_turned, factor_row_ready, factor_spread,
                soft_steps, soft_turn, move_begun, load_begun):
            idx_staged, moved = (idx_staged0, idx_staged1), (moved0, moved1)
            rows_loaded = (rows_loaded0, rows_loaded1)

            def walk(eng, body):
                body(0, True, None, None)
                body(1, True, LAG, CG)
                with eng.Fori(2, CHUNKS) as c:
                    body(c, True, 0, CG)
                body(CHUNKS, False, 0, CG)
                body(CHUNKS + 1, False, 0, LAG)

            def stage3_group(c, g_):
                return (c - 1) * CG + g_ - LAG, (c - 2 if g_ < LAG else c - 1), (g_ - LAG) % CG

            def has_softmax(c):
                return not isinstance(c, int) or 1 <= c <= CHUNKS

            @block.gpsimd
            def _(pool):
                with pool.Fori(0, STEPS) as i:
                    for r in range(2):
                        pool.wait_ge(idx_staged[r], (i + 1) * 16)
                        pool.wait_ge(moved[r], (i + 1) * 16)
                        pool.sem_inc(group_begun, 1)
                        for k in range(GROUP):
                            nc.gpsimd.indirect_dma_start(
                                out=g.gat_ring[:, r, k, :], out_offset=None, in_=g.gat_table[:, :],
                                in_offset=bass.IndirectOffsetOnAxis(ap=g.idx_stage[:, r, k:k + 1], axis=0),
                            ).then_inc(rows_landed[r], 16)
                for r in range(2):
                    pool.wait_ge(rows_landed[r], 16 * GROUP * STEPS)

            @block.sync
            def _(sp):
                def stage_indices(q, r):
                    sp.dma_start(g.idx_stage[:, r, :], g.idx[:, bass.ds(q * GROUP, GROUP)])\
                        .then_inc(idx_staged[r], 16)

                for r in range(2):
                    sp.sem_inc(moved[r], 16)
                    stage_indices(r, r)
                with sp.Fori(0, CHUNKS) as c:
                    with sp.Fori(0, CG // 2) as u:
                        for r in range(2):
                            q = c * CG + u * 2 + r
                            i = c * (CG // 2) + u
                            sp.wait_ge(rows_landed[r], (i + 1) * (16 * GROUP))
                            sp.wait_ge(msg_built, q + 1)
                            sp.sem_inc(move_begun, 1)
                            sp.dma_start(
                                g.gat_rows[:, bass.ds((c & 1) * CHUNK + (u * 2 + r) * GROUP, GROUP), :],
                                g.gat_ring[:, r]).then_inc(moved[r], 16)
                            stage_indices(q + 2, r)
                for r in range(2):
                    sp.wait_ge(moved[r], 16 * (STEPS + 1))
                    sp.wait_ge(idx_staged[r], 16 * (STEPS + 1))

            @block.scalar
            def _(act):
                for r in range(2):
                    load_dloc_rows(nc, g, act, 1, r, r, rows_loaded[r])

                def body(c, stage1, first, end):
                    for g_ in range(CG):
                        if first is not None and first <= g_ < end:
                            q, chunk, place = stage3_group(c, g_)
                            rm = (g_ - LAG) % 2
                            if place == 0:
                                act.wait_ge(weights_ready, chunk + 1)
                            act.wait_ge(summed, q + 1)
                            nc.scalar.activation(g.gat_msg[:, rm, :, D:D + H],
                                                 g.weights[:, place * GROUP:(place + 1) * GROUP, :], ACT.Copy)\
                                .then_inc(weights_in_msg, 1)
                        if stage1:
                            act.wait_ge(onehot_t_ready, c * CG + g_ + 1)
                            act.sem_inc(load_begun, 1)
                            load_dloc_rows(nc, g, act, 1, c * CG + g_ + 2, g_ % 2, rows_loaded[g_ % 2])
                        if g_ == 1 and has_softmax(c):
                            act.wait_ge(drop_ready, c)
                            nc.scalar.activation(g.drop, g.drop, ACT.Exp).then_inc(factor_ready, 1)
                            act.wait_ge(below_max, c)
                            nc.scalar.activation(g.score_rows, g.score_rows, ACT.Exp).then_inc(weighed, 1)

                walk(act, body)
                for r in range(2):
                    act.wait_ge(rows_loaded[r], 16 * (STEPS + 1))

            @block.tensor
            def _(pe):
                pe.sem_inc(summed, 2)

                def turn(to, what, n):
                    return nc.tensor.transpose(to, what, g.ident[0:n, 0:n])

                def soft(c, point):
                    if not has_softmax(c):
                        return
                    if point == "start":
                        pe.wait_ge(scored, c * CG + 1)
                        for h in range(H):
                            last = turn(ps_rows[0:CHUNK, h * P:(h + 1) * P], g.scores[:, :, h], P)
                        last.then_inc(rows_turned, 1)
                    elif point in ((0, 0), (0, 2)):
                        n = (c - 1) * 2 + (point == (0, 2)) + 1
                        pe.wait_ge(edge_ready, n)
                        edge = g.run_max[:, :, P - 1] if point == (0, 0) else g.run_total[:, :, 0]
                        pe.sem_inc(soft_turn, 1)
                        turn(ps_edge, edge, CHUNK).then_inc(edge_turned, 1)
                    elif point in ((0, 1), (1, 0)):
                        n = (c - 1) * 2 + (point == (1, 0)) + 1
                        pe.wait_ge(carry_ready, n)
                        carry = g.carry_fwd[:, 0:CHUNK] if point == (0, 1) else g.carry_bwd[:, 1:CHUNK + 1]
                        pe.sem_inc(soft_turn, 1)
                        turn(ps_carry, carry, H).then_inc(carry_turned, 1)
                    elif point == (1, 1):
                        pe.wait_ge(factor_ready, c)
                        pe.sem_inc(soft_turn, 1)
                        turn(ps_factor_row, g.drop, H).then_inc(factor_turned, 1)
                    elif point == (1, 2):
                        pe.wait_ge(weighed, c)
                        for h in range(H):
                            last = turn(ps_back[:, h, :], g.score_rows[:, h, :], CHUNK)
                        last.then_inc(back_turned, 1)
                    elif point == (2, 0):
                        pe.wait_ge(factor_row_ready, c)
                        nc.tensor.matmul(ps_factor, g.first_onehot, g.factor_row, start=True, stop=True)\
                            .then_inc(factor_spread, 1)

                def body(c, stage1, first, end):
                    soft(c, "start")
                    for g_ in range(CG):
                        r = g_ % 2
                        q1 = c * CG + g_
                        if stage1:
                            node_tiles = load_node_tiles(nc, g, mybir.EngineType.PE, q1)
                            pe.wait_ge(onehot_t_ready, q1 + 1)
                            pe.wait_ge(scored, q1 + 1)
                            for k in range(GROUP):
                                last = nc.tensor.matmul(
                                    ps_dst[:, k:k + 1], g.gat_onehot_t[:, r, k, :],
                                    g.alpha_parts[:, bass.ds(node_tiles[k], 1)], start=True, stop=True)
                            last.then_inc(dst_ready, 1)
                        soft(c, (g_, 0))
                        if first is not None and first <= g_ < end:
                            q, _, _ = stage3_group(c, g_)
                            rm = (g_ - LAG) % 2
                            pe.wait_ge(onehot_ready, q + 1)
                            pe.wait_ge(weights_in_msg, q + 1)
                            pe.wait_ge(msg_built, q + 1 + ROW_RING)
                            pe.wait_ge(acc_steps, (q + 1) * GROUP + 1)
                            sum_matmuls(nc, g.gat_onehot, ps_sum[:, rm], rm, g.gat_msg, D + H).then_inc(summed, 1)
                        soft(c, (g_, 1))
                        soft(c, (g_, 2))

                walk(pe, body)

            @block.vector
            def _(dve):
                nc.vector.memset(g.acc_flat, 0.0).then_inc(acc_steps, 1)
                dve.wait_ge(acc_steps, 1)
                dve.sem_inc(acc_steps, 2 * GROUP)
                dve.sem_inc(scored, 1)
                dve.sem_inc(msg_built, ROW_RING)
                split = Chain(dve, split_steps)
                given = g.alpha_dst[:]
                for part in range(3):
                    split(nc.vector.tensor_copy(g.alpha_parts[:, :, :, part], given))
                    if part < 2:
                        split(nc.vector.tensor_tensor(g.alpha_rest, given, g.alpha_parts[:, :, :, part],
                                                      ALU.subtract))
                        given = g.alpha_rest
                opened = Chain(dve, soft_steps)
                opened(nc.vector.memset(g.carry_fwd, -BIG))
                opened(nc.vector.memset(g.carry_bwd, -BIG))
                SOFT = 2 * H + 12

                def add_scores(c, g_):
                    q = c * CG + g_
                    r = g_ % 2
                    dve.wait_ge(dst_ready, q + 1)
                    Chain(dve, split_steps, q + 5)(nc.vector.tensor_reduce(g.dst_scores, ps_dst, AX, ALU.add))
                    dve.wait_ge(moved[r], (c * (CG // 2) + g_ // 2 + 2) * 16)
                    if has_softmax(c):
                        dve.wait_ge(rows_turned, c)
                    nc.vector.tensor_tensor(
                        g.scores[:, g_ * GROUP:(g_ + 1) * GROUP, :],
                        g.gat_rows[:, bass.ds((c & 1) * CHUNK + g_ * GROUP, GROUP), D:D + H],
                        g.dst_scores, ALU.add).then_inc(scored, 1)

                def add_group(c, g_):
                    q, _, _ = stage3_group(c, g_)
                    rm = (g_ - LAG) % 2
                    node_tiles = load_node_tiles(nc, g, mybir.EngineType.DVE, q)
                    dve.wait_ge(summed, q + 1 + 2)
                    add_sums(nc, g, dve, Chain(dve, acc_steps, (q + 2) * GROUP + 1), ps_sum[:, rm],
                             node_tiles,
                             D + H)

                state = {}

                def soft(c, point):
                    if not has_softmax(c):
                        return
                    cc = c - 1
                    if point == (0, 0):
                        state["done"] = Chain(dve, soft_steps, cc * SOFT + 2)
                    done = state.get("done")
                    tiles = bass.ds(cc * CHUNK, CHUNK)

                    def scan_fwd(h, initial):
                        return nc.vector.tensor_tensor_scan(
                            out=g.run_max[:, h, :], data0=g.chunk_break[:, 0:P], data1=g.score_rows[:, h, :],
                            initial=initial, op0=ALU.add, op1=ALU.max)

                    def scan_bwd(h, initial):
                        return nc.vector.tensor_tensor_scan(
                            out=g.run_total[:, h, ::-1], data0=g.chunk_break[:, P:0:-1],
                            data1=g.run_max[:, h, ::-1], initial=initial, op0=ALU.add, op1=ALU.max)

                    if point == (0, 0):
                        dve.wait_ge(rows_turned, c)
                        done(nc.vector.tensor_copy(g.chunk_end, g.any_break[:, 1, tiles]))
                        done(nc.vector.tensor_copy(
                            g.chunk_break, g.run_break[:, bass.ds(cc, 1), :].rearrange("p a e -> p (a e)")))
                        rows = ps_rows[0:CHUNK, :].rearrange("p (h e) -> p h e", h=H)
                        done(nc.vector.tensor_scalar(out=g.run_max, in0=rows, scalar1=SLOPE,
                                                     scalar2=None, op0=ALU.mult))
                        done(nc.vector.tensor_tensor(g.score_rows, g.run_max, rows, ALU.max))
                        for h in range(H):
                            last = scan_fwd(h, -BIG)
                        last.then_inc(edge_ready, 1)
                    elif point == (0, 1):
                        dve.wait_ge(edge_turned, cc * 2 + 1)
                        nc.vector.tensor_tensor_scan(
                            out=g.carry_fwd[:, 1:CHUNK + 1], data0=g.any_break[:, 0, tiles], data1=ps_edge,
                            initial=g.carry_fwd[:, 0:1], op0=ALU.add, op1=ALU.max).then_inc(carry_ready, 1)
                    elif point == (0, 2):
                        dve.wait_ge(carry_turned, cc * 2 + 1)
                        done(nc.vector.tensor_copy(g.carry_col, ps_carry))
                        for h in range(H):
                            done(scan_fwd(h, g.carry_col[:, h:h + 1]))
                        for h in range(H):
                            last = scan_bwd(h, -BIG)
                        last.then_inc(edge_ready, 1)
                    elif point == (1, 0):
                        dve.wait_ge(edge_turned, cc * 2 + 2)
                        nc.vector.tensor_tensor_scan(
                            out=g.carry_bwd[:, CHUNK - 1::-1], data0=g.chunk_end[:, ::-1],
                            data1=ps_edge[:, ::-1], initial=-BIG, op0=ALU.add, op1=ALU.max)\
                            .then_inc(carry_ready, 1)
                    elif point == (1, 1):
                        dve.wait_ge(carry_ready, cc * 2 + 2)
                        done(nc.vector.tensor_tensor(g.drop, g.carry_fwd[:, 0:1], g.carry_bwd[:, 0:1],
                                                     ALU.subtract))
                        nc.vector.tensor_scalar(out=g.drop, in0=g.drop, scalar1=0.0, scalar2=None,
                                                op0=ALU.min).then_inc(drop_ready, 1)
                        dve.wait_ge(carry_turned, cc * 2 + 2)
                        done(nc.vector.tensor_copy(g.carry_fwd[:, 0:1], g.carry_fwd[:, CHUNK:CHUNK + 1]))
                        done(nc.vector.tensor_copy(g.carry_col, ps_carry))
                        for h in range(H):
                            done(scan_bwd(h, g.carry_col[:, h:h + 1]))
                        nc.vector.tensor_tensor(g.score_rows, g.score_rows, g.run_total, ALU.subtract)\
                            .then_inc(below_max, 1)
                    elif point == (1, 2):
                        dve.wait_ge(factor_turned, c)
                        done(nc.vector.tensor_scalar(
                            out=g.first_onehot, in0=g.iota[0:1, :],
                            scalar1=g.first_dloc[0:1, bass.ds(cc, 1)], scalar2=None, op0=ALU.is_equal))
                        nc.vector.tensor_scalar(out=g.factor_row, in0=ps_factor_row, scalar1=-1.0,
                                                scalar2=None, op0=ALU.add).then_inc(factor_row_ready, 1)
                    elif point == (2, 1):
                        dve.wait_ge(back_turned, c)
                        if not (isinstance(c, int) and c == 1):
                            dve.wait_ge(weights_in_msg, cc * CG)
                            dve.wait_ge(msg_built, cc * CG + ROW_RING)
                        nc.vector.tensor_copy(g.weights.rearrange("p t h -> p h t"), ps_back)\
                            .then_inc(weights_ready, 1)
                    elif point == (2, 2):
                        dve.wait_ge(factor_spread, c)
                        done(nc.vector.tensor_scalar(out=g.factor, in0=ps_factor, scalar1=1.0,
                                                     scalar2=None, op0=ALU.add))
                        state["scale"] = True

                def scale_open_node(c):
                    cc = c - 1
                    done = state["done"]
                    node_tile = nc.values_load(
                        g.tile_row[0:1, bass.ds(cc * CHUNK, 1)], engines=[mybir.EngineType.DVE],
                        min_val=0, max_val=NT - 1,
                        skip_runtime_bounds_check_because="the plan counts at most NT - 1 starts")
                    sums = g.acc[:, bass.ds(node_tile, 1), 0:D].rearrange("p a (h c) -> p (a h) c", h=H)
                    done(nc.vector.tensor_tensor(sums, sums, g.factor.unsqueeze(2).to_broadcast([P, H, C]),
                                                 ALU.mult))
                    sums = g.acc[:, bass.ds(node_tile, 1), D:D + H].rearrange("p a h -> p (a h)")
                    done(nc.vector.tensor_tensor(sums, sums, g.factor, ALU.mult))

                def body(c, stage1, first, end):
                    if isinstance(c, int) and c == 0:
                        left_scores = left_sums = False
                    else:
                        left_scores = not isinstance(c, int) or c <= CHUNKS
                        left_sums = not isinstance(c, int) or c >= 2
                    for g_ in range(CG):
                        r = g_ % 2
                        q1 = c * CG + g_
                        stage3 = first is not None and first <= g_ < end
                        if g_ == 0 and left_scores:
                            add_scores(c - 1, CG - 1)
                        elif g_ > 0 and stage1:
                            add_scores(c, g_ - 1)
                        if stage1:
                            dve.wait_ge(rows_loaded[r], (c * (CG // 2) + g_ // 2 + 1) * 16)
                            build_onehot_t(nc, g, g.gat_onehot_t[:, r], r).then_inc(onehot_t_ready, 1)
                        if stage3:
                            q, chunk, place = stage3_group(c, g_)
                            rm = (g_ - LAG) % 2
                            dve.wait_ge(summed, q + 1)
                            build_onehot(nc, g, g.gat_onehot, q, rm).then_inc(onehot_ready, 1)
                        soft(c, (g_, 0))
                        if stage3:
                            if place == 0:
                                dve.wait_ge(weights_ready, chunk + 1)
                            nc.vector.tensor_tensor(
                                g.gat_msg[:, rm, :, 0:D].rearrange("p k (h c) -> p k h c", h=H),
                                g.gat_rows[:, bass.ds((chunk & 1) * CHUNK + place * GROUP, GROUP), 0:D]
                                .rearrange("p k (h c) -> p k h c", h=H),
                                g.weights[:, place * GROUP:(place + 1) * GROUP, :].unsqueeze(3)
                                .to_broadcast([P, GROUP, H, C]), ALU.mult).then_inc(msg_built, 1)
                        soft(c, (g_, 1))
                        if g_ == 0:
                            if left_sums:
                                add_group(c - 1, CG - 1)
                        elif first is not None and first <= g_ - 1 < end:
                            add_group(c, g_ - 1)
                        soft(c, (g_, 2))
                        if g_ == LAG and has_softmax(c):
                            scale_open_node(c)
                            assert not isinstance(state["done"].count, int) or \
                                state["done"].count == c * SOFT + 2, state["done"].count

                walk(dve, body)


def gat_finish(nc, g, l, x):
    with phase(nc, "finish_steps", "tail_zeroed", "x_loaded") as (
            block, finish_steps, tail_zeroed, x_loaded):
        if l == 2:
            @block.gpsimd
            def _(pool):
                nc.gpsimd.memset(g.x[:, N_FULL, :], 0.0).then_inc(tail_zeroed, 1)

            @block.sync
            def _(sp):
                load_x(sp, g, x, x_loaded, tail_zeroed)

        @block.vector
        def _(dve):
            done = Chain(dve, finish_steps)
            done(nc.vector.tensor_scalar(out=g.recip[:], in0=g.acc[:, :, D:D + H], scalar1=1e-16,
                                         scalar2=None, op0=ALU.add))
            done(nc.vector.reciprocal(g.recip[:], g.recip[:]))
            done(nc.vector.tensor_tensor(
                g.h.rearrange("p n (h c) -> p n h c", h=H),
                g.acc[:, :, 0:D].rearrange("p n (h c) -> p n h c", h=H),
                g.recip[:].unsqueeze(3).to_broadcast([P, NT, H, C]), ALU.mult))
            done(nc.vector.tensor_tensor(g.h, g.h,
                                         g.bias[:, l, :].unsqueeze(1).to_broadcast([P, NT, D]), ALU.add))
            if l == 2:
                dve.wait_ge(x_loaded, 32)
                done(nc.vector.scalar_tensor_tensor(out=g.x, in0=g.h, scalar=0.0, in1=g.x,
                                                    op0=ALU.max, op1=ALU.add))


def attention(nc, g):
    with ExitStack() as ctx:
        def pb(name):
            return ctx.enter_context(nc.psum_tensor(name, [P, 2, GROUP // 4, 512], F32,
                                                    allow_name_mangling=True))

        ps_query, ps_sum = pb("ps_query"), pb("ps_sum")
        rows_landed = g.rows_landed()
        with phase(nc, "group_begun", "idx_staged", "rows_used", "onehot_ready", "rows_loaded0",
                   "rows_loaded1", "load_begun", "onehot_t_ready", "query_ready", "multiplied", "clipped",
                   "weights_in_msg", "sums_ready", "sum_steps", "score_steps") as (
                block, group_begun, idx_staged, rows_used, onehot_ready, rows_loaded0,
                rows_loaded1, load_begun, onehot_t_ready, query_ready, multiplied, clipped,
                weights_in_msg, sums_ready, sum_steps, score_steps):
            rows_loaded = (rows_loaded0, rows_loaded1)

            @block.gpsimd
            def _(pool):
                gather_loop(nc, g, g.kv_table, 2 * D, g.kv_ring, idx_staged, rows_landed, rows_used,
                            group_begun, pool)

            @block.scalar
            def _(act):
                for r in range(2):
                    stage_indices(nc, g, act, idx_staged, rows_used, r, r)
                    load_dloc_rows(nc, g, act, 0, r, r, rows_loaded[r])
                act.wait_ge(onehot_t_ready, 1)
                load_dloc_rows(nc, g, act, 0, 2, 0, rows_loaded[0])
                with act.Fori(0, STEPS) as i:
                    for r in range(2):
                        q = i * 2 + r
                        act.wait_ge(clipped, q + 1)
                        act.wait_ge(sums_ready, q + 1)
                        nc.scalar.activation(g.msg[:, r, :, D:D + H], g.score8[:], ACT.Exp)\
                            .then_inc(weights_in_msg, 1)
                        act.wait_ge(onehot_t_ready, q + 2)
                        act.sem_inc(load_begun, 1)
                        load_dloc_rows(nc, g, act, 0, q + 3, 1 - r, rows_loaded[1 - r])
                        stage_indices(nc, g, act, idx_staged, rows_used, r, q + 2)
                act.wait_ge(rows_loaded[0], 16 * (STEPS + 2))
                act.wait_ge(rows_loaded[1], 16 * (STEPS + 1))

            @block.tensor
            def _(pe):
                pe.sem_inc(sums_ready, 2)

                def spread_queries(q, r):
                    node_tiles = load_node_tiles(nc, g, mybir.EngineType.PE, q)
                    pe.wait_ge(onehot_t_ready, q + 1)
                    pe.wait_ge(multiplied, q + 1)
                    for k in range(GROUP):
                        last = nc.tensor.matmul(
                            ps_query[:, r, k // 4:k // 4 + 1, (k % 4) * D:(k % 4 + 1) * D],
                            g.onehot_t[:, k, :], g.query[:, bass.ds(node_tiles[k], 1), :],
                            start=True, stop=True)
                    last.then_inc(query_ready, 1)

                spread_queries(0, 0)
                with pe.Fori(0, STEPS) as i:
                    for r in range(2):
                        q = i * 2 + r
                        spread_queries(q + 1, 1 - r)
                        pe.wait_ge(onehot_ready, q + 1)
                        pe.wait_ge(weights_in_msg, q + 1)
                        pe.wait_ge(rows_used, q + 1 + 2)
                        pe.wait_ge(sum_steps, (q + 1) * GROUP + 1)
                        sum_matmuls(nc, g.onehot, ps_sum[:, r], r, g.msg, D + H).then_inc(sums_ready, 1)

            @block.vector
            def _(dve):
                nc.vector.memset(g.acc_flat, 0.0).then_inc(sum_steps, 1)
                dve.wait_ge(sum_steps, 1)
                dve.sem_inc(sum_steps, 2 * GROUP)
                dve.sem_inc(rows_used, 2)
                dve.sem_inc(multiplied, 2)

                def add_group(q, r):
                    node_tiles = load_node_tiles(nc, g, mybir.EngineType.DVE, q)
                    dve.wait_ge(sums_ready, q + 1 + 2)
                    add_sums(nc, g, dve, Chain(dve, sum_steps, (q + 2) * GROUP + 1), ps_sum[:, r],
                             node_tiles, D + H)

                def body(i):
                    for r in range(2):
                        q = i * 2 + r
                        dve.wait_ge(rows_landed[r], (i + 1) * (16 * GROUP))
                        dve.wait_ge(query_ready, q + 1)
                        keys = g.kv_ring[:, r, :, 0:D]
                        nc.vector.tensor_tensor(
                            keys.rearrange("p (b k) d -> p b k d", b=GROUP // 4),
                            keys.rearrange("p (b k) d -> p b k d", b=GROUP // 4),
                            ps_query[:, r, :, 0:4 * D].rearrange("p b (k d) -> p b k d", k=4), ALU.mult)\
                            .then_inc(multiplied, 1)
                        dve.wait_ge(multiplied, q + 1 + 2)
                        steps = Chain(dve, score_steps, q)
                        steps(nc.vector.tensor_reduce(
                            g.score8[:], keys.rearrange("p k (h c) -> p k h c", h=H), AX, ALU.add))
                        nc.vector.tensor_scalar(out=g.score8[:], in0=g.score8[:], scalar1=-10.0,
                                                scalar2=10.0, op0=ALU.max, op1=ALU.min).then_inc(clipped, 1)
                        dve.wait_ge(rows_loaded[1 - r], (i + 1 + r) * 16)
                        build_onehot_t(nc, g, g.onehot_t, 1 - r).then_inc(onehot_t_ready, 1)
                        dve.wait_ge(weights_in_msg, q + 1)
                        nc.vector.tensor_tensor(
                            g.msg[:, r, :, 0:D].rearrange("p k (h c) -> p k h c", h=H),
                            g.kv_ring[:, r, :, D:2 * D].rearrange("p k (h c) -> p k h c", h=H),
                            g.msg[:, r, :, D:D + H].unsqueeze(3)
                            .to_broadcast([P, GROUP, H, C]), ALU.mult).then_inc(rows_used, 1)
                        if r == 1 or not isinstance(i, int):
                            add_group(q - 1, 1 - r)
                        build_onehot(nc, g, g.onehot, q + 1, 1 - r).then_inc(onehot_ready, 1)

                dve.wait_ge(rows_loaded[0], 16)
                build_onehot_t(nc, g, g.onehot_t, 0).then_inc(onehot_t_ready, 1)
                build_onehot(nc, g, g.onehot, 0, 0).then_inc(onehot_ready, 1)
                body(0)
                with dve.Fori(1, STEPS) as i:
                    body(i)
                add_group(2 * STEPS - 1, 1)


def attention_finish(nc, g):
    with phase(nc, "finish_steps") as (block, finish_steps):
        @block.vector
        def _(dve):
            done = Chain(dve, finish_steps)
            done(nc.vector.tensor_scalar(out=g.recip[:], in0=g.acc[:, :, D:D + H], scalar1=1e-8,
                                         scalar2=None, op0=ALU.add))
            done(nc.vector.reciprocal(g.recip[:], g.recip[:]))
            done(nc.vector.tensor_tensor(
                g.query.rearrange("p n (h c) -> p n h c", h=H),
                g.acc[:, :, 0:D].rearrange("p n (h c) -> p n h c", h=H),
                g.recip[:].unsqueeze(3).to_broadcast([P, NT, H, C]), ALU.mult))
            done(nc.vector.tensor_tensor(g.x, g.x, g.h, ALU.add))
            done(nc.vector.tensor_tensor(g.x, g.x, g.query, ALU.add))


def plain_sums(nc, g):
    with ExitStack() as ctx:
        ps_sum = ctx.enter_context(nc.psum_tensor("ps_sum", [P, 2, GROUP // 4, 512], F32, allow_name_mangling=True))
        rows_landed = g.rows_landed()
        with phase(nc, "group_begun", "idx_staged", "rows_used", "onehot_ready", "ones_set", "sums_ready",
                   "sum_steps") as (
                block, group_begun, idx_staged, rows_used, onehot_ready, ones_set, sums_ready, sum_steps):
            @block.gpsimd
            def _(pool):
                nc.gpsimd.memset(g.sum_ring[:, :, :, D:D + 1], 1.0).then_inc(ones_set, 1)
                gather_loop(nc, g, g.row_table, D, g.sum_ring, idx_staged, rows_landed, rows_used, group_begun, pool)

            @block.scalar
            def _(act):
                with act.Fori(0, STEPS) as i:
                    for r in range(2):
                        stage_indices(nc, g, act, idx_staged, rows_used, r, i * 2 + r)

            @block.tensor
            def _(pe):
                pe.wait_ge(ones_set, 1)
                pe.sem_inc(rows_used, 2)
                with pe.Fori(0, STEPS) as i:
                    for r in range(2):
                        q = i * 2 + r
                        pe.wait_ge(rows_landed[r], (i + 1) * (16 * GROUP))
                        pe.wait_ge(onehot_ready, q + 1)
                        pe.wait_ge(sums_ready, q + 1)
                        sum_matmuls(nc, g.onehot, ps_sum[:, r], r, g.sum_ring, D + 1).then_inc(rows_used, 1)

            @block.vector
            def _(dve):
                nc.vector.memset(g.acc_flat, 0.0).then_inc(sum_steps, 1)
                dve.wait_ge(sum_steps, 1)
                dve.sem_inc(sums_ready, 2)
                build_onehot(nc, g, g.onehot, 0, 0).then_inc(onehot_ready, 1)
                with dve.Fori(0, STEPS) as i:
                    for r in range(2):
                        q = i * 2 + r
                        done = Chain(dve, sum_steps, q * GROUP + 1)
                        node_tiles = load_node_tiles(nc, g, mybir.EngineType.DVE, q)
                        dve.wait_ge(rows_used, q + 2)
                        build_onehot(nc, g, g.onehot, q + 1, 1 - r).then_inc(onehot_ready, 1)
                        dve.wait_ge(rows_used, q + 1 + 2)
                        add_sums(nc, g, dve, done, ps_sum[:, r], node_tiles, D + 1)
                        dve.sem_inc(sums_ready, 1)
                last = Chain(dve, sum_steps, 2 * STEPS * GROUP + 1)
                last(nc.vector.memset(g.acc[:, :, D + 1:D + 2], 1.0))


def mean_finish(nc, g, out):
    with phase(nc, "finish_steps", "ready", "out_stored") as (block, finish_steps, ready, out_stored):
        @block.vector
        def _(dve):
            done = Chain(dve, finish_steps)
            done(nc.vector.tensor_scalar(out=g.spread[:], in0=g.acc[:, :, D], scalar1=1.0,
                                         scalar2=None, op0=ALU.max))
            done(nc.vector.reciprocal(g.spread[:], g.spread[:]))
            done(nc.vector.tensor_tensor(g.h, g.h, g.spread[:].unsqueeze(2).to_broadcast([P, NT, D]),
                                         ALU.mult))
            nc.vector.tensor_tensor(g.x, g.x, g.h, ALU.add).then_inc(ready, 1)

        @block.sync
        def _(sp):
            sp.wait_ge(ready, 1)
            sp.dma_start(out[0:N_FULL * P, :].rearrange("(n p) d -> p n d", p=P), g.x[:, 0:N_FULL, :])\
                .then_inc(out_stored, 16)
            sp.dma_start(out[N_FULL * P:N, :], g.x[0:N_TAIL, N_FULL, :]).then_inc(out_stored, 16)
            sp.wait_ge(out_stored, 32)


def gnn_kernel(nc, x, src, dst, gat_w, att_src, att_dst, gat_bias, qw, kw, vw, w0, b0, w1, b1, w2, b2,
               w3, b3, out):
    g = Graph()
    with ExitStack() as ctx:
        g.plan_fetched = ctx.enter_context(nc.semaphore("plan_fetched"))
        g.scattered = [ctx.enter_context(nc.semaphore(f"scattered{r}")) for r in range(2)]
        loops = [0]

        def rows_landed():
            loops[0] += 1
            return [ctx.enter_context(nc.semaphore(f"rows_landed{loops[0]}_{r}")) for r in range(2)]

        g.rows_landed = rows_landed
        allocate_small(nc, ctx, g)
        plan_edge_tiles(nc, g, src, dst)
        allocate_large(nc, ctx, g)
        load_inputs(nc, g, x, gat_w, att_src, att_dst, gat_bias, qw, kw, vw, w0, b0, w1, b1, w2, b2, w3, b3)

        find_breaks(nc, g)

        normalise(nc, g)
        for l in range(3):
            node_matmul(nc, g, [(g.h, D, g.gat_w[:, l, :])], D + 2 * H, l > 0,
                        [(g.alpha_dst[:], slice(D + H, D + 2 * H))], (g.gat_table,), (slice(0, D + H),))
            gat_edges(nc, g, l)
            gat_finish(nc, g, l, x)

        normalise(nc, g)
        node_matmul(nc, g, [(g.h, D, g.qkv_w[:])], 3 * D, False,
                    [(g.query, slice(0, D))], (g.kv_table,), (slice(D, 3 * D),))
        switch_plan(nc, g, 0)
        attention(nc, g)
        switch_plan(nc, g, 1)
        attention_finish(nc, g)

        normalise(nc, g, g.row_table)
        for i in range(2):
            if i == 1:
                table_store(nc, g, "sum", g.row_table, g.h)
            plain_sums(nc, g)
            node_matmul(nc, g, [(g.h, D, g.self_w[:, i, :]), (g.acc[:], D + 2, g.sum_w[:, i, :])],
                        D, False, [(g.h, slice(0, D))])
            standardise(nc, g, into_x=i == 1)

        normalise(nc, g, g.row_table)
        plain_sums(nc, g)
        node_matmul(nc, g, [(g.acc[:], D + 1, g.mean_w[:])], D, False, [(g.h, slice(0, D))])
        mean_finish(nc, g, out)


_INS = ["x", "src", "dst", "L0_gnn_W", "L0_gnn_att_src", "L0_gnn_att_dst", "L0_gnn_bias", "L1_gnn_qW",
        "L1_gnn_kW", "L1_gnn_vW", "L2_gnn_W0", "L2_gnn_b0", "L2_gnn_W1", "L2_gnn_b1", "L2_gnn_W2",
        "L2_gnn_b2", "L3_gnn_W", "L3_gnn_b"]


def kernel(**inputs):
    import numpy as _np
    import concourse.bacc as _bacc
    from concourse import mybir as _mybir
    from concourse.bass_utils import run_bass_kernel_spmd as _run

    nc = _bacc.Bacc("TRN2", target_bir_lowering=False, num_devices=1)
    arrays, args = {}, []
    for name in _INS:
        a = _np.ascontiguousarray(inputs[name])
        arrays[f"in_{name}"] = a
        args.append(nc.dram_tensor(f"in_{name}", a.shape, _mybir.dt.from_np(a.dtype), kind="ExternalInput").ap())
    out = nc.dram_tensor("out", (N, D), F32, kind="ExternalOutput").ap()
    gnn_kernel(nc, *args, out)
    r = _run(nc, [arrays], core_ids=[0])
    return r.results[0]["out"]
```
